# Optimizing a Trainium2 kernel written in Bass

```python
import numpy as np
import jax
import jax.numpy as jnp

def _softmax(x, axis=-1):
    return jax.nn.softmax(x, axis=axis)

def _gelu(x):
    return jax.nn.gelu(x, approximate=True)

def _silu(x):
    return jax.nn.silu(x)

def _sigmoid(x):
    return jax.nn.sigmoid(x)

def _layernorm(x, axis=-1, eps=1e-05):
    m = jnp.mean(x, axis=axis, keepdims=True)
    v = jnp.var(x, axis=axis, keepdims=True)
    return (x - m) / jnp.sqrt(v + eps)

def _scatter_add(tgt, idx, src, axis=0):
    return tgt.at[idx].add(src)

def _segment_sum(src, seg, n):
    return jax.ops.segment_sum(src, seg, n)
kernel_name = 'mk_flamingo_gated_d2_seqx_r8_8509d0'

def setup_inputs(seed: int=0):
    np.random.seed(seed)
    _w = jnp.asarray

    def _rec_inputs():
        import jax
        import jax.numpy as jnp
        _rk = jax.random.key(seed)
        x = -0.0002928 + 1 * jax.random.normal(jax.random.fold_in(_rk, 1), (4, 512, 128), jnp.float32)
        _lenS = 512 - jax.random.randint(jax.random.fold_in(_rk, 7), (4,), 0, max(1, 512 // 4) + 1, jnp.int32)
        _lenS2 = 77 - jax.random.randint(jax.random.fold_in(_rk, 8), (4,), 0, max(1, 77 // 4) + 1, jnp.int32)
        _ctx_1024P = jax.random.normal(jax.random.fold_in(_rk, 11), (4, 16, 128), jnp.float32)
        _ctx_1024c = jax.random.dirichlet(jax.random.fold_in(_rk, 511), 0.3 * jnp.ones((16,), jnp.float32), (4, 77))
        _ctx_1024t = jnp.einsum('bsk,bkd->bsd', _ctx_1024c, _ctx_1024P)
        _ctx_1024t = _ctx_1024t * jax.lax.rsqrt(jnp.mean(jnp.square(_ctx_1024t)) + 1e-12) * 0.953939
        ctx_1024 = 4.13588e-05 + 0.999923 * (_ctx_1024t + 0.3 * jax.random.normal(jax.random.fold_in(_rk, 611), (4, 77, 128), jnp.float32))
        itok_BxS_8_8191 = jax.random.randint(jax.random.fold_in(_rk, 12), (4, 512), 8, 1024, jnp.int32)
        itok_BxS2_1_8191 = jax.random.randint(jax.random.fold_in(_rk, 13), (4, 77), 1, 1024, jnp.int32)
        _validS = jnp.arange(512)[None, :] < _lenS[:, None]
        _validS2 = jnp.arange(77)[None, :] < _lenS2[:, None]
        _causal = jnp.tril(jnp.ones((512, 512), dtype=bool))
        mask_BxSxS2_if1 = jnp.where(jnp.ones((4, 512, 77), dtype=bool), 1, 0).astype(jnp.int32)
        _g = jax.random.normal(jax.random.fold_in(_rk, 9001), (2, 2), jnp.float32)
        _g = jnp.sign(_g) * jnp.maximum(jnp.abs(_g), 1.0) + (_g == 0) * 1.0
        g_xattn = _g[0]
        g_ffn = _g[1]
        return (x, ctx_1024, itok_BxS_8_8191, itok_BxS2_1_8191, mask_BxSxS2_if1, g_xattn, g_ffn)
    x, ctx_1024, itok_BxS_8_8191, itok_BxS2_1_8191, mask_BxSxS2_if1, g_xattn, g_ffn = _rec_inputs()

    def _L0_xattn_setup():
        import jax, jax.numpy as jnp
        import numpy as np
        EMB = 128
        HEADS = 16
        HEAD_DIM = EMB // HEADS
        key = jax.random.key(seed)
        ks = jax.random.split(key, 7)
        B, Q, KV = (2, 256, 512)
        s = 1.0 / np.sqrt(EMB)
        return {'x': jax.random.normal(ks[0], (B, Q, EMB), dtype=jnp.float32), 'context': jax.random.normal(ks[1], (B, KV, EMB), dtype=jnp.float32), 'Wq': jax.random.normal(ks[2], (EMB, EMB), dtype=jnp.float32) * s, 'Wk': jax.random.normal(ks[3], (EMB, EMB), dtype=jnp.float32) * s, 'Wv': jax.random.normal(ks[4], (EMB, EMB), dtype=jnp.float32) * s, 'Wo': jax.random.normal(ks[5], (EMB, EMB), dtype=jnp.float32) * s, 'bo': jax.random.normal(ks[6], (EMB,), dtype=jnp.float32) * 0.01}
    _L0_xattn_all = _L0_xattn_setup()
    _L0_xattn_in = {k: v for k, v in _L0_xattn_all.items() if k in ('Wq', 'Wk', 'Wv', 'Wo', 'bo')}
    del _L0_xattn_all

    def _L0_ffn_setup():
        import jax, jax.numpy as jnp
        import numpy as np
        EMBED_DIM = 128
        HIDDEN_DIM = 512
        NUM_EXPERTS = 8
        TOP_K = 2
        key = jax.random.key(seed)
        ks = jax.random.split(key, 4)
        std1 = float(np.sqrt(2.0 / EMBED_DIM))
        std2 = float(np.sqrt(2.0 / HIDDEN_DIM))
        x = jax.random.normal(ks[0], (1, 256, EMBED_DIM), dtype=jnp.float32)
        w_router = jax.random.normal(ks[1], (EMBED_DIM, NUM_EXPERTS), dtype=jnp.float32) * 0.02
        w1 = jax.random.normal(ks[2], (NUM_EXPERTS, EMBED_DIM, HIDDEN_DIM), dtype=jnp.float32) * std1
        b1 = jnp.zeros((NUM_EXPERTS, HIDDEN_DIM), dtype=jnp.float32)
        w2 = jax.random.normal(ks[3], (NUM_EXPERTS, HIDDEN_DIM, EMBED_DIM), dtype=jnp.float32) * std2
        b2 = jnp.zeros((NUM_EXPERTS, EMBED_DIM), dtype=jnp.float32)
        return {'x': x, 'w_router': w_router, 'w1': w1, 'b1': b1, 'w2': w2, 'b2': b2}
    _L0_ffn_all = _L0_ffn_setup()
    _L0_ffn_in = {k: v for k, v in _L0_ffn_all.items() if k in ('w_router', 'w1', 'b1', 'w2', 'b2')}
    del _L0_ffn_all

    def _L1_xattn_setup():
        import jax, jax.numpy as jnp
        import numpy as np
        DIM = 128
        NUM_HEADS = 16
        HEAD_DIM = DIM // NUM_HEADS

        def _slopes(num_heads):
            ratio = 2.0 ** (-8.0 / num_heads)
            return jnp.asarray([ratio ** i for i in range(1, num_heads + 1)], dtype=jnp.float32)
        key = jax.random.key(seed)
        ks = jax.random.split(key, 10)
        b, q_len, k_len = (2, 256, 512)
        query = jax.random.normal(ks[0], (b, q_len, DIM), dtype=jnp.float32)
        keys = jax.random.normal(ks[1], (b, k_len, DIM), dtype=jnp.float32)
        values = jax.random.normal(ks[2], (b, k_len, DIM), dtype=jnp.float32)
        query_pos = jnp.sort(jax.random.randint(ks[3], (b, q_len), 0, 1024), axis=-1)
        key_pos = jnp.sort(jax.random.randint(ks[4], (b, k_len), 0, 1024), axis=-1)
        mask = jnp.ones((b, q_len, k_len), dtype=jnp.int32)
        lim = float(np.sqrt(6.0 / (DIM + DIM)))
        W_q = jax.random.uniform(ks[5], (DIM, DIM), minval=-lim, maxval=lim, dtype=jnp.float32)
        W_k = jax.random.uniform(ks[6], (DIM, DIM), minval=-lim, maxval=lim, dtype=jnp.float32)
        W_v = jax.random.uniform(ks[7], (DIM, DIM), minval=-lim, maxval=lim, dtype=jnp.float32)
        W_o = jax.random.uniform(ks[8], (DIM, DIM), minval=-lim, maxval=lim, dtype=jnp.float32)
        return {'query': query, 'keys': keys, 'values': values, 'W_q': W_q, 'W_k': W_k, 'W_v': W_v, 'W_o': W_o, 'query_pos': query_pos, 'key_pos': key_pos, 'mask': mask}
    _L1_xattn_all = _L1_xattn_setup()
    _L1_xattn_in = {k: v for k, v in _L1_xattn_all.items() if k in ('W_q', 'W_k', 'W_v', 'W_o')}
    del _L1_xattn_all

    def _L1_ffn_setup():
        import jax, jax.numpy as jnp
        import numpy as np
        NUM_EXPERTS = 8
        TOP_K = 2
        key = jax.random.key(seed)
        ks = jax.random.split(key, 6)
        B, S, D, F = (2, 256, 128, 512)
        E = NUM_EXPERTS
        sd = 1.0 / np.sqrt(D)
        sf = 1.0 / np.sqrt(F)
        return {'x': jax.random.normal(ks[0], (B, S, D), dtype=jnp.float32), 'gate_w': jax.random.normal(ks[1], (E, D), dtype=jnp.float32) * sd, 'w1': jax.random.uniform(ks[2], (F, E, D), dtype=jnp.float32, minval=-sd, maxval=sd), 'b1': jax.random.uniform(ks[3], (E, F), dtype=jnp.float32, minval=-sd, maxval=sd), 'w2': jax.random.uniform(ks[4], (D, E, F), dtype=jnp.float32, minval=-sf, maxval=sf), 'b2': jax.random.uniform(ks[5], (E, D), dtype=jnp.float32, minval=-sf, maxval=sf)}
    _L1_ffn_all = _L1_ffn_setup()
    _L1_ffn_in = {k: v for k, v in _L1_ffn_all.items() if k in ('gate_w', 'w1', 'b1', 'w2', 'b2')}
    del _L1_ffn_all
    return {'x': x, 'ctx_1024': ctx_1024, 'itok_BxS_8_8191': itok_BxS_8_8191, 'itok_BxS2_1_8191': itok_BxS2_1_8191, 'mask_BxSxS2_if1': mask_BxSxS2_if1, 'g_xattn': g_xattn, 'g_ffn': g_ffn, 'L0_xattn_Wq': _L0_xattn_in['Wq'], 'L0_xattn_Wk': _L0_xattn_in['Wk'], 'L0_xattn_Wv': _L0_xattn_in['Wv'], 'L0_xattn_Wo': _L0_xattn_in['Wo'], 'L0_xattn_bo': _L0_xattn_in['bo'], 'L0_ffn_w_router': _L0_ffn_in['w_router'], 'L0_ffn_w1': _L0_ffn_in['w1'], 'L0_ffn_b1': _L0_ffn_in['b1'], 'L0_ffn_w2': _L0_ffn_in['w2'], 'L0_ffn_b2': _L0_ffn_in['b2'], 'L1_xattn_W_q': _L1_xattn_in['W_q'], 'L1_xattn_W_k': _L1_xattn_in['W_k'], 'L1_xattn_W_v': _L1_xattn_in['W_v'], 'L1_xattn_W_o': _L1_xattn_in['W_o'], 'L1_ffn_gate_w': _L1_ffn_in['gate_w'], 'L1_ffn_w1': _L1_ffn_in['w1'], 'L1_ffn_b1': _L1_ffn_in['b1'], 'L1_ffn_w2': _L1_ffn_in['w2'], 'L1_ffn_b2': _L1_ffn_in['b2']}

def reference(x, ctx_1024, itok_BxS_8_8191, itok_BxS2_1_8191, mask_BxSxS2_if1, g_xattn, g_ffn, L0_xattn_Wq, L0_xattn_Wk, L0_xattn_Wv, L0_xattn_Wo, L0_xattn_bo, L0_ffn_w_router, L0_ffn_w1, L0_ffn_b1, L0_ffn_w2, L0_ffn_b2, L1_xattn_W_q, L1_xattn_W_k, L1_xattn_W_v, L1_xattn_W_o, L1_ffn_gate_w, L1_ffn_w1, L1_ffn_b1, L1_ffn_w2, L1_ffn_b2):
    import jax
    import jax.numpy as jnp

    def _L0_xattn_ref(x, context, Wq, Wk, Wv, Wo, bo):
        import jax, jax.numpy as jnp
        import numpy as np
        EMB = 128
        HEADS = 16
        HEAD_DIM = EMB // HEADS
        B, Qlen, _ = x.shape
        KVlen = context.shape[1]
        scale = jnp.asarray(HEAD_DIM ** 0.5, x.dtype)
        q = (x @ Wq.T).reshape(B, Qlen, HEADS, HEAD_DIM).transpose(0, 2, 1, 3)
        k = (context @ Wk.T).reshape(B, KVlen, HEADS, HEAD_DIM).transpose(0, 2, 1, 3)
        v = (context @ Wv.T).reshape(B, KVlen, HEADS, HEAD_DIM).transpose(0, 2, 1, 3)
        scores = jnp.einsum('bhqd,bhkd->bhqk', q, k) / scale
        attn = jax.nn.softmax(scores, axis=-1)
        out = jnp.einsum('bhqk,bhkd->bhqd', attn, v)
        out = out.transpose(0, 2, 1, 3).reshape(B, Qlen, EMB)
        return out @ Wo.T + bo

    def _L0_ffn_ref(x, w_router, w1, b1, w2, b2):
        import jax, jax.numpy as jnp
        import numpy as np
        EMBED_DIM = 128
        HIDDEN_DIM = 512
        NUM_EXPERTS = 8
        TOP_K = 2
        orig_shape = x.shape
        xf = x.reshape(-1, EMBED_DIM)
        logits = xf @ w_router
        probs = jax.nn.softmax(logits, axis=-1)
        topk_w, topk_idx = jax.lax.top_k(probs, TOP_K)
        mask = jax.nn.one_hot(topk_idx, NUM_EXPERTS, dtype=xf.dtype)
        weights = jnp.sum(topk_w[..., None] * mask, axis=1)
        h = jnp.einsum('te,ieh->tih', xf, w1) + b1
        h = jax.nn.gelu(h)
        out = jnp.einsum('tih,ihe->tie', h, w2) + b2
        out = jnp.sum(out * weights[..., None], axis=1)
        return out.reshape(orig_shape)

    def _L1_xattn_ref(query, keys, values, W_q, W_k, W_v, W_o, query_pos, key_pos, mask):
        import jax, jax.numpy as jnp
        import numpy as np
        DIM = 128
        NUM_HEADS = 16
        HEAD_DIM = DIM // NUM_HEADS

        def _slopes(num_heads):
            ratio = 2.0 ** (-8.0 / num_heads)
            return jnp.asarray([ratio ** i for i in range(1, num_heads + 1)], dtype=jnp.float32)
        b, q_len, _ = query.shape
        k_len = keys.shape[1]
        scale = 1.0 / np.sqrt(HEAD_DIM)
        Q = (query @ W_q.T).reshape(b, q_len, NUM_HEADS, HEAD_DIM).transpose(0, 2, 1, 3)
        K = (keys @ W_k.T).reshape(b, k_len, NUM_HEADS, HEAD_DIM).transpose(0, 2, 1, 3)
        V = (values @ W_v.T).reshape(b, k_len, NUM_HEADS, HEAD_DIM).transpose(0, 2, 1, 3)
        scores = jnp.einsum('bhqd,bhkd->bhqk', Q, K) * scale
        dist = (query_pos[:, :, None] - key_pos[:, None, :]).astype(scores.dtype)
        bias = -_slopes(NUM_HEADS)[None, :, None, None] * dist[:, None, :, :]
        scores = scores + bias
        scores = jnp.where(mask[:, None, :, :] == 0, -jnp.inf, scores)
        m = jnp.max(scores, axis=-1, keepdims=True)
        e = jnp.exp(scores - m)
        attn = e / (1.0 + jnp.sum(e, axis=-1, keepdims=True))
        out = jnp.einsum('bhqk,bhkd->bhqd', attn, V)
        out = out.transpose(0, 2, 1, 3).reshape(b, q_len, DIM)
        return out @ W_o.T

    def _L1_ffn_ref(x, gate_w, w1, b1, w2, b2):
        import jax, jax.numpy as jnp
        import numpy as np
        NUM_EXPERTS = 8
        TOP_K = 2
        logits = jnp.einsum('bsd,ed->bse', x, gate_w)
        probs = jax.nn.softmax(logits, axis=-1)
        topk_probs, topk_idx = jax.lax.top_k(probs, TOP_K)
        oh = jax.nn.one_hot(topk_idx, NUM_EXPERTS, dtype=x.dtype)
        h = jnp.einsum('bsd,fed,bske->bskf', x, w1, oh)
        h = h + jnp.take(b1, topk_idx, axis=0)
        h = jax.nn.gelu(h)
        y = jnp.einsum('bskf,def,bske->bskd', h, w2, oh)
        y = y + jnp.take(b2, topk_idx, axis=0)
        out = jnp.sum(y * topk_probs[..., None], axis=-2)
        return out
    x = x + jnp.tanh(g_xattn[0]) * _L0_xattn_ref(_layernorm(x, axis=-1), ctx_1024, L0_xattn_Wq, L0_xattn_Wk, L0_xattn_Wv, L0_xattn_Wo, L0_xattn_bo)
    x = x + jnp.tanh(g_ffn[0]) * _L0_ffn_ref(_layernorm(x, axis=-1), L0_ffn_w_router, L0_ffn_w1, L0_ffn_b1, L0_ffn_w2, L0_ffn_b2)
    x = x + jnp.tanh(g_xattn[1]) * _L1_xattn_ref(_layernorm(x, axis=-1), ctx_1024, ctx_1024, L1_xattn_W_q, L1_xattn_W_k, L1_xattn_W_v, L1_xattn_W_o, itok_BxS_8_8191, itok_BxS2_1_8191, mask_BxSxS2_if1)
    x = x + jnp.tanh(g_ffn[1]) * _L1_ffn_ref(_layernorm(x, axis=-1), L1_ffn_gate_w, L1_ffn_w1, L1_ffn_b1, L1_ffn_w2, L1_ffn_b2)
    return x

_drawn_inputs = setup_inputs


def setup_inputs(seed=0):
    import zlib

    import numpy as np

    out = dict(_drawn_inputs(seed))
    spreads = {'g_ffn': (-1.0, 0.6), 'L0_ffn_b1': (0.0, 0.529), 'L0_ffn_b2': (0.0, 0.541)}
    factors = {'L0_xattn_bo': 3.142, 'L1_ffn_b1': 8.0, 'L1_ffn_b2': 7.014}
    for name, (base, spread) in spreads.items():
        noise = np.random.default_rng([zlib.crc32(name.encode()), seed]).standard_normal(out[name].shape)
        drawn = base * np.exp(spread * noise) if base else spread * noise
        out[name] = jnp.asarray(drawn.astype(out[name].dtype))
    for name, factor in factors.items():
        out[name] = (out[name] * factor).astype(out[name].dtype)
    return out
```

```python
from contextlib import ExitStack

import numpy as np

import concourse.bass as bass
from concourse import mybir

F32, F32R, BF16 = mybir.dt.float32, mybir.dt.float32r, mybir.dt.bfloat16
I32, U32 = mybir.dt.int32, mybir.dt.uint32
ALU, ACT, AX = mybir.AluOpType, mybir.ActivationFunctionType, mybir.AxisListType

B, Q, KV, D, H, HD = 4, 512, 77, 128, 16, 8
E, F, TOPK = 8, 512, 2
P = 128
LAYERS = 2
NT = B * Q // P
TPB = Q // P
G = 4
JH = H // G
GK = JH * KV
PW = GK + 1
NC3 = 3
CH = PW // NC3
FC = F // P
SLOTS = B * Q * TOPK // P + E - 1
PAIRS = NT * TOPK
BIG = 1e30
HUGE = 3e38
LN_EPS = 1e-5

C_ID, C_LO = 0, 128
C_HI = 256
C_TRI = C_HI + SLOTS
C_TK = C_TRI + P
C_P = C_TK + PAIRS
C_HM = C_P + 1
C_NEG = C_HM + JH
C_QA = C_NEG + H
C_SL = C_QA + 3
C_BD = C_SL + 1
C_J = C_BD + LAYERS * NC3 * 32
C_LT = C_J + NT
C_LE = C_LT + E * E
C_END = C_LE + E * E


def constant_table():
    c = np.zeros((P, C_END), np.float32)
    p = np.arange(P)
    c[:, C_ID:C_ID + P] = np.eye(P)
    c[:, C_LO:C_LO + P] = np.arange(P)
    c[:, C_HI:C_HI + SLOTS] = np.arange(SLOTS)
    c[:, C_TRI:C_TRI + P] = p[:, None] < p[None, :]
    for t in range(NT):
        for k in range(TOPK):
            c[:, C_TK + TOPK * t + k] = t + NT * k + 1
    c[:, C_P] = p
    for j in range(JH):
        c[:96, C_HM + j] = (p[:96] % 32) // HD == j
    ratio = 2.0 ** (-8.0 / H)
    slope = np.array([ratio ** i for i in range(1, H + 1)], np.float32)
    high = (((slope.view(np.uint32) + 0x800) >> 12) << 12).astype(np.uint32).view(np.float32)
    for r, part in ((2, high), (3, slope - high), (4, high), (5, slope - high)):
        c[96 + r, C_NEG:C_NEG + H] = -part
    c[98:100, C_QA] = 1.0
    c[100:102, C_QA + 1] = 1.0
    c[96:98, C_QA + 2] = 1.0
    c[:H, C_SL] = slope
    for layer in range(LAYERS):
        for n in range(NC3):
            for i in range(CH):
                r = n * CH + i
                at = C_BD + (layer * NC3 + n) * 32
                if r < GK:
                    c[i, at + HD * (r // KV):at + HD * (r // KV) + HD] = 1.0
                elif layer == 1:
                    c[i, at:at + 32] = 1.0
    c[:, C_J:C_J + NT] = P * np.arange(NT)
    e = np.arange(E)
    c[:, C_LT:C_LT + E * E] = (e[None, :] < e[:, None]).reshape(1, -1)
    c[:, C_LE:C_LE + E * E] = (e[None, :] <= e[:, None]).reshape(1, -1)
    return c


def build(nc, x, ctxT, attnw, bo, gates, posq, posk, mask, router, w1, b1, w2, b2, consts, out):
    ctx = ExitStack()
    with ctx:
        def sb(name, shape, dt=F32):
            return ctx.enter_context(nc.sbuf_tensor(name, shape, dt))

        made = {}

        def sem(name):
            if name not in made:
                made[name] = ctx.enter_context(nc.semaphore(name))
            return made[name]

        cst = sb("cst", [P, C_END])
        aw = sb("aw", [P, LAYERS, 4, D])
        rw = sb("rw", [P, LAYERS, E])
        X = sb("X", [P, NT, D])
        XM = sb("XM", [P, NT, D])
        xnT = sb("xnT", [P, 2, Q])
        qhi = sb("qhi", [P, Q], F32R)
        qlo = sb("qlo", [P, Q], F32R)
        qaug = sb("qaug", [P, 2, G, Q], F32R)
        kaug = sb("kaug", [P, LAYERS, G * B, JH, KV], F32R)
        vbd = sb("vbd", [CH, LAYERS, NC3, B * G, 32])
        rden = sb("rden", [P, 256])
        pos = sb("pos", [P, B * Q], F32R)
        maskb = sb("maskb", [P, NT, KV], BF16)
        nanrow = sb("nanrow", [P, NT])
        W1 = sb("W1", [P, E * F])
        W2 = sb("W2", [P, E * FC * D])
        B1 = sb("B1", [P, E * F])
        B2 = sb("B2", [P, E * D])
        tgbo = sb("tgbo", [P, D])
        gt = sb("gt", [P, 4])
        tg = sb("tg", [P, 4])
        identb = sb("identb", [P, P], BF16)
        trib = sb("trib", [P, P], BF16)
        onesb = sb("onesb", [P, P], BF16)
        stat = sb("stat", [P, TPB, 6])
        mv = sb("mv", [P, TPB, 2])
        rstd = sb("rstd", [P, 3, TPB])
        mx = sb("mx", [P, 2, 8])
        arenaA = sb("arenaA", [P, 6144])
        arenaB = sb("arenaB", [P, 4352])
        PT = arenaA[0:CH, :].rearrange("p (u m q) -> p u m q", u=2, m=G * NC3)
        Dm = arenaB[:, 0:2 * 2 * GK].rearrange("p (n g k) -> p n g k", n=2, g=2)
        Pr = arenaB[:, 4 * GK:4 * GK + 2 * G * PW].rearrange("p (u g k) -> p u g k", u=2, g=G)
        OT = arenaB[:, 3704:4216].rearrange("p (u q) -> p u q", u=2)
        GX = arenaB[:, 0:512].rearrange("p (n d) -> p n d", n=4)
        XT = arenaB[:, 512:768].rearrange("p (n d) -> p n d", n=2)
        hb = arenaB[:, 768:1792].rearrange("p (n f) -> p n f", n=2)
        ge = arenaB[:, 1792:2816].rearrange("p (n f) -> p n f", n=2)
        hT = arenaB[:, 2816:3840].rearrange("p (n f) -> p n f", n=2)
        Yb = arenaB[:, 3840:4352].rearrange("p (n d) -> p n d", n=4)
        cmp1 = arenaA[:, 0:1024].rearrange("p (t e f) -> p t e f", t=NT, e=E)
        cmp2 = arenaA[:, 1024:2048].rearrange("p (t e f) -> p t e f", t=NT, e=E)
        ohlo = arenaA[:, 2048:4096].bitcast(BF16).rearrange("p (n c) -> p n c", n=PAIRS)
        ohhi = arenaA[:, 4096:4096 + PAIRS * SLOTS // 2].bitcast(BF16).rearrange("p (n c) -> p n c", n=PAIRS)
        ohpt = arenaA[:, 4736:4736 + PAIRS * SLOTS].bitcast(BF16).rearrange("p (n c) -> p n c", n=PAIRS)
        Yin = arenaA[:, 0:4096].rearrange("p (k t d) -> p k t d", k=TOPK, t=NT)
        posi = W1[96:128, 0:2048].bitcast(I32)
        posf = W1[96:128, 2048:4096]
        posh = W2[96:128, 0:2048].bitcast(F32R)
        KR = [W2[0:96, 1232 * l:1232 * l + 1232].bitcast(F32R) for l in range(LAYERS)]
        Vs = [W2[0:KV, 2464 + 512 * l:2464 + 512 * l + 512] for l in range(LAYERS)]
        Khl = arenaA[:, 4912:6144]
        Kh = [Khl[:, 616 * l:616 * l + 308].bitcast(F32R) for l in range(LAYERS)]
        Kl = [Khl[:, 616 * l + 308:616 * l + 616].bitcast(F32R) for l in range(LAYERS)]
        mski = B1[:, 0:NT * KV].bitcast(I32)
        ctxs = B1[:, 1232:1232 + B * KV]
        kpi = B1[0:H, 1540:1540 + B * KV].bitcast(I32)
        kpf = B1[0:H, 1848:1848 + B * KV]
        kph = B1[0:H, 2156:2156 + B * KV].bitcast(F32R)
        kpl = B1[0:H, 2464:2464 + B * KV].bitcast(F32R)
        mcnt = B1[:, 2772:2772 + NT * KV]
        qh32, ql32 = qhi[:, :].bitcast(F32), qlo[:, :].bitcast(F32)
        L, rank, ex, tmpE = (qh32[:, 128 * i:128 * i + 128].rearrange("p (t e) -> p t e", e=E) for i in range(4))
        M = ql32[:, 0:256].rearrange("p (k t e) -> p k t e", k=TOPK, e=E)
        n16 = ql32[:, 256:384].rearrange("p (e t) -> p e t", e=E)
        slot = ql32[:, 384:416].rearrange("p (t k) -> p t k", k=TOPK)
        slotb = ql32[:, 416:480].rearrange("p (a n) -> p a n", a=2)
        xof = arenaB[0:1, 0:SLOTS * E].rearrange("p (s e) -> p s e", e=E)
        Ab = sb("Ab", [P, NT, E], BF16)
        wk = sb("wk", [P, TOPK, NT])
        small = sb("small", [P, 4, NT])
        tbl = sb("tbl", [P, 4, E])
        sloti = sb("sloti", [P, 3, PAIRS], I32)
        xoff = sb("xoff", [1, SLOTS + 1])
        xofi = sb("xofi", [1, SLOTS + 1], I32)
        idf = sb("idf", [P, 3, SLOTS])
        gidx = sb("gidx", [P, SLOTS], U32)
        sidx = sb("sidx", [P, SLOTS], U32)
        idi = sb("idi", [P, SLOTS], I32)

        PS = ctx.enter_context(nc.psum_tensor("PS", [P, 8 * 512], F32))

        def bank(n):
            return PS[:, 512 * n:512 * n + 512]

        xnd = [nc.dram_tensor(f"xnd{l}", (B * Q, D), F32, kind="Internal").ap() for l in range(LAYERS)]
        yd = [nc.dram_tensor(f"yd{l}", (TOPK * B * Q, D), F32, kind="Internal").ap() for l in range(LAYERS)]

        ident = cst[:, C_ID:C_ID + P]
        x_v = x.rearrange("(t p) d -> p t d", p=P)
        out_v = out.rearrange("(t p) d -> p t d", p=P)

        block = ctx.enter_context(nc.Block())

        @block.sync
        def _(sp):
            sp.dma_start(B1[:, 1232:1232 + B * KV], ctxT).then_inc(sem("ctx_in"), 16)
            sp.dma_start(aw[:, 0], attnw[:, 0]).then_inc(sem("aw_in0"), 16)
            for b in range(B):
                sp.dma_start(X[:, TPB * b:TPB * b + TPB, :], x_v[:, TPB * b:TPB * b + TPB, :])\
                  .then_inc(sem(f"x_in{b}"), 16)
            sp.dma_start(aw[:, 1], attnw[:, 1]).then_inc(sem("aw_in1"), 16)
            sp.dma_start(mski, mask.rearrange("(t p) k -> p t k", p=P)).then_inc(sem("mask_in"), 16)
            sp.dma_start(rw[:, :, :], router).then_inc(sem("rw_in"), 16)

            def spread_k(l):
                sp.wait_ge(sem("kl_ready"), l + 1)
                for g in range(G):
                    for part, src in enumerate((Kh[l], Kl[l], Kh[l])):
                        sp.dma_start(KR[l][32 * part:32 * part + 32, 308 * g:308 * g + 308].bitcast(F32),
                                     src[32 * g:32 * g + 32, :].bitcast(F32)).then_inc(sem(f"kr_in{l}"), 16)

            def spread_v(l):
                sp.wait_ge(sem("v_ready"), l + 1)
                sp.wait_ge(sem("vbd_zero"), 1)
                for j in range(JH):
                    k = 0
                    while k < KV:
                        n, r = divmod(KV * j + k, CH)
                        m = min(CH - r, KV - k)
                        src = Vs[l][k:k + m, :].rearrange("k (b g j d) -> k (b g) j d", b=B, g=G, j=JH)
                        sp.dma_start(vbd[r:r + m, l, n, :, HD * j:HD * j + HD], src[:, :, j, :])\
                          .then_inc(sem(f"vbd_in{l}"), 16)
                        k += m

            def spread_q(l, b):
                u = b % 2
                sp.wait_ge(sem(f"qlo_ready{l}"), b + 1)
                if l:
                    sp.wait_ge(sem("pos_ready"), 1)
                    if b < 2:
                        sp.wait_ge(sem("s_ps0"), 2 * NT)
                if b >= 2:
                    sp.wait_ge(sem(f"s_ps{l}"), 2 * TPB * (b - 1))
                for g in range(G):
                    for part, src in enumerate((qhi, qhi, qlo)):
                        sp.dma_start(qaug[32 * part:32 * part + 32, u, g, :].bitcast(F32),
                                     src[32 * g:32 * g + 32, :].bitcast(F32)).then_inc(sem(f"qa_in{l}{b}"), 16)
                    if l:
                        sp.dma_start(qaug[96:128, u, g, :].bitcast(F32), pos[96:128, Q * b:Q * b + Q].bitcast(F32))\
                          .then_inc(sem(f"qa_in{l}{b}"), 16)

            spread_k(0)
            spread_q(0, 0)
            spread_v(0)
            spread_k(1)
            spread_v(1)
            sp.wait_ge(sem("kbias_ready"), 1)
            sp.wait_ge(sem("kconst_ready"), G)
            for h in range(H):
                g, j = divmod(h, JH)
                for r, src in enumerate((kph, kpl)):
                    dst = kaug[96 + r:97 + r, 1, B * g:B * g + B, j, :].bitcast(F32)
                    sp.dma_start(dst, src[h:h + 1, :].bitcast(F32).rearrange("p (b k) -> p b k", b=B))\
                      .then_inc(sem("kbias_in"), 16)

            def expert_weights(l):
                sp.dma_start(W1[:, :], w1[l]).then_inc(sem(f"ew_in{l}"), 16)
                sp.dma_start(W2[:, :], w2[l]).then_inc(sem(f"ew_in{l}"), 16)
                sp.dma_start(B1[:, :], b1[l:l + 1, :].to_broadcast([P, E * F])).then_inc(sem(f"ew_in{l}"), 16)
                sp.dma_start(B2[:, :], b2[l:l + 1, :].to_broadcast([P, E * D])).then_inc(sem(f"ew_in{l}"), 16)

            for l in range(LAYERS):
                for b in range(1, B):
                    if l == 0 and b == 2:
                        sp.wait_ge(sem("pos_ready"), 1)
                        sp.wait_ge(sem("kaug_ready"), 1)
                        sp.wait_ge(sem("kaug_ready1"), JH)
                        sp.wait_ge(sem("vbd_in0"), 16 * 6)
                        sp.wait_ge(sem("vbd_in1"), 16 * 6)
                        sp.wait_ge(sem("kbias_in"), 16 * 2 * H)
                        sp.wait_ge(sem("mask_ready"), 1)
                        expert_weights(0)
                    spread_q(l, b)
                for b in range(B):
                    sp.wait_ge(sem(f"xm_ready{l}"), b + 1)
                    sp.dma_start(xnd[l].rearrange("(t p) d -> p t d", p=P)[:, TPB * b:TPB * b + TPB, :],
                                 XM[:, TPB * b:TPB * b + TPB, :]).then_inc(sem(f"xnd_in{l}"), 16)
                for j in range(4):
                    sp.wait_ge(sem(f"scat{l}{j}"), 16 * ((SLOTS - j + 3) // 4))
                yv = yd[l].rearrange("(k t p) d -> p k t d", k=TOPK, p=P)
                for b in range(B):
                    for k in range(TOPK):
                        sp.dma_start(Yin[:, k, TPB * b:TPB * b + TPB, :], yv[:, k, TPB * b:TPB * b + TPB, :])\
                          .then_inc(sem(f"y_in{l}{b}"), 16)
                if l == 0:
                    expert_weights(1)
                    spread_q(1, 0)
            for b in range(B):
                sp.wait_ge(sem("x_done1"), b + 1)
                sp.dma_start(out_v[:, TPB * b:TPB * b + TPB, :], X[:, TPB * b:TPB * b + TPB, :])\
                  .then_inc(sem("out_done"), 16)
            sp.wait_ge(sem("out_done"), 16 * B)

        @block.gpsimd
        def _(pool):
            chain = [0]

            def link(ins):
                chain[0] += 1
                ins.then_inc(sem("pool_chain"), 1)
                pool.wait_ge(sem("pool_chain"), chain[0])

            def apart(name, count):
                pool.wait_ge(sem(name), count)

            pool.memset(vbd[:, :, :, :, :], 0.0).then_inc(sem("vbd_zero"), 1)
            pool.memset(onesb[:, :], 1.0).then_inc(sem("ones_ready"), 1)
            pool.memset(Pr[:, :, :, GK:PW], 1.0).then_inc(sem("pad_ready0"), 1)
            pool.wait_ge(sem("cst_in"), 16)
            pool.tensor_copy(identb[:, :], ident).then_inc(sem("identb_ready"), 1)
            pool.tensor_copy(trib[:, :], cst[:, C_TRI:C_TRI + P]).then_inc(sem("trib_ready"), 1)

            def biased(b):
                pool.wait_ge(sem("xn_ready0"), b + 1)
                pool.tensor_tensor(X[:, TPB * b:TPB * b + TPB, :], X[:, TPB * b:TPB * b + TPB, :],
                                   tgbo[:, :].unsqueeze(1).to_broadcast([P, TPB, D]), ALU.add)\
                    .then_inc(sem("xb_ready0"), 1)
                apart("xb_ready0", b + 1)

            pool.wait_ge(sem("tg_ready"), 1)
            pool.wait_ge(sem("bo_in"), 16)
            link(pool.tensor_scalar(tgbo[:, :], tgbo[:, :], tg[:, 0:1], None, ALU.mult))
            biased(0)
            biased(1)
            neg = cst[96:128, C_NEG:C_NEG + H].rearrange("p (g j) -> p g j", g=G)
            kc = kaug[96:128, 1, :, :, :].rearrange("p (g b) j k -> p g b j k", g=G)
            for g in range(G):
                pool.tensor_copy(kc[:, g], neg[:, g, :].unsqueeze(1).unsqueeze(3).to_broadcast([32, B, JH, KV]))\
                    .then_inc(sem("kconst_ready"), 1)
                apart("kconst_ready", g + 1)
            pool.wait_ge(sem("kpos_in"), 16)
            link(pool.tensor_copy(kpf, kpi))
            link(pool.tensor_scalar(kpf, kpf, cst[0:H, C_SL:C_SL + 1], None, ALU.mult))
            link(pool.tensor_copy(kph, kpf))
            pool.tensor_tensor(kpl, kpf, kph.bitcast(F32), ALU.subtract).then_inc(sem("kbias_ready"), 1)
            apart("kbias_ready", 1)
            pool.wait_ge(sem("kr_in1"), 16 * 3 * G)
            for j in range(JH):
                pool.tensor_scalar(kaug[0:96, 1, :, j, :],
                                          KR[1].bitcast(F32).rearrange("p (n k) -> p n k", k=KV),
                                   cst[0:96, C_HM + j:C_HM + j + 1], None, ALU.mult)\
                    .then_inc(sem("kaug_ready1"), 1)
                apart("kaug_ready1", j + 1)
            pool.wait_ge(sem("qpos_in"), 16)
            link(pool.tensor_copy(posf, posi))
            link(pool.tensor_copy(posh, posf))
            link(pool.tensor_tensor(posf, posf, posh.bitcast(F32), ALU.subtract))
            link(pool.tensor_scalar(posf, posf, cst[96:128, C_QA + 1:C_QA + 2],
                                    cst[96:128, C_QA + 2:C_QA + 3], ALU.mult, ALU.add))
            link(pool.tensor_scalar(posh, posh.bitcast(F32), cst[96:128, C_QA:C_QA + 1], None, ALU.mult))
            pool.tensor_tensor(pos[96:128, :], posh.bitcast(F32), posf, ALU.add).then_inc(sem("pos_ready"), 1)
            apart("pos_ready", 1)
            pool.wait_ge(sem("mask_in"), 16)
            link(pool.tensor_scalar(mcnt, mski, 0.0, None, ALU.is_equal))
            pool.tensor_scalar(maskb[:, :, :], mcnt.rearrange("p (t k) -> p t k", t=NT), -BIG, None, ALU.mult)\
                .then_inc(sem("maskb_ready"), 1)
            apart("maskb_ready", 1)
            biased(2)
            biased(3)

            for l in range(LAYERS):
                if l:
                    pool.wait_ge(sem("y_ready0"), SLOTS)
                    for j in range(4):
                        pool.wait_ge(sem(f"scat0{j}"), 16 * ((SLOTS - j + 3) // 4))
                    pool.memset(Pr[:, :, :, GK:PW], 1.0).then_inc(sem("pad_ready1"), 1)
                    apart("pad_ready1", 1)
                    for b in range(B):
                        pool.wait_ge(sem("xn_ready1"), b + 1)
                        pool.wait_ge(sem("mask_ready"), 1)
                        pool.tensor_tensor(X[:, TPB * b:TPB * b + TPB, :], X[:, TPB * b:TPB * b + TPB, :],
                                           nanrow[:, TPB * b:TPB * b + TPB].unsqueeze(2).to_broadcast([P, TPB, D]),
                                           ALU.add).then_inc(sem("xb_ready1"), 1)
                        apart("xb_ready1", b + 1)

                def gather(s):
                    pool.indirect_dma_start(GX[:, s % 4, :], None, xnd[l],
                                            bass.IndirectOffsetOnAxis(ap=gidx[:, s:s + 1], axis=0))\
                        .then_inc(sem(f"gath{l}{s % 4}"), 16)

                pool.wait_ge(sem(f"gidx_ready{l}"), 1)
                pool.wait_ge(sem(f"xnd_in{l}"), 16 * B)
                pool.wait_ge(sem(f"resid{l}"), B * 2)
                for s in range(4):
                    gather(s)
                for s in range(SLOTS):
                    if s + 4 < SLOTS:
                        pool.wait_ge(sem(f"xT_ps{l}"), s + 1)
                        gather(s + 4)
                    pool.wait_ge(sem(f"y_ready{l}"), s + 1)
                    pool.indirect_dma_start(yd[l], bass.IndirectOffsetOnAxis(ap=sidx[:, s:s + 1], axis=0),
                                            Yb[:, s % 4, :], None, bounds_check=TOPK * B * Q - 1,
                                            oob_is_err=False).then_inc(sem(f"scat{l}{s % 4}"), 16)

        @block.scalar
        def _(act):
            act.dma_start(cst[:, :], consts).then_inc(sem("cst_in"), 16)
            act.dma_start(gt[:, :], gates.to_broadcast([P, 4])).then_inc(sem("gt_in"), 16)
            act.dma_start(tgbo[:, :], bo.to_broadcast([P, D])).then_inc(sem("bo_in"), 16)
            act.dma_start(kpi, posk.to_broadcast([H, B * KV])).then_inc(sem("kpos_in"), 16)
            act.dma_start(posi, posq.to_broadcast([32, B * Q])).then_inc(sem("qpos_in"), 16)
            act.wait_ge(sem("gt_in"), 16)
            act.activation(tg[:, :], gt[:, :], ACT.Tanh).then_inc(sem("tg_ready"), 1)

            def k_high(l):
                act.wait_ge(sem("k_ps"), l + 1)
                act.activation(Kh[l], bank(l)[:, 0:B * KV], ACT.Copy, scale=HD ** -0.5).then_inc(sem("kh_ready"), 1)

            def v_copy(l):
                act.wait_ge(sem("v_ps"), l + 1)
                act.activation(Vs[l], bank(2 + l)[0:KV, :], ACT.Copy).then_inc(sem("v_ready"), 1)

            def xnT_copy(l, b):
                act.wait_ge(sem(f"xt_ps{l}"), b + 1)
                act.activation(xnT[:, b % 2, :], bank(7), ACT.Copy).then_inc(sem(f"xt_ready{l}"), 1)

            def q_high(l, b):
                act.wait_ge(sem(f"q_ps{l}"), b + 1)
                if b:
                    act.wait_ge(sem(f"qa_in{l}{b - 1}"), 16 * G * (4 if l else 3))
                act.activation(qhi[:, :], bank(7), ACT.Copy).then_inc(sem(f"qhi_ready{l}"), 1)

            def attention(l):
                if l == 0:
                    k_high(0)
                xnT_copy(l, 0)
                q_high(l, 0)
                if l == 0:
                    v_copy(0)
                    k_high(1)
                    v_copy(1)
                for t in range(NT):
                    b = t // TPB
                    for hf in range(2):
                        n = 2 * t + hf
                        act.wait_ge(sem(f"sub{l}"), n + 1)
                        if t >= 2:
                            act.wait_ge(sem(f"pt_ps{l}"), G * (t - 1))
                        act.activation(Pr[:, t % 2, 2 * hf:2 * hf + 2, 0:GK], Dm[:, hf, :, :], ACT.Exp)\
                           .then_inc(sem(f"exp{l}"), 1)
                    if t % TPB == 1 and b + 1 < B:
                        q_high(l, b + 1)
                    v = t // 2
                    if t % 2 == 0 and v >= 2:
                        act.wait_ge(sem(f"o_ps{l}"), v - 1)
                    if l == 0 and t == 2:
                        act.wait_ge(sem("kr_in1"), 16 * 3 * G)
                    for g in range(G):
                        m = G * t + g
                        act.wait_ge(sem(f"pt_ps{l}"), m + 1)
                        dst = PT[:, v % 2, NC3 * g:NC3 * g + NC3, P * (t % 2):P * (t % 2) + P]
                        act.activation(dst, bank(4 + m % 2)[0:CH, 0:NC3 * P].rearrange("p (c q) -> p c q", c=NC3),
                                       ACT.Copy).then_inc(sem(f"pt_ready{l}"), 1)
                    if t % TPB == 0 and b + 1 < B:
                        xnT_copy(l, b + 1)

            def routing(l):
                for b in range(B):
                    act.wait_ge(sem(f"xmt_ps{l}"), b + 1)
                    if b >= 2:
                        act.wait_ge(sem(f"lg_ps{l}"), b - 1)
                    act.activation(xnT[:, b % 2, :], bank(b), ACT.Copy).then_inc(sem(f"xmt_ready{l}"), 1)
                act.wait_ge(sem(f"lsub{l}"), 1)
                act.activation(ex, tmpE, ACT.Exp).then_inc(sem(f"lexp{l}"), 1)

            def experts(l):
                def gelu(s, j):
                    act.wait_ge(sem(f"h_ready{l}"), s + 1)
                    act.activation(ge[:, j % 2, :], hb[:, j % 2, :], ACT.Gelu_apprx_tanh)\
                       .then_inc(sem(f"gelu{l}"), 1)

                def hT_copy(s, j):
                    act.wait_ge(sem(f"ht_ps{l}"), s + 1)
                    act.activation(hT[:, j % 2, :], bank(4 + j % 2), ACT.Copy).then_inc(sem(f"ht_ready{l}"), 1)

                gelu(0, 0)
                gelu(1, 1)
                for s in range(4):
                    hT_copy(s, s)
                    gelu(s + 2, s + 2)
                with act.Fori(1, (SLOTS - 3) // 4) as i:
                    for j in range(4):
                        hT_copy(4 * i + j, j)
                        gelu(4 * i + j + 2, j + 2)
                for s in range(SLOTS - 3, SLOTS):
                    hT_copy(s, s)
                    if s + 2 < SLOTS:
                        gelu(s + 2, s + 2)

            for l in range(LAYERS):
                attention(l)
                routing(l)
                experts(l)

        @block.tensor
        def _(pe):
            pe.wait_ge(sem("cst_in"), 16)
            pe.wait_ge(sem("ctx_in"), 16)

            def k_and_v(l):
                pe.wait_ge(sem(f"aw_in{l}"), 16)
                pe.matmul(bank(l)[:, 0:B * KV], aw[:, l, 1, :], ctxs, start=True, stop=True)\
                  .then_inc(sem("k_ps"), 1)
                for b in range(B):
                    last = pe.matmul(bank(2 + l)[0:KV, P * b:P * b + P], ctxs[:, KV * b:KV * b + KV],
                                     aw[:, l, 2, :], start=True, stop=True)
                last.then_inc(sem("v_ps"), 1)

            sent = [0, 0]

            def xn_turn(l, b):
                pe.wait_ge(sem(f"xn_ready{l}"), b + 1)
                if sent[l]:
                    pe.wait_ge(sem(f"resid{l}"), sent[l])
                for i in range(TPB):
                    last = pe.transpose(bank(7)[:, P * i:P * i + P], XM[:, TPB * b + i, :], ident)
                last.then_inc(sem(f"xt_ps{l}"), 1)

            def q_product(l, b):
                pe.wait_ge(sem(f"xt_ready{l}"), b + 1)
                pe.matmul(bank(7), aw[:, l, 0, :], xnT[:, b % 2, :], start=True, stop=True)\
                  .then_inc(sem(f"q_ps{l}"), 1)

            def scores(l, t):
                b = t // TPB
                if t == 0:
                    pe.wait_ge(sem("kaug_ready" if l == 0 else "kaug_ready1"), 1 if l == 0 else JH)
                    if l:
                        pe.wait_ge(sem("kbias_in"), 16 * 2 * H)
                        pe.wait_ge(sem("maskb_ready"), 1)
                        pe.wait_ge(sem("identb_ready"), 1)
                if t % TPB == 0:
                    pe.wait_ge(sem(f"qa_in{l}{b}"), 16 * G * (4 if l else 3))
                K = P if l else 96
                for hf in range(2):
                    n = 2 * t + hf
                    if n >= 2:
                        pe.wait_ge(sem(f"sub{l}"), n - 1)
                    for g in (2 * hf, 2 * hf + 1):
                        at = P * (t % TPB)
                        rhs = kaug[0:K, l, B * g + b, :, :].rearrange("p j k -> p (j k)")
                        last = pe.matmul(bank(g)[:, 0:GK], qaug[0:K, b % 2, g, at:at + P], rhs,
                                         start=True, stop=(l == 0))
                        if l:
                            last = pe.matmul(bank(g)[:, 0:GK].rearrange("p (j k) -> p j k", j=JH), identb[:, :],
                                             maskb[:, t, :].unsqueeze(1).to_broadcast([P, JH, KV]),
                                             start=False, stop=True)
                    last.then_inc(sem(f"s_ps{l}"), 1)

            def turn(l, t):
                for g in range(G):
                    m = G * t + g
                    if g % 2 == 0:
                        pe.wait_ge(sem(f"exp{l}"), 2 * t + g // 2 + 1)
                    if t == 0 and g == 0:
                        pe.wait_ge(sem(f"pad_ready{l}"), 1)
                    if m >= 2:
                        pe.wait_ge(sem(f"pt_ready{l}"), m - 1)
                    for c in range(NC3):
                        last = pe.transpose(bank(4 + m % 2)[0:CH, P * c:P * c + P],
                                            Pr[:, t % 2, g, CH * c:CH * c + CH], ident)
                    last.then_inc(sem(f"pt_ps{l}"), 1)

            def values(l, v):
                b = v // 2
                pe.wait_ge(sem(f"pt_ready{l}"), 2 * G * (v + 1))
                if v == 0:
                    pe.wait_ge(sem(f"vbd_in{l}"), 16 * 6)
                else:
                    pe.wait_ge(sem(f"ot_ready{l}"), v)
                for den in range(2):
                    for c in range(NC3):
                        for g in range(G):
                            at = C_BD + (l * NC3 + c) * 32
                            lhs = cst[0:CH, at:at + 32] if den else vbd[:, l, c, G * b + g, :]
                            last = pe.matmul(bank(6)[32 * g:32 * g + 32, 256 * den:256 * den + 256], lhs,
                                             PT[:, v % 2, NC3 * g + c, :], start=(c == 0), stop=(c == NC3 - 1))
                last.then_inc(sem(f"o_ps{l}"), 1)

            def out_product(l, v):
                pe.wait_ge(sem(f"ot_ready{l}"), v + 1)
                if v:
                    pe.wait_ge(sem(f"resid{l}"), v)
                pe.wait_ge(sem(f"qlo_ready{l}"), min(1 + (v + 3) // 2, B))
                for i in range(2):
                    last = pe.matmul(bank(7)[:, P * i:P * i + P], OT[:, v % 2, P * i:P * i + P],
                                     aw[:, l, 3, :], start=True, stop=True)
                last.then_inc(sem(f"y_ps{l}"), 1)
                sent[l] += 1

            def attention(l):
                if l == 0:
                    k_and_v(0)
                xn_turn(l, 0)
                q_product(l, 0)
                if l == 0:
                    k_and_v(1)
                    pe.wait_ge(sem("kl_ready"), 2)
                    pe.wait_ge(sem("v_ready"), 2)
                scores(l, 0)
                for t in range(NT):
                    b = t // TPB
                    if t + 1 < NT:
                        scores(l, t + 1)
                    if t % TPB == 1 and b + 1 < B:
                        q_product(l, b + 1)
                    turn(l, t)
                    if t % TPB == 0 and b + 1 < B:
                        xn_turn(l, b + 1)
                    if t % 2:
                        if t > 1:
                            out_product(l, t // 2 - 1)
                        values(l, t // 2)
                out_product(l, NT // 2 - 1)

            def routing(l):
                for b in range(B):
                    pe.wait_ge(sem(f"xm_ready{l}"), b + 1)
                    for i in range(TPB):
                        last = pe.transpose(bank(b)[:, P * i:P * i + P], XM[:, TPB * b + i, :], ident)
                    last.then_inc(sem(f"xmt_ps{l}"), 1)
                if l == 0:
                    pe.wait_ge(sem("rw_in"), 16)
                pe.wait_ge(sem(f"resid{l}"), 2 * B)
                for b in range(B):
                    pe.wait_ge(sem(f"xmt_ready{l}"), b + 1)
                    for i in range(TPB):
                        t = TPB * b + i
                        last = pe.matmul(bank(7)[:, E * t:E * t + E], xnT[:, b % 2, P * i:P * i + P],
                                         rw[:, l, :], start=True, stop=True)
                    last.then_inc(sem(f"lg_ps{l}"), 1)
                pe.wait_ge(sem(f"chosen{l}"), 1)
                if l == 0:
                    pe.wait_ge(sem("trib_ready"), 1)
                    pe.wait_ge(sem("ones_ready"), 1)
                place = bank(6)[:, 0:(NT + 1) * E]
                pe.matmul(place[:, 0:NT * E], trib[:, :], Ab[:, :, :].rearrange("p t e -> p (t e)"),
                          start=True, stop=False, skip_group_check=True)
                for t in range(NT):
                    n = NT - t
                    last = pe.matmul(place[:, E * (t + 1):].rearrange("p (t e) -> p t e", e=E), onesb[:, :],
                                     Ab[:, t, :].unsqueeze(1).to_broadcast([P, n, E]),
                                     start=False, stop=(t == NT - 1), skip_group_check=True)
                last.then_inc(sem(f"place_ps{l}"), 1)
                pe.wait_ge(sem(f"onehot{l}"), 1)
                for n in range(PAIRS):
                    last = pe.matmul(bank(5)[:, 0:2 * SLOTS], ohlo[:, n, :], ohpt[:, n, :],
                                     start=(n == 0), stop=(n == PAIRS - 1))
                last.then_inc(sem(f"inv_ps{l}"), 1)

            def experts(l):
                pe.wait_ge(sem(f"xof_ready{l}"), 1)
                pe.wait_ge(sem(f"ew_in{l}"), 16 * 4)

                def expert_of(s):
                    return pe.value_load(xofi[0:1, bass.ds(s, 1)], min_val=0, max_val=E - 1)

                def x_turn(s, j, round_):
                    pe.wait_ge(sem(f"gath{l}{j % 4}"), 16 * (round_ + 1))
                    if not isinstance(s, int) or s >= 2:
                        pe.wait_ge(sem(f"xT_ready{l}"), s - 1)
                    pe.transpose(bank(j % 2)[:, 0:P], GX[:, j % 4, :], ident).then_inc(sem(f"xT_ps{l}"), 1)

                def up(s, j):
                    e = expert_of(s)
                    pe.wait_ge(sem(f"xT_ready{l}"), s + 1)
                    if not isinstance(s, int) or s >= 2:
                        pe.wait_ge(sem(f"h_ready{l}"), s - 1)
                    pe.matmul(bank(2 + j % 2), XT[:, j % 2, :], W1[:, bass.ds(e * F, F)], start=True, stop=True)\
                      .then_inc(sem(f"h_ps{l}"), 1)

                def h_turn(s, j):
                    pe.wait_ge(sem(f"gelu{l}"), s + 1)
                    if not isinstance(s, int) or s >= 2:
                        pe.wait_ge(sem(f"ht_ready{l}"), s - 1)
                    for c in range(FC):
                        last = pe.transpose(bank(4 + j % 2)[:, P * c:P * c + P], ge[:, j % 2, P * c:P * c + P], ident)
                    last.then_inc(sem(f"ht_ps{l}"), 1)

                def down(s, j):
                    e = expert_of(s)
                    pe.wait_ge(sem(f"ht_ready{l}"), s + 1)
                    if not isinstance(s, int) or s >= 2:
                        pe.wait_ge(sem(f"y_ready{l}"), s - 1)
                    for c in range(FC):
                        last = pe.matmul(bank(6 + j % 2)[:, 0:D], hT[:, j % 2, P * c:P * c + P],
                                         W2[:, bass.ds(e * (FC * D) + c * D, D)], start=(c == 0), stop=(c == FC - 1))
                    last.then_inc(sem(f"yt_ps{l}"), 1)

                for s in range(3):
                    x_turn(s, s, 0)
                for s in range(2):
                    up(s, s)

                def step(s, j, round_):
                    h_turn(s, j)
                    x_turn(s + 3, j + 3, round_ + (j + 3) // 4)
                    up(s + 2, j + 2)
                    down(s, j)

                for s in range(4):
                    step(s, s, 0)
                with pe.Fori(1, (SLOTS - 3) // 4) as i:
                    for j in range(4):
                        step(4 * i + j, j, i)
                for s in range(SLOTS - 3, SLOTS):
                    h_turn(s, s)
                    if s + 2 < SLOTS:
                        up(s + 2, s + 2)
                    down(s, s)

            for l in range(LAYERS):
                attention(l)
                routing(l)
                experts(l)

        @block.vector
        def _(dve):
            chain = [0]

            def link(ins):
                chain[0] += 1
                ins.then_inc(sem("dve_chain"), 1)
                dve.wait_ge(sem("dve_chain"), chain[0])

            def normalise(src, dst):
                for i in range(TPB):
                    last = dve.bn_stats(stat[:, i, :], src[:, i, :])
                link(last)
                for i in range(TPB):
                    last = dve.bn_aggr(mv[:, i, :], stat[:, i, :])
                link(last)
                y, yi, var, t = rstd[:, 0, :], rstd[:, 0, :].bitcast(I32), rstd[:, 1, :], rstd[:, 2, :]
                link(dve.tensor_scalar(var, mv[:, :, 1], LN_EPS, None, ALU.add))
                link(dve.tensor_scalar(yi, var.bitcast(I32), 1, None, ALU.logical_shift_right))
                link(dve.tensor_scalar(yi, yi, -1.0, float(0x5F3759DF), ALU.mult, ALU.add))
                for _ in range(3):
                    link(dve.tensor_tensor(t, y, y, ALU.mult))
                    link(dve.tensor_tensor(t, t, var, ALU.mult))
                    link(dve.tensor_scalar(t, t, -0.5, 1.5, ALU.mult, ALU.add))
                    link(dve.tensor_tensor(y, y, t, ALU.mult))
                for i in range(TPB):
                    last = dve.tensor_scalar(dst[:, i, :], src[:, i, :], mv[:, i, 0:1], y[:, i:i + 1],
                                             ALU.subtract, ALU.mult)
                return last

            def batch_tiles(t, b):
                return t[:, TPB * b:TPB * b + TPB, :]

            def norm_x(l, b):
                if l == 0:
                    dve.wait_ge(sem(f"x_in{b}"), 16)
                else:
                    dve.wait_ge(sem("xnd_in0"), 16 * B)
                normalise(batch_tiles(X, b), batch_tiles(XM, b)).then_inc(sem(f"xn_ready{l}"), 1)

            def k_low(l):
                dve.wait_ge(sem("kh_ready"), l + 1)
                dve.scalar_tensor_tensor(out=Kl[l], in0=bank(l)[:, 0:B * KV], scalar=HD ** -0.5,
                                         in1=Kh[l].bitcast(F32), op0=ALU.mult, op1=ALU.subtract)\
                   .then_inc(sem("kl_ready"), 1)

            def q_low(l, b):
                dve.wait_ge(sem(f"qhi_ready{l}"), b + 1)
                dve.tensor_tensor(qlo[:, :], bank(7), qhi[:, :].bitcast(F32), ALU.subtract)\
                   .then_inc(sem(f"qlo_ready{l}"), 1)

            def soft(l, n):
                dve.wait_ge(sem(f"s_ps{l}"), n + 1)
                hf = n % 2
                s = PS[:, 1024 * hf:1024 * hf + 1024].rearrange("p (g c) -> p g c", g=2)[:, :, 0:GK]\
                    .rearrange("p g (j k) -> p g j k", j=JH)
                m = mx[:, hf, :].rearrange("p (g j) -> p g j", g=2)
                link(dve.tensor_reduce(m, s, AX.X, ALU.max))
                if n >= 2:
                    dve.wait_ge(sem(f"exp{l}"), n - 1)
                dve.tensor_tensor(Dm[:, hf, :, :].rearrange("p g (j k) -> p g j k", j=JH), s,
                                  m.unsqueeze(3).to_broadcast([P, 2, JH, KV]), ALU.subtract)\
                   .then_inc(sem(f"sub{l}"), 1)

            def divide(l, v):
                dve.wait_ge(sem(f"o_ps{l}"), v + 1)
                link(dve.reciprocal(rden[:, :], bank(6)[:, 256:512]))
                dve.tensor_tensor(OT[:, v % 2, :], bank(6)[:, 0:256], rden[:, :], ALU.mult)\
                   .then_inc(sem(f"ot_ready{l}"), 1)

            def residual(l, v):
                dve.wait_ge(sem(f"y_ps{l}"), v + 1)
                dve.wait_ge(sem(f"xb_ready{l}"), v // 2 + 1)
                xs = X[:, 2 * v:2 * v + 2, :]
                ins = dve.scalar_tensor_tensor(out=xs, in0=bank(7)[:, 0:256].rearrange("p (t d) -> p t d", t=2),
                                               scalar=tg[:, l:l + 1], in1=xs, op0=ALU.mult, op1=ALU.add)
                ins.then_inc(sem(f"resid{l}"), 1)
                if v % 2:
                    b = v // 2
                    dve.wait_ge(sem(f"resid{l}"), v + 1)
                    dve.wait_ge(sem(f"xt_ps{l}"), b + 1)
                    normalise(batch_tiles(X, b), batch_tiles(XM, b)).then_inc(sem(f"xm_ready{l}"), 1)

            def attention(l):
                if l == 0:
                    norm_x(0, 0)
                    dve.wait_ge(sem("cst_in"), 16)
                    k_low(0)
                    q_low(0, 0)
                    norm_x(0, 1)
                    dve.wait_ge(sem("kr_in0"), 16 * 3 * G)
                    for j in range(JH):
                        last = dve.tensor_scalar(kaug[0:96, 0, :, j, :],
                                                 KR[0].bitcast(F32).rearrange("p (n k) -> p n k", k=KV),
                                                 cst[0:96, C_HM + j:C_HM + j + 1], None, ALU.mult)
                    last.then_inc(sem("kaug_ready"), 1)
                    k_low(1)
                else:
                    q_low(l, 0)
                for t in range(NT):
                    b = t // TPB
                    soft(l, 2 * t)
                    soft(l, 2 * t + 1)
                    if l == 0 and t == 5:
                        dve.wait_ge(sem("maskb_ready"), 1)
                        link(dve.tensor_reduce(nanrow[:, :], mcnt.rearrange("p (t k) -> p t k", t=NT), AX.X, ALU.min))
                        link(dve.tensor_scalar(nanrow[:, :], nanrow[:, :], -HUGE, 10.0, ALU.mult, ALU.mult))
                        dve.tensor_scalar(nanrow[:, :], nanrow[:, :], 0.0, None, ALU.mult).then_inc(sem("mask_ready"), 1)
                    if t % TPB == 1 and b + 1 < B:
                        q_low(l, b + 1)
                    if t % TPB == 2 and b + 2 < B:
                        norm_x(l, b + 2)
                    if t % 2 == 0 and t >= 4:
                        residual(l, t // 2 - 2)
                    if t % 2 == 0 and t >= 2:
                        divide(l, t // 2 - 1)
                residual(l, NT // 2 - 2)
                divide(l, NT // 2 - 1)
                residual(l, NT // 2 - 1)

            def routing(l):
                dve.wait_ge(sem(f"lg_ps{l}"), B)
                link(dve.tensor_copy(L, bank(7)[:, 0:NT * E].rearrange("p (t e) -> p t e", e=E)))
                full = [P, NT, E, E]
                other = L.unsqueeze(2).to_broadcast(full)
                own = L.unsqueeze(3).to_broadcast(full)
                dve.tensor_tensor(cmp1, other, own, ALU.is_equal)
                link(dve.tensor_reduce(small[:, 0, :], L, AX.X, ALU.max))
                dve.tensor_tensor(cmp1, cmp1, cst[:, C_LT:C_LT + E * E].rearrange("p (e f) -> p e f", e=E)
                                  .unsqueeze(1).to_broadcast(full), ALU.mult)
                dve.tensor_tensor(tmpE, L, small[:, 0, :].unsqueeze(2).to_broadcast([P, NT, E]),
                                  ALU.subtract).then_inc(sem(f"lsub{l}"), 1)
                link(dve.tensor_tensor(cmp2, other, own, ALU.is_gt))
                link(dve.tensor_tensor(cmp1, cmp1, cmp2, ALU.add))
                link(dve.tensor_reduce(rank, cmp1, AX.X, ALU.add))
                dve.tensor_scalar(Ab[:, :, :], rank, 1.5, None, ALU.is_lt).then_inc(sem(f"chosen{l}"), 1)
                for k in range(TOPK):
                    last = dve.tensor_scalar(M[:, k, :, :], rank, float(k), None, ALU.is_equal)
                link(last)
                dve.wait_ge(sem(f"lexp{l}"), 1)
                link(dve.tensor_reduce(small[:, 1, :], ex, AX.X, ALU.add))
                link(dve.reciprocal(small[:, 2, :], small[:, 1, :]))
                link(dve.tensor_scalar(small[:, 2, :], small[:, 2, :], tg[:, 2 + l:3 + l], None, ALU.mult))
                for k in range(TOPK):
                    link(dve.tensor_tensor(tmpE, ex, M[:, k, :, :], ALU.mult))
                    link(dve.tensor_reduce(small[:, 3, :], tmpE, AX.X, ALU.add))
                    link(dve.tensor_tensor(wk[:, k, :], small[:, 3, :], small[:, 2, :], ALU.mult))
                dve.wait_ge(sem(f"place_ps{l}"), 1)
                place = bank(6)[:, 0:NT * E].rearrange("p (t e) -> p t e", e=E)
                count = bank(6)[:, NT * E:(NT + 1) * E]
                link(dve.tensor_copy(tbl[:, 0, :], count))
                link(dve.tensor_tensor(n16, tbl[:, 0, :].unsqueeze(2).to_broadcast([P, E, NT]),
                                       cst[:, C_J:C_J + NT].unsqueeze(1).to_broadcast([P, E, NT]), ALU.is_gt))
                link(dve.tensor_reduce(tbl[:, 1, :], n16, AX.X, ALU.add))
                sq = n16[:, :, 0:E]
                for row, c0 in ((2, C_LT), (3, C_LE)):
                    link(dve.tensor_tensor(sq, tbl[:, 1, :].unsqueeze(1).to_broadcast([P, E, E]),
                                           cst[:, c0:c0 + E * E].rearrange("p (e f) -> p e f", e=E), ALU.mult))
                    link(dve.tensor_reduce(tbl[:, row, :], sq, AX.X, ALU.add))
                link(dve.tensor_scalar(tbl[:, 2, :], tbl[:, 2, :], float(P), None, ALU.mult))
                link(dve.tensor_tensor(rank, place, tbl[:, 2, :].unsqueeze(1).to_broadcast([P, NT, E]), ALU.add))
                for k in range(TOPK):
                    link(dve.tensor_tensor(tmpE, rank, M[:, k, :, :], ALU.mult))
                    link(dve.tensor_reduce(slot[:, :, k], tmpE, AX.X, ALU.add))
                link(dve.tensor_copy(sloti[:, 0, :], slot[:, :, :].rearrange("p t k -> p (t k)")))
                dve.tensor_scalar(sloti[:, 1, :], sloti[:, 0, :], P - 1, None, ALU.bitwise_and)
                link(dve.tensor_scalar(sloti[:, 2, :], sloti[:, 0, :], 7, None, ALU.logical_shift_right))
                link(dve.tensor_copy(slotb[:, :, :], sloti[:, 1:3, :]))
                link(dve.tensor_tensor(ohhi, cst[:, C_HI:C_HI + SLOTS].unsqueeze(1).to_broadcast([P, PAIRS, SLOTS]),
                                       slotb[:, 1, :].unsqueeze(2).to_broadcast([P, PAIRS, SLOTS]), ALU.is_equal))
                dve.tensor_scalar(ohpt[:, :, 0:SLOTS], ohhi, cst[:, C_P:C_P + 1], None, ALU.mult)
                dve.tensor_tensor(ohpt[:, :, SLOTS:2 * SLOTS], ohhi,
                                  cst[:, C_TK:C_TK + PAIRS].unsqueeze(2).to_broadcast([P, PAIRS, SLOTS]), ALU.mult)
                dve.tensor_tensor(ohlo, cst[:, C_LO:C_LO + P].unsqueeze(1).to_broadcast([P, PAIRS, P]),
                                  slotb[:, 0, :].unsqueeze(2).to_broadcast([P, PAIRS, P]), ALU.is_equal)\
                   .then_inc(sem(f"onehot{l}"), 1)
                link(dve.tensor_tensor(xof[:, 0:SLOTS, :], cst[0:1, C_HI:C_HI + SLOTS].unsqueeze(2).to_broadcast([1, SLOTS, E]),
                                       tbl[0:1, 3, :].unsqueeze(1).to_broadcast([1, SLOTS, E]), ALU.is_ge))
                link(dve.tensor_reduce(xoff[:, 0:SLOTS], xof[:, 0:SLOTS, :], AX.X, ALU.add))
                dve.tensor_scalar(xofi[:, 0:SLOTS], xoff[:, 0:SLOTS], float(E - 1), None, ALU.min)\
                   .then_inc(sem(f"xof_ready{l}"), 1)
                dve.wait_ge(sem(f"inv_ps{l}"), 1)
                tk = idf[:, 1, :]
                link(dve.tensor_copy(idf[:, 0:2, :], bank(5)[:, 0:2 * SLOTS].rearrange("p (a s) -> p a s", a=2)))
                link(dve.tensor_scalar(idf[:, 2, :], tk, -1.0, float(P), ALU.add, ALU.mult))
                link(dve.tensor_tensor(idf[:, 0, :], idf[:, 0, :], idf[:, 2, :], ALU.add))
                link(dve.tensor_copy(idi[:, :], idf[:, 0, :]))
                dve.tensor_scalar(gidx[:, :], idi[:, :].bitcast(U32), B * Q - 1, None, ALU.bitwise_and)\
                   .then_inc(sem(f"gidx_ready{l}"), 1)
                link(dve.tensor_scalar(idf[:, 2, :], tk, 0.5, float(4 * B * Q), ALU.is_lt, ALU.mult))
                dve.tensor_tensor(sidx[:, :], idf[:, 0, :], idf[:, 2, :], ALU.add).then_inc(sem(f"sidx_ready{l}"), 1)

            def experts(l):
                dve.wait_ge(sem(f"xof_ready{l}"), 1)
                dve.wait_ge(sem(f"ew_in{l}"), 16 * 4)

                def expert_of(s):
                    return dve.value_load(xofi[0:1, bass.ds(s, 1)], min_val=0, max_val=E - 1)

                def x_copy(s, j):
                    dve.wait_ge(sem(f"xT_ps{l}"), s + 1)
                    if not isinstance(s, int) or s >= 2:
                        dve.wait_ge(sem(f"h_ps{l}"), s - 1)
                    dve.tensor_copy(XT[:, j % 2, :], bank(j % 2)[:, 0:P]).then_inc(sem(f"xT_ready{l}"), 1)

                def bias(s, j):
                    e = expert_of(s)
                    dve.wait_ge(sem(f"h_ps{l}"), s + 1)
                    if not isinstance(s, int) or s >= 2:
                        dve.wait_ge(sem(f"gelu{l}"), s - 1)
                    dve.tensor_tensor(hb[:, j % 2, :], bank(2 + j % 2), B1[:, bass.ds(e * F, F)], ALU.add)\
                       .then_inc(sem(f"h_ready{l}"), 1)

                def finish(s, j, round_):
                    e = expert_of(s)
                    dve.wait_ge(sem(f"yt_ps{l}"), s + 1)
                    if not isinstance(s, int) or s >= 4:
                        dve.wait_ge(sem(f"scat{l}{j % 4}"), 16 * round_)
                    dve.tensor_tensor(Yb[:, j % 4, :], bank(6 + j % 2)[:, 0:D], B2[:, bass.ds(e * D, D)], ALU.add)\
                       .then_inc(sem(f"y_ready{l}"), 1)

                x_copy(0, 0)
                x_copy(1, 1)
                bias(0, 0)
                x_copy(2, 2)
                bias(1, 1)
                for s in range(4):
                    x_copy(s + 3, s + 3)
                    bias(s + 2, s + 2)
                    finish(s, s, 0)
                with dve.Fori(1, (SLOTS - 3) // 4) as i:
                    for j in range(4):
                        x_copy(4 * i + j + 3, j + 3)
                        bias(4 * i + j + 2, j + 2)
                        finish(4 * i + j, j, i)
                for s in range(SLOTS - 3, SLOTS):
                    if s + 2 < SLOTS:
                        bias(s + 2, s + 2)
                    finish(s, s, s // 4)

            def combine(l, b):
                dve.wait_ge(sem(f"y_in{l}{b}"), 16 * TOPK)
                for k in range(TOPK):
                    for t in range(TPB * b, TPB * b + TPB):
                        last = dve.scalar_tensor_tensor(out=X[:, t, :], in0=Yin[:, k, t, :], scalar=wk[:, k, t:t + 1],
                                                        in1=X[:, t, :], op0=ALU.mult, op1=ALU.add)
                    if k < TOPK - 1:
                        link(last)
                last.then_inc(sem(f"x_done{l}"), 1)

            attention(0)
            routing(0)
            experts(0)
            for b in range(B):
                combine(0, b)
                if b < 2:
                    dve.wait_ge(sem("x_done0"), b + 1)
                    norm_x(1, b)
            dve.wait_ge(sem("x_done0"), B)
            attention(1)
            routing(1)
            experts(1)
            for b in range(B):
                combine(1, b)


_OUT = ((B * Q, D), "float32")


def kernel(**inputs):
    import concourse.bacc as bacc
    from concourse.bass_utils import run_bass_kernel_spmd as run

    a = {n: np.asarray(v) for n, v in inputs.items()}
    T = np.transpose
    attnw = np.stack([
        np.stack([T(a["L0_xattn_Wq"]), T(a["L0_xattn_Wk"]), T(a["L0_xattn_Wv"]), T(a["L0_xattn_Wo"])], 1),
        np.stack([T(a["L1_xattn_W_q"]), T(a["L1_xattn_W_k"]), T(a["L1_xattn_W_v"]), T(a["L1_xattn_W_o"])], 1)], 1)
    w1 = np.stack([T(a["L0_ffn_w1"], (1, 0, 2)).reshape(D, E * F), T(a["L1_ffn_w1"], (2, 1, 0)).reshape(D, E * F)])
    w2 = np.stack([T(a["L0_ffn_w2"].reshape(E, FC, P, D), (2, 0, 1, 3)).reshape(P, E * FC * D),
                   T(a["L1_ffn_w2"].reshape(D, E, FC, P), (3, 1, 2, 0)).reshape(P, E * FC * D)])
    arrays = {
        "x": a["x"].reshape(B * Q, D),
        "ctxT": T(a["ctx_1024"].reshape(B * KV, D)),
        "attnw": attnw,
        "bo": a["L0_xattn_bo"].reshape(1, D),
        "gates": np.concatenate([a["g_xattn"].reshape(1, 2), a["g_ffn"].reshape(1, 2)], 1),
        "posq": a["itok_BxS_8_8191"].reshape(1, B * Q),
        "posk": a["itok_BxS2_1_8191"].reshape(1, B * KV),
        "mask": a["mask_BxSxS2_if1"].reshape(B * Q, KV),
        "router": np.stack([a["L0_ffn_w_router"], T(a["L1_ffn_gate_w"])], 1),
        "w1": w1,
        "b1": np.stack([a["L0_ffn_b1"].reshape(E * F), a["L1_ffn_b1"].reshape(E * F)]),
        "w2": w2,
        "b2": np.stack([a["L0_ffn_b2"].reshape(E * D), a["L1_ffn_b2"].reshape(E * D)]),
        "consts": constant_table(),
    }
    nc = bacc.Bacc("TRN2", target_bir_lowering=False, num_devices=1)
    feed, args = {}, {}
    for name, v in arrays.items():
        v = np.ascontiguousarray(v)
        feed[f"in_{name}"] = v
        args[name] = nc.dram_tensor(f"in_{name}", v.shape, mybir.dt.from_np(v.dtype), kind="ExternalInput").ap()
    args["out"] = nc.dram_tensor("out_x", _OUT[0], F32, kind="ExternalOutput").ap()
    build(nc, **args)
    r = run(nc, [feed], core_ids=[0])
    return r.results[0]["out_x"].reshape(B, Q, D)
```

```python
from contextlib import ExitStack

import numpy as np

import concourse.bass as bass
from concourse import mybir

F32, F32R, BF16 = mybir.dt.float32, mybir.dt.float32r, mybir.dt.bfloat16
I32, U32 = mybir.dt.int32, mybir.dt.uint32
ALU, ACT, AX = mybir.AluOpType, mybir.ActivationFunctionType, mybir.AxisListType

B, Q, KV, D, H, HD = 4, 512, 77, 128, 16, 8
E, F, TOPK = 8, 512, 2
P = 128
LAYERS = 2
NT = B * Q // P
TPB = Q // P
G = 4
JH = H // G
GK = JH * KV
PW = GK + 1
NC3 = 3
CH = PW // NC3
FC = F // P
BW = FC + D
SLOTS = B * Q * TOPK // P + E - 1
PAIRS = NT * TOPK
RING = 8
HEAD, TAIL = 4, 3
ROUNDS = (SLOTS - HEAD - TAIL) // RING
BIG = 1e30
HUGE = 3e38
LN_EPS = 1e-5

C_ID, C_LO = 0, 128
C_HI = 256
C_TRI = C_HI + SLOTS
C_TK = C_TRI + P
C_P = C_TK + PAIRS
C_HM = C_P + 1
C_NEG = C_HM + JH
C_QA = C_NEG + H
C_SL = C_QA + 3
C_BD = C_SL + 1
C_J = C_BD + LAYERS * NC3 * 32
C_LT = C_J + NT
C_LE = C_LT + E * E
C_END = C_LE + E * E


def constant_table():
    c = np.zeros((P, C_END), np.float32)
    p = np.arange(P)
    c[:, C_ID:C_ID + P] = np.eye(P)
    c[:, C_LO:C_LO + P] = np.arange(P)
    c[:, C_HI:C_HI + SLOTS] = np.arange(SLOTS)
    c[:, C_TRI:C_TRI + P] = p[:, None] < p[None, :]
    for t in range(NT):
        for k in range(TOPK):
            c[:, C_TK + TOPK * t + k] = t + NT * k + 1
    c[:, C_P] = p
    for j in range(JH):
        c[:96, C_HM + j] = (p[:96] % 32) // HD == j
    ratio = 2.0 ** (-8.0 / H)
    slope = np.array([ratio ** i for i in range(1, H + 1)], np.float32)
    high = (((slope.view(np.uint32) + 0x800) >> 12) << 12).astype(np.uint32).view(np.float32)
    for r, part in ((2, high), (3, slope - high), (4, high), (5, slope - high)):
        c[96 + r, C_NEG:C_NEG + H] = -part
    c[98:100, C_QA] = 1.0
    c[100:102, C_QA + 1] = 1.0
    c[96:98, C_QA + 2] = 1.0
    c[:H, C_SL] = slope
    for layer in range(LAYERS):
        for n in range(NC3):
            for i in range(CH):
                r = n * CH + i
                at = C_BD + (layer * NC3 + n) * 32
                if r < GK:
                    c[i, at + HD * (r // KV):at + HD * (r // KV) + HD] = 1.0
                elif layer == 1:
                    c[i, at:at + 32] = 1.0
    c[:, C_J:C_J + NT] = P * np.arange(NT)
    e = np.arange(E)
    c[:, C_LT:C_LT + E * E] = (e[None, :] < e[:, None]).reshape(1, -1)
    c[:, C_LE:C_LE + E * E] = (e[None, :] <= e[:, None]).reshape(1, -1)
    return c


def build(nc, x, ctxT, attnw, bo, gates, posq, posk, mask, router, w1, w2, b1, b2, consts, out):
    ctx = ExitStack()
    with ctx:
        def sb(name, shape, dt=F32):
            return ctx.enter_context(nc.sbuf_tensor(name, shape, dt))

        made = {}

        def sem(name):
            if name not in made:
                made[name] = ctx.enter_context(nc.semaphore(name))
            return made[name]

        cst = sb("cst", [P, C_END])
        aw = sb("aw", [P, LAYERS, 4, D])
        rw = sb("rw", [P, LAYERS, E])
        X = sb("X", [P, NT, D])
        XM = sb("XM", [P, NT, D])
        xnT = sb("xnT", [P, 2, Q])
        qhi = sb("qhi", [P, Q], F32R)
        qlo = sb("qlo", [P, Q], F32R)
        qaug = sb("qaug", [P, 2, G, Q], F32R)
        kaug = sb("kaug", [P, LAYERS, G * B, JH, KV], F32R)
        vbd = sb("vbd", [CH, LAYERS, NC3, B * G, 32])
        rden = sb("rden", [P, 256])
        pos = sb("pos", [P, B * Q], F32R)
        maskb = sb("maskb", [P, NT, KV], BF16)
        nanrow = sb("nanrow", [P, NT])
        W1 = sb("W1", [P, E * F])
        W2 = sb("W2", [P, E * FC * D])
        BB = sb("BB", [P, E * BW])
        scratch = sb("scratch", [P, 4004])
        tgbo = sb("tgbo", [P, D])
        gt = sb("gt", [P, 4])
        tg = sb("tg", [P, 4])
        identb = sb("identb", [P, P], BF16)
        trib = sb("trib", [P, P], BF16)
        onesb = sb("onesb", [P, P], BF16)
        stat = sb("stat", [P, TPB, 6])
        mv = sb("mv", [P, TPB, 2])
        rstd = sb("rstd", [P, 3, TPB])
        mx = sb("mx", [P, 2, 8])
        arenaA = sb("arenaA", [P, 6144])
        arenaB = sb("arenaB", [P, 4216])
        PT = arenaA[0:CH, :].rearrange("p (u m q) -> p u m q", u=2, m=G * NC3)
        Dm = arenaB[:, 0:2 * 2 * GK].rearrange("p (n g k) -> p n g k", n=2, g=2)
        Pr = arenaB[:, 4 * GK:4 * GK + 2 * G * PW].rearrange("p (u g k) -> p u g k", u=2, g=G)
        OT = arenaB[:, 3704:4216].rearrange("p (u q) -> p u q", u=2)
        GX = arenaA[:, 0:RING * D].rearrange("p (n d) -> p n d", n=RING)
        W1s = arenaA[:, RING * D:RING * D + 4 * F].rearrange("p (n f) -> p n f", n=4)
        XT = arenaB[:, 0:256].rearrange("p (n d) -> p n d", n=2)
        hb = arenaB[:, 256:1280].rearrange("p (n f) -> p n f", n=2)
        ge = arenaB[:, 1280:3328].rearrange("p (n f) -> p n f", n=4)
        Yb = arenaB[:, 3328:3840].rearrange("p (n d) -> p n d", n=4)
        cmp1 = arenaA[:, 0:1024].rearrange("p (t e f) -> p t e f", t=NT, e=E)
        cmp2 = arenaA[:, 1024:2048].rearrange("p (t e f) -> p t e f", t=NT, e=E)
        ohlo = arenaA[:, 2048:4096].bitcast(BF16).rearrange("p (n c) -> p n c", n=PAIRS)
        ohhi = arenaA[:, 4096:4096 + PAIRS * SLOTS // 2].bitcast(BF16).rearrange("p (n c) -> p n c", n=PAIRS)
        ohpt = arenaA[:, 4736:4736 + PAIRS * SLOTS].bitcast(BF16).rearrange("p (n c) -> p n c", n=PAIRS)
        Yin = arenaA[:, 0:4096].rearrange("p (k t d) -> p k t d", k=TOPK, t=NT)
        posi = W1[96:128, 0:2048].bitcast(I32)
        posf = W1[96:128, 2048:4096]
        posh = W2[96:128, 0:2048].bitcast(F32R)
        KR = [W2[0:96, 1232 * l:1232 * l + 1232].bitcast(F32R) for l in range(LAYERS)]
        Vs = [W2[0:KV, 2464 + 512 * l:2464 + 512 * l + 512] for l in range(LAYERS)]
        Khl = arenaA[:, 4912:6144]
        Kh = [Khl[:, 616 * l:616 * l + 308].bitcast(F32R) for l in range(LAYERS)]
        Kl = [Khl[:, 616 * l + 308:616 * l + 616].bitcast(F32R) for l in range(LAYERS)]
        mski = scratch[:, 0:NT * KV].bitcast(I32)
        ctxs = scratch[:, 1232:1232 + B * KV]
        kpi = scratch[0:H, 1540:1540 + B * KV].bitcast(I32)
        kpf = scratch[0:H, 1848:1848 + B * KV]
        kph = scratch[0:H, 2156:2156 + B * KV].bitcast(F32R)
        kpl = scratch[0:H, 2464:2464 + B * KV].bitcast(F32R)
        mcnt = scratch[:, 2772:2772 + NT * KV]
        qh32, ql32 = qhi[:, :].bitcast(F32), qlo[:, :].bitcast(F32)
        L, rank, ex, tmpE = (qh32[:, 128 * i:128 * i + 128].rearrange("p (t e) -> p t e", e=E) for i in range(4))
        M = ql32[:, 0:256].rearrange("p (k t e) -> p k t e", k=TOPK, e=E)
        n16 = ql32[:, 256:384].rearrange("p (e t) -> p e t", e=E)
        slot = ql32[:, 384:416].rearrange("p (t k) -> p t k", k=TOPK)
        slotb = ql32[:, 416:480].rearrange("p (a n) -> p a n", a=2)
        xof = arenaB[0:1, 0:SLOTS * E].rearrange("p (s e) -> p s e", e=E)
        Ab = sb("Ab", [P, NT, E], BF16)
        wk = sb("wk", [P, TOPK, NT])
        small = sb("small", [P, 4, NT])
        tbl = sb("tbl", [P, 4, E])
        sloti = sb("sloti", [P, 3, PAIRS], I32)
        xoff = sb("xoff", [1, SLOTS + 1])
        xofi = sb("xofi", [1, 2, SLOTS + 1], I32)
        idf = sb("idf", [P, 3, SLOTS])
        gidx = sb("gidx", [P, SLOTS], U32)
        sidx = sb("sidx", [P, SLOTS], U32)
        idi = sb("idi", [P, SLOTS], I32)

        PS = ctx.enter_context(nc.psum_tensor("PS", [P, 8 * 512], F32))

        def bank(n):
            return PS[:, 512 * n:512 * n + 512]

        xnd = [nc.dram_tensor(f"xnd{l}", (B * Q, D), F32, kind="Internal").ap() for l in range(LAYERS)]
        yd = [nc.dram_tensor(f"yd{l}", (TOPK * B * Q, D), F32, kind="Internal").ap() for l in range(LAYERS)]

        def gathers_of(j):
            return (SLOTS - j + RING - 1) // RING

        def scatters_of(j):
            return (SLOTS - j + 3) // 4

        ident = cst[:, C_ID:C_ID + P]
        x_v = x.rearrange("(t p) d -> p t d", p=P)
        out_v = out.rearrange("(t p) d -> p t d", p=P)

        block = ctx.enter_context(nc.Block())

        @block.sync
        def _(sp):
            sp.dma_start(scratch[:, 1232:1232 + B * KV], ctxT).then_inc(sem("ctx_in"), 16)
            sp.dma_start(aw[:, 0], attnw[:, 0]).then_inc(sem("aw_in0"), 16)
            for b in range(B):
                sp.dma_start(X[:, TPB * b:TPB * b + TPB, :], x_v[:, TPB * b:TPB * b + TPB, :])\
                  .then_inc(sem(f"x_in{b}"), 16)
            sp.dma_start(aw[:, 1], attnw[:, 1]).then_inc(sem("aw_in1"), 16)
            sp.dma_start(mski, mask.rearrange("(t p) k -> p t k", p=P)).then_inc(sem("mask_in"), 16)
            sp.dma_start(rw[:, :, :], router).then_inc(sem("rw_in"), 16)

            def spread_k(l):
                sp.wait_ge(sem("kl_ready"), l + 1)
                for g in range(G):
                    for part, src in enumerate((Kh[l], Kl[l], Kh[l])):
                        sp.dma_start(KR[l][32 * part:32 * part + 32, 308 * g:308 * g + 308].bitcast(F32),
                                     src[32 * g:32 * g + 32, :].bitcast(F32)).then_inc(sem(f"kr_in{l}"), 16)

            def spread_v(l):
                sp.wait_ge(sem("v_ready"), l + 1)
                sp.wait_ge(sem("vbd_zero"), 1)
                for j in range(JH):
                    k = 0
                    while k < KV:
                        n, r = divmod(KV * j + k, CH)
                        m = min(CH - r, KV - k)
                        src = Vs[l][k:k + m, :].rearrange("k (b g j d) -> k (b g) j d", b=B, g=G, j=JH)
                        sp.dma_start(vbd[r:r + m, l, n, :, HD * j:HD * j + HD], src[:, :, j, :])\
                          .then_inc(sem(f"vbd_in{l}"), 16)
                        k += m

            def spread_q(l, b):
                u = b % 2
                sp.wait_ge(sem(f"qlo_ready{l}"), b + 1)
                if l:
                    sp.wait_ge(sem("pos_ready"), 1)
                    if b < 2:
                        sp.wait_ge(sem("s_ps0"), 2 * NT)
                if b >= 2:
                    sp.wait_ge(sem(f"s_ps{l}"), 2 * TPB * (b - 1))
                for g in range(G):
                    for part, src in enumerate((qhi, qhi, qlo)):
                        sp.dma_start(qaug[32 * part:32 * part + 32, u, g, :].bitcast(F32),
                                     src[32 * g:32 * g + 32, :].bitcast(F32)).then_inc(sem(f"qa_in{l}{b}"), 16)
                    if l:
                        sp.dma_start(qaug[96:128, u, g, :].bitcast(F32), pos[96:128, Q * b:Q * b + Q].bitcast(F32))\
                          .then_inc(sem(f"qa_in{l}{b}"), 16)

            spread_k(0)
            spread_q(0, 0)
            spread_v(0)
            spread_k(1)
            spread_v(1)
            sp.wait_ge(sem("kbias_ready"), 1)
            sp.wait_ge(sem("kconst_ready"), G)
            for h in range(H):
                g, j = divmod(h, JH)
                for r, src in enumerate((kph, kpl)):
                    dst = kaug[96 + r:97 + r, 1, B * g:B * g + B, j, :].bitcast(F32)
                    sp.dma_start(dst, src[h:h + 1, :].bitcast(F32).rearrange("p (b k) -> p b k", b=B))\
                      .then_inc(sem("kbias_in"), 16)

            def expert_weights(l):
                sp.dma_start(W1[:, :], w1[l]).then_inc(sem(f"ew_in{l}"), 16)
                sp.dma_start(W2[:, :], w2[l]).then_inc(sem(f"ew_in{l}"), 16)
                biases = BB[:, :].rearrange("p (e c) -> p e c", c=BW)
                sp.dma_start(biases[:, :, 0:FC], b1[l]).then_inc(sem(f"ew_in{l}"), 16)
                sp.dma_start(biases[:, :, FC:BW], b2[l:l + 1].to_broadcast([P, E, D])).then_inc(sem(f"ew_in{l}"), 16)

            for l in range(LAYERS):
                for b in range(1, B):
                    if l == 0 and b == 2:
                        sp.wait_ge(sem("pos_ready"), 1)
                        sp.wait_ge(sem("kaug_ready"), 1)
                        sp.wait_ge(sem("kaug_ready1"), JH)
                        sp.wait_ge(sem("vbd_in0"), 16 * 6)
                        sp.wait_ge(sem("vbd_in1"), 16 * 6)
                        sp.wait_ge(sem("kbias_in"), 16 * 2 * H)
                        sp.wait_ge(sem("mask_ready"), 1)
                        expert_weights(0)
                    spread_q(l, b)
                for b in range(B):
                    sp.wait_ge(sem(f"xm_ready{l}"), b + 1)
                    sp.dma_start(xnd[l].rearrange("(t p) d -> p t d", p=P)[:, TPB * b:TPB * b + TPB, :],
                                 XM[:, TPB * b:TPB * b + TPB, :]).then_inc(sem(f"xnd_in{l}"), 16)
                for j in range(4):
                    sp.wait_ge(sem(f"scat{j}"), 16 * (l + 1) * scatters_of(j))
                yv = yd[l].rearrange("(k t p) d -> p k t d", k=TOPK, p=P)
                for b in range(B):
                    for k in range(TOPK):
                        sp.dma_start(Yin[:, k, TPB * b:TPB * b + TPB, :], yv[:, k, TPB * b:TPB * b + TPB, :])\
                          .then_inc(sem(f"y_in{l}{b}"), 16)
                if l == 0:
                    expert_weights(1)
                    spread_q(1, 0)
            for b in range(B):
                sp.wait_ge(sem("x_done1"), b + 1)
                sp.dma_start(out_v[:, TPB * b:TPB * b + TPB, :], X[:, TPB * b:TPB * b + TPB, :])\
                  .then_inc(sem("out_done"), 16)
            sp.wait_ge(sem("out_done"), 16 * B)

        @block.gpsimd
        def _(pool):
            chain = [0]

            def link(ins):
                chain[0] += 1
                ins.then_inc(sem("pool_chain"), 1)
                pool.wait_ge(sem("pool_chain"), chain[0])

            def apart(name, count):
                pool.wait_ge(sem(name), count)

            pool.memset(vbd[:, :, :, :, :], 0.0).then_inc(sem("vbd_zero"), 1)
            pool.memset(onesb[:, :], 1.0).then_inc(sem("ones_ready"), 1)
            pool.memset(Pr[:, :, :, GK:PW], 1.0).then_inc(sem("pad_ready0"), 1)
            pool.wait_ge(sem("cst_in"), 16)
            pool.tensor_copy(identb[:, :], ident).then_inc(sem("identb_ready"), 1)
            pool.tensor_copy(trib[:, :], cst[:, C_TRI:C_TRI + P]).then_inc(sem("trib_ready"), 1)

            def biased(b):
                pool.wait_ge(sem("xn_ready0"), b + 1)
                pool.tensor_tensor(X[:, TPB * b:TPB * b + TPB, :], X[:, TPB * b:TPB * b + TPB, :],
                                   tgbo[:, :].unsqueeze(1).to_broadcast([P, TPB, D]), ALU.add)\
                    .then_inc(sem("xb_ready0"), 1)
                apart("xb_ready0", b + 1)

            pool.wait_ge(sem("tg_ready"), 1)
            pool.wait_ge(sem("bo_in"), 16)
            link(pool.tensor_scalar(tgbo[:, :], tgbo[:, :], tg[:, 0:1], None, ALU.mult))
            biased(0)
            biased(1)
            neg = cst[96:128, C_NEG:C_NEG + H].rearrange("p (g j) -> p g j", g=G)
            kc = kaug[96:128, 1, :, :, :].rearrange("p (g b) j k -> p g b j k", g=G)
            for g in range(G):
                pool.tensor_copy(kc[:, g], neg[:, g, :].unsqueeze(1).unsqueeze(3).to_broadcast([32, B, JH, KV]))\
                    .then_inc(sem("kconst_ready"), 1)
                apart("kconst_ready", g + 1)
            pool.wait_ge(sem("kpos_in"), 16)
            link(pool.tensor_copy(kpf, kpi))
            link(pool.tensor_scalar(kpf, kpf, cst[0:H, C_SL:C_SL + 1], None, ALU.mult))
            link(pool.tensor_copy(kph, kpf))
            pool.tensor_tensor(kpl, kpf, kph.bitcast(F32), ALU.subtract).then_inc(sem("kbias_ready"), 1)
            apart("kbias_ready", 1)
            pool.wait_ge(sem("kr_in1"), 16 * 3 * G)
            for j in range(JH):
                pool.tensor_scalar(kaug[0:96, 1, :, j, :],
                                          KR[1].bitcast(F32).rearrange("p (n k) -> p n k", k=KV),
                                   cst[0:96, C_HM + j:C_HM + j + 1], None, ALU.mult)\
                    .then_inc(sem("kaug_ready1"), 1)
                apart("kaug_ready1", j + 1)
            pool.wait_ge(sem("qpos_in"), 16)
            link(pool.tensor_copy(posf, posi))
            link(pool.tensor_copy(posh, posf))
            link(pool.tensor_tensor(posf, posf, posh.bitcast(F32), ALU.subtract))
            link(pool.tensor_scalar(posf, posf, cst[96:128, C_QA + 1:C_QA + 2],
                                    cst[96:128, C_QA + 2:C_QA + 3], ALU.mult, ALU.add))
            link(pool.tensor_scalar(posh, posh.bitcast(F32), cst[96:128, C_QA:C_QA + 1], None, ALU.mult))
            pool.tensor_tensor(pos[96:128, :], posh.bitcast(F32), posf, ALU.add).then_inc(sem("pos_ready"), 1)
            apart("pos_ready", 1)
            pool.wait_ge(sem("mask_in"), 16)
            link(pool.tensor_scalar(mcnt, mski, 0.0, None, ALU.is_equal))
            pool.tensor_scalar(maskb[:, :, :], mcnt.rearrange("p (t k) -> p t k", t=NT), -BIG, None, ALU.mult)\
                .then_inc(sem("maskb_ready"), 1)
            apart("maskb_ready", 1)
            biased(2)
            biased(3)

            for l in range(LAYERS):
                if l:
                    pool.wait_ge(sem("y_ready0"), SLOTS)
                    for j in range(4):
                        pool.wait_ge(sem(f"scat{j}"), 16 * scatters_of(j))
                    pool.memset(Pr[:, :, :, GK:PW], 1.0).then_inc(sem("pad_ready1"), 1)
                    apart("pad_ready1", 1)
                    for b in range(B):
                        pool.wait_ge(sem("xn_ready1"), b + 1)
                        pool.wait_ge(sem("mask_ready"), 1)
                        pool.tensor_tensor(X[:, TPB * b:TPB * b + TPB, :], X[:, TPB * b:TPB * b + TPB, :],
                                           nanrow[:, TPB * b:TPB * b + TPB].unsqueeze(2).to_broadcast([P, TPB, D]),
                                           ALU.add).then_inc(sem("xb_ready1"), 1)
                        apart("xb_ready1", b + 1)

                def gather(s):
                    pool.indirect_dma_start(GX[:, s % RING, :], None, xnd[l],
                                            bass.IndirectOffsetOnAxis(ap=gidx[:, s:s + 1], axis=0))\
                        .then_inc(sem(f"gath{s % RING}"), 16)

                pool.wait_ge(sem(f"gidx_ready{l}"), 1)
                pool.wait_ge(sem(f"xnd_in{l}"), 16 * B)
                pool.wait_ge(sem(f"resid{l}"), B * 2)
                for s in range(RING):
                    gather(s)
                for s in range(SLOTS):
                    if s + RING < SLOTS:
                        pool.wait_ge(sem(f"xT_ps{l}"), s + 1)
                        gather(s + RING)
                    pool.wait_ge(sem(f"y_ready{l}"), s + 1)
                    pool.indirect_dma_start(yd[l], bass.IndirectOffsetOnAxis(ap=sidx[:, s:s + 1], axis=0),
                                            Yb[:, s % 4, :], None, bounds_check=TOPK * B * Q - 1,
                                            oob_is_err=False).then_inc(sem(f"scat{s % 4}"), 16)

        @block.scalar
        def _(act):
            act.dma_start(cst[:, :], consts).then_inc(sem("cst_in"), 16)
            act.dma_start(gt[:, :], gates.to_broadcast([P, 4])).then_inc(sem("gt_in"), 16)
            act.dma_start(tgbo[:, :], bo.to_broadcast([P, D])).then_inc(sem("bo_in"), 16)
            act.dma_start(kpi, posk.to_broadcast([H, B * KV])).then_inc(sem("kpos_in"), 16)
            act.dma_start(posi, posq.to_broadcast([32, B * Q])).then_inc(sem("qpos_in"), 16)
            act.wait_ge(sem("gt_in"), 16)
            act.activation(tg[:, :], gt[:, :], ACT.Tanh).then_inc(sem("tg_ready"), 1)

            def k_high(l):
                act.wait_ge(sem("k_ps"), l + 1)
                act.activation(Kh[l], bank(l)[:, 0:B * KV], ACT.Copy, scale=HD ** -0.5).then_inc(sem("kh_ready"), 1)

            def v_copy(l):
                act.wait_ge(sem("v_ps"), l + 1)
                act.activation(Vs[l], bank(2 + l)[0:KV, :], ACT.Copy).then_inc(sem("v_ready"), 1)

            def xnT_copy(l, b):
                act.wait_ge(sem(f"xt_ps{l}"), b + 1)
                act.activation(xnT[:, b % 2, :], bank(7), ACT.Copy).then_inc(sem(f"xt_ready{l}"), 1)

            def q_high(l, b):
                act.wait_ge(sem(f"q_ps{l}"), b + 1)
                if b:
                    act.wait_ge(sem(f"qa_in{l}{b - 1}"), 16 * G * (4 if l else 3))
                act.activation(qhi[:, :], bank(7), ACT.Copy).then_inc(sem(f"qhi_ready{l}"), 1)

            def attention(l):
                if l == 0:
                    k_high(0)
                xnT_copy(l, 0)
                q_high(l, 0)
                if l == 0:
                    v_copy(0)
                    k_high(1)
                    v_copy(1)
                for t in range(NT):
                    b = t // TPB
                    for hf in range(2):
                        n = 2 * t + hf
                        act.wait_ge(sem(f"sub{l}"), n + 1)
                        if t >= 2:
                            act.wait_ge(sem(f"pt_ps{l}"), G * (t - 1))
                        act.activation(Pr[:, t % 2, 2 * hf:2 * hf + 2, 0:GK], Dm[:, hf, :, :], ACT.Exp)\
                           .then_inc(sem(f"exp{l}"), 1)
                    if t % TPB == 1 and b + 1 < B:
                        q_high(l, b + 1)
                    v = t // 2
                    if t % 2 == 0 and v >= 2:
                        act.wait_ge(sem(f"o_ps{l}"), v - 1)
                    if l == 0 and t == 2:
                        act.wait_ge(sem("kr_in1"), 16 * 3 * G)
                    for g in range(G):
                        m = G * t + g
                        act.wait_ge(sem(f"pt_ps{l}"), m + 1)
                        dst = PT[:, v % 2, NC3 * g:NC3 * g + NC3, P * (t % 2):P * (t % 2) + P]
                        act.activation(dst, bank(4 + m % 2)[0:CH, 0:NC3 * P].rearrange("p (c q) -> p c q", c=NC3),
                                       ACT.Copy).then_inc(sem(f"pt_ready{l}"), 1)
                    if t % TPB == 0 and b + 1 < B:
                        xnT_copy(l, b + 1)

            def routing(l):
                for b in range(B):
                    act.wait_ge(sem(f"xmt_ps{l}"), b + 1)
                    if b >= 2:
                        act.wait_ge(sem(f"lg_ps{l}"), b - 1)
                    act.activation(xnT[:, b % 2, :], bank(b), ACT.Copy).then_inc(sem(f"xmt_ready{l}"), 1)
                act.wait_ge(sem(f"lsub{l}"), 1)
                act.activation(ex, tmpE, ACT.Exp).then_inc(sem(f"lexp{l}"), 1)

            def experts(l):
                def gelu(s, c):
                    act.wait_ge(sem(f"h_ready{l}"), s + 1)
                    if c >= 4:
                        act.wait_ge(sem(f"yt_ps{l}"), s - 3)
                    act.activation(ge[:, c % 4, :], hb[:, c % 2, :], ACT.Gelu_apprx_tanh)\
                       .then_inc(sem(f"gelu{l}"), 1)

                def w1_copy(s, c):
                    e = act.value_load(xofi[0:1, 0, bass.ds(s, 1)], min_val=0, max_val=(E - 1) * F)
                    if c >= 4:
                        act.wait_ge(sem(f"h_ps{l}"), s - 3)
                    act.activation(W1s[:, c % 4, :], W1[:, bass.ds(e, F)], ACT.Copy)\
                       .then_inc(sem(f"w1_ready{l}"), 1)

                act.wait_ge(sem(f"xof_ready{l}"), 1)
                act.wait_ge(sem(f"ew_in{l}"), 16 * 4)
                act.wait_ge(sem(f"inv_ps{l}"), 1)
                for s in range(3):
                    w1_copy(s, s)
                for s in range(HEAD):
                    gelu(s, s)
                    w1_copy(s + 3, s + 3)
                with act.Fori(0, ROUNDS) as i:
                    for c in range(HEAD, HEAD + RING):
                        gelu(RING * i + c, c)
                        w1_copy(RING * i + c + 3, c + 3)
                for s in range(SLOTS - TAIL, SLOTS):
                    gelu(s, s)

            for l in range(LAYERS):
                attention(l)
                routing(l)
                experts(l)

        @block.tensor
        def _(pe):
            pe.wait_ge(sem("cst_in"), 16)
            pe.wait_ge(sem("ctx_in"), 16)

            def k_and_v(l):
                pe.wait_ge(sem(f"aw_in{l}"), 16)
                pe.matmul(bank(l)[:, 0:B * KV], aw[:, l, 1, :], ctxs, start=True, stop=True)\
                  .then_inc(sem("k_ps"), 1)
                for b in range(B):
                    last = pe.matmul(bank(2 + l)[0:KV, P * b:P * b + P], ctxs[:, KV * b:KV * b + KV],
                                     aw[:, l, 2, :], start=True, stop=True)
                last.then_inc(sem("v_ps"), 1)

            sent = [0, 0]

            def xn_turn(l, b):
                pe.wait_ge(sem(f"xn_ready{l}"), b + 1)
                if sent[l]:
                    pe.wait_ge(sem(f"resid{l}"), sent[l])
                for i in range(TPB):
                    last = pe.transpose(bank(7)[:, P * i:P * i + P], XM[:, TPB * b + i, :], ident)
                last.then_inc(sem(f"xt_ps{l}"), 1)

            def q_product(l, b):
                pe.wait_ge(sem(f"xt_ready{l}"), b + 1)
                pe.matmul(bank(7), aw[:, l, 0, :], xnT[:, b % 2, :], start=True, stop=True)\
                  .then_inc(sem(f"q_ps{l}"), 1)

            def scores(l, t):
                b = t // TPB
                if t == 0:
                    pe.wait_ge(sem("kaug_ready" if l == 0 else "kaug_ready1"), 1 if l == 0 else JH)
                    if l:
                        pe.wait_ge(sem("kbias_in"), 16 * 2 * H)
                        pe.wait_ge(sem("maskb_ready"), 1)
                        pe.wait_ge(sem("identb_ready"), 1)
                if t % TPB == 0:
                    pe.wait_ge(sem(f"qa_in{l}{b}"), 16 * G * (4 if l else 3))
                K = P if l else 96
                for hf in range(2):
                    n = 2 * t + hf
                    if n >= 2:
                        pe.wait_ge(sem(f"sub{l}"), n - 1)
                    for g in (2 * hf, 2 * hf + 1):
                        at = P * (t % TPB)
                        rhs = kaug[0:K, l, B * g + b, :, :].rearrange("p j k -> p (j k)")
                        last = pe.matmul(bank(g)[:, 0:GK], qaug[0:K, b % 2, g, at:at + P], rhs,
                                         start=True, stop=(l == 0))
                        if l:
                            last = pe.matmul(bank(g)[:, 0:GK].rearrange("p (j k) -> p j k", j=JH), identb[:, :],
                                             maskb[:, t, :].unsqueeze(1).to_broadcast([P, JH, KV]),
                                             start=False, stop=True)
                    last.then_inc(sem(f"s_ps{l}"), 1)

            def turn(l, t):
                for g in range(G):
                    m = G * t + g
                    if g % 2 == 0:
                        pe.wait_ge(sem(f"exp{l}"), 2 * t + g // 2 + 1)
                    if t == 0 and g == 0:
                        pe.wait_ge(sem(f"pad_ready{l}"), 1)
                    if m >= 2:
                        pe.wait_ge(sem(f"pt_ready{l}"), m - 1)
                    for c in range(NC3):
                        last = pe.transpose(bank(4 + m % 2)[0:CH, P * c:P * c + P],
                                            Pr[:, t % 2, g, CH * c:CH * c + CH], ident)
                    last.then_inc(sem(f"pt_ps{l}"), 1)

            def values(l, v):
                b = v // 2
                pe.wait_ge(sem(f"pt_ready{l}"), 2 * G * (v + 1))
                if v == 0:
                    pe.wait_ge(sem(f"vbd_in{l}"), 16 * 6)
                else:
                    pe.wait_ge(sem(f"ot_ready{l}"), v)
                for den in range(2):
                    for c in range(NC3):
                        for g in range(G):
                            at = C_BD + (l * NC3 + c) * 32
                            lhs = cst[0:CH, at:at + 32] if den else vbd[:, l, c, G * b + g, :]
                            last = pe.matmul(bank(6)[32 * g:32 * g + 32, 256 * den:256 * den + 256], lhs,
                                             PT[:, v % 2, NC3 * g + c, :], start=(c == 0), stop=(c == NC3 - 1))
                last.then_inc(sem(f"o_ps{l}"), 1)

            def out_product(l, v):
                pe.wait_ge(sem(f"ot_ready{l}"), v + 1)
                if v:
                    pe.wait_ge(sem(f"resid{l}"), v)
                pe.wait_ge(sem(f"qlo_ready{l}"), min(1 + (v + 3) // 2, B))
                for i in range(2):
                    last = pe.matmul(bank(7)[:, P * i:P * i + P], OT[:, v % 2, P * i:P * i + P],
                                     aw[:, l, 3, :], start=True, stop=True)
                last.then_inc(sem(f"y_ps{l}"), 1)
                sent[l] += 1

            def attention(l):
                if l == 0:
                    k_and_v(0)
                xn_turn(l, 0)
                q_product(l, 0)
                if l == 0:
                    k_and_v(1)
                    pe.wait_ge(sem("kl_ready"), 2)
                    pe.wait_ge(sem("v_ready"), 2)
                scores(l, 0)
                for t in range(NT):
                    b = t // TPB
                    if t + 1 < NT:
                        scores(l, t + 1)
                    if t % TPB == 1 and b + 1 < B:
                        q_product(l, b + 1)
                    turn(l, t)
                    if t % TPB == 0 and b + 1 < B:
                        xn_turn(l, b + 1)
                    if t % 2:
                        if t > 1:
                            out_product(l, t // 2 - 1)
                        values(l, t // 2)
                out_product(l, NT // 2 - 1)

            def routing(l):
                for b in range(B):
                    pe.wait_ge(sem(f"xm_ready{l}"), b + 1)
                    for i in range(TPB):
                        last = pe.transpose(bank(b)[:, P * i:P * i + P], XM[:, TPB * b + i, :], ident)
                    last.then_inc(sem(f"xmt_ps{l}"), 1)
                if l == 0:
                    pe.wait_ge(sem("rw_in"), 16)
                pe.wait_ge(sem(f"resid{l}"), 2 * B)
                for b in range(B):
                    pe.wait_ge(sem(f"xmt_ready{l}"), b + 1)
                    for i in range(TPB):
                        t = TPB * b + i
                        last = pe.matmul(bank(7)[:, E * t:E * t + E], xnT[:, b % 2, P * i:P * i + P],
                                         rw[:, l, :], start=True, stop=True)
                    last.then_inc(sem(f"lg_ps{l}"), 1)
                pe.wait_ge(sem(f"chosen{l}"), 1)
                if l == 0:
                    pe.wait_ge(sem("trib_ready"), 1)
                    pe.wait_ge(sem("ones_ready"), 1)
                place = bank(6)[:, 0:(NT + 1) * E]
                pe.matmul(place[:, 0:NT * E], trib[:, :], Ab[:, :, :].rearrange("p t e -> p (t e)"),
                          start=True, stop=False, skip_group_check=True)
                for t in range(NT):
                    n = NT - t
                    last = pe.matmul(place[:, E * (t + 1):].rearrange("p (t e) -> p t e", e=E), onesb[:, :],
                                     Ab[:, t, :].unsqueeze(1).to_broadcast([P, n, E]),
                                     start=False, stop=(t == NT - 1), skip_group_check=True)
                last.then_inc(sem(f"place_ps{l}"), 1)
                pe.wait_ge(sem(f"onehot{l}"), 1)
                for n in range(PAIRS):
                    last = pe.matmul(bank(5)[:, 0:2 * SLOTS], ohlo[:, n, :], ohpt[:, n, :],
                                     start=(n == 0), stop=(n == PAIRS - 1))
                last.then_inc(sem(f"inv_ps{l}"), 1)

            def experts(l):
                pe.wait_ge(sem(f"xof_ready{l}"), 1)
                pe.wait_ge(sem(f"ew_in{l}"), 16 * 4)

                at = {}

                def load_expert(s, c):
                    at[c] = pe.value_load(xofi[0:1, 0, bass.ds(s, 1)], min_val=0, max_val=(E - 1) * F)

                def x_turn(s, c, i):
                    pe.wait_ge(sem(f"gath{c % RING}"), 16 * (l * gathers_of(c % RING) + i + c // RING + 1))
                    if c >= 2:
                        pe.wait_ge(sem(f"xT_ready{l}"), s - 1)
                    pe.transpose(bank(c % 2)[:, 0:P], GX[:, c % RING, :], ident).then_inc(sem(f"xT_ps{l}"), 1)

                def up(s, c):
                    pe.wait_ge(sem(f"xT_ready{l}"), s + 1)
                    if c >= 2:
                        pe.wait_ge(sem(f"h_ready{l}"), s - 1)
                    pe.wait_ge(sem(f"w1_ready{l}"), s + 1)
                    for n in range(FC):
                        last = pe.matmul(bank(2 + c % 2)[:, P * n:P * n + P], W1s[:, c % 4, P * n:P * n + P],
                                         XT[:, c % 2, :], start=True, stop=True)
                    last.then_inc(sem(f"h_ps{l}"), 1)

                def down(s, c):
                    pe.wait_ge(sem(f"gelu{l}"), s + 1)
                    if c >= 2:
                        pe.wait_ge(sem(f"y_ready{l}"), s - 1)
                    for n in range(FC):
                        last = pe.matmul(bank(6 + c % 2)[:, 0:D], ge[:, c % 4, P * n:P * n + P],
                                         W2[:, bass.ds(at[c] + n * D, D)], start=(n == 0), stop=(n == FC - 1))
                    last.then_inc(sem(f"yt_ps{l}"), 1)

                def steps(i, first, n):
                    for c in range(first, first + n):
                        s = RING * i + c
                        x_turn(s + 3, c + 3, i)
                        up(s + 2, c + 2)
                        load_expert(s, c)
                        down(s, c)

                for s in range(3):
                    x_turn(s, s, 0)
                for s in range(2):
                    up(s, s)
                steps(0, 0, HEAD)
                with pe.Fori(0, ROUNDS) as i:
                    steps(i, HEAD, RING)
                for s in range(SLOTS - TAIL, SLOTS):
                    load_expert(s, s)
                    if s + 2 < SLOTS:
                        up(s + 2, s + 2)
                    down(s, s)

            for l in range(LAYERS):
                attention(l)
                routing(l)
                experts(l)

        @block.vector
        def _(dve):
            chain = [0]

            def link(ins):
                chain[0] += 1
                ins.then_inc(sem("dve_chain"), 1)
                dve.wait_ge(sem("dve_chain"), chain[0])

            def normalise(src, dst):
                for i in range(TPB):
                    last = dve.bn_stats(stat[:, i, :], src[:, i, :])
                link(last)
                for i in range(TPB):
                    last = dve.bn_aggr(mv[:, i, :], stat[:, i, :])
                link(last)
                y, yi, var, t = rstd[:, 0, :], rstd[:, 0, :].bitcast(I32), rstd[:, 1, :], rstd[:, 2, :]
                link(dve.tensor_scalar(var, mv[:, :, 1], LN_EPS, None, ALU.add))
                link(dve.tensor_scalar(yi, var.bitcast(I32), 1, None, ALU.logical_shift_right))
                link(dve.tensor_scalar(yi, yi, -1.0, float(0x5F3759DF), ALU.mult, ALU.add))
                for _ in range(3):
                    link(dve.tensor_tensor(t, y, y, ALU.mult))
                    link(dve.tensor_tensor(t, t, var, ALU.mult))
                    link(dve.tensor_scalar(t, t, -0.5, 1.5, ALU.mult, ALU.add))
                    link(dve.tensor_tensor(y, y, t, ALU.mult))
                for i in range(TPB):
                    last = dve.tensor_scalar(dst[:, i, :], src[:, i, :], mv[:, i, 0:1], y[:, i:i + 1],
                                             ALU.subtract, ALU.mult)
                return last

            def batch_tiles(t, b):
                return t[:, TPB * b:TPB * b + TPB, :]

            def norm_x(l, b):
                if l == 0:
                    dve.wait_ge(sem(f"x_in{b}"), 16)
                else:
                    dve.wait_ge(sem("xnd_in0"), 16 * B)
                normalise(batch_tiles(X, b), batch_tiles(XM, b)).then_inc(sem(f"xn_ready{l}"), 1)

            def k_low(l):
                dve.wait_ge(sem("kh_ready"), l + 1)
                dve.scalar_tensor_tensor(out=Kl[l], in0=bank(l)[:, 0:B * KV], scalar=HD ** -0.5,
                                         in1=Kh[l].bitcast(F32), op0=ALU.mult, op1=ALU.subtract)\
                   .then_inc(sem("kl_ready"), 1)

            def q_low(l, b):
                dve.wait_ge(sem(f"qhi_ready{l}"), b + 1)
                dve.tensor_tensor(qlo[:, :], bank(7), qhi[:, :].bitcast(F32), ALU.subtract)\
                   .then_inc(sem(f"qlo_ready{l}"), 1)

            def soft(l, n):
                dve.wait_ge(sem(f"s_ps{l}"), n + 1)
                hf = n % 2
                s = PS[:, 1024 * hf:1024 * hf + 1024].rearrange("p (g c) -> p g c", g=2)[:, :, 0:GK]\
                    .rearrange("p g (j k) -> p g j k", j=JH)
                m = mx[:, hf, :].rearrange("p (g j) -> p g j", g=2)
                link(dve.tensor_reduce(m, s, AX.X, ALU.max))
                if n >= 2:
                    dve.wait_ge(sem(f"exp{l}"), n - 1)
                dve.tensor_tensor(Dm[:, hf, :, :].rearrange("p g (j k) -> p g j k", j=JH), s,
                                  m.unsqueeze(3).to_broadcast([P, 2, JH, KV]), ALU.subtract)\
                   .then_inc(sem(f"sub{l}"), 1)

            def divide(l, v):
                dve.wait_ge(sem(f"o_ps{l}"), v + 1)
                link(dve.reciprocal(rden[:, :], bank(6)[:, 256:512]))
                dve.tensor_tensor(OT[:, v % 2, :], bank(6)[:, 0:256], rden[:, :], ALU.mult)\
                   .then_inc(sem(f"ot_ready{l}"), 1)

            def residual(l, v):
                dve.wait_ge(sem(f"y_ps{l}"), v + 1)
                dve.wait_ge(sem(f"xb_ready{l}"), v // 2 + 1)
                xs = X[:, 2 * v:2 * v + 2, :]
                ins = dve.scalar_tensor_tensor(out=xs, in0=bank(7)[:, 0:256].rearrange("p (t d) -> p t d", t=2),
                                               scalar=tg[:, l:l + 1], in1=xs, op0=ALU.mult, op1=ALU.add)
                ins.then_inc(sem(f"resid{l}"), 1)
                if v % 2:
                    b = v // 2
                    dve.wait_ge(sem(f"resid{l}"), v + 1)
                    dve.wait_ge(sem(f"xt_ps{l}"), b + 1)
                    normalise(batch_tiles(X, b), batch_tiles(XM, b)).then_inc(sem(f"xm_ready{l}"), 1)

            def attention(l):
                if l == 0:
                    norm_x(0, 0)
                    dve.wait_ge(sem("cst_in"), 16)
                    k_low(0)
                    q_low(0, 0)
                    norm_x(0, 1)
                    dve.wait_ge(sem("kr_in0"), 16 * 3 * G)
                    for j in range(JH):
                        last = dve.tensor_scalar(kaug[0:96, 0, :, j, :],
                                                 KR[0].bitcast(F32).rearrange("p (n k) -> p n k", k=KV),
                                                 cst[0:96, C_HM + j:C_HM + j + 1], None, ALU.mult)
                    last.then_inc(sem("kaug_ready"), 1)
                    k_low(1)
                else:
                    q_low(l, 0)
                for t in range(NT):
                    b = t // TPB
                    soft(l, 2 * t)
                    soft(l, 2 * t + 1)
                    if l == 0 and t == 5:
                        dve.wait_ge(sem("maskb_ready"), 1)
                        link(dve.tensor_reduce(nanrow[:, :], mcnt.rearrange("p (t k) -> p t k", t=NT), AX.X, ALU.min))
                        link(dve.tensor_scalar(nanrow[:, :], nanrow[:, :], -HUGE, 10.0, ALU.mult, ALU.mult))
                        dve.tensor_scalar(nanrow[:, :], nanrow[:, :], 0.0, None, ALU.mult).then_inc(sem("mask_ready"), 1)
                    if t % TPB == 1 and b + 1 < B:
                        q_low(l, b + 1)
                    if t % TPB == 2 and b + 2 < B:
                        norm_x(l, b + 2)
                    if t % 2 == 0 and t >= 4:
                        residual(l, t // 2 - 2)
                    if t % 2 == 0 and t >= 2:
                        divide(l, t // 2 - 1)
                residual(l, NT // 2 - 2)
                divide(l, NT // 2 - 1)
                residual(l, NT // 2 - 1)

            def routing(l):
                dve.wait_ge(sem(f"lg_ps{l}"), B)
                link(dve.tensor_copy(L, bank(7)[:, 0:NT * E].rearrange("p (t e) -> p t e", e=E)))
                full = [P, NT, E, E]
                other = L.unsqueeze(2).to_broadcast(full)
                own = L.unsqueeze(3).to_broadcast(full)
                dve.tensor_tensor(cmp1, other, own, ALU.is_equal)
                link(dve.tensor_reduce(small[:, 0, :], L, AX.X, ALU.max))
                dve.tensor_tensor(cmp1, cmp1, cst[:, C_LT:C_LT + E * E].rearrange("p (e f) -> p e f", e=E)
                                  .unsqueeze(1).to_broadcast(full), ALU.mult)
                dve.tensor_tensor(tmpE, L, small[:, 0, :].unsqueeze(2).to_broadcast([P, NT, E]),
                                  ALU.subtract).then_inc(sem(f"lsub{l}"), 1)
                link(dve.tensor_tensor(cmp2, other, own, ALU.is_gt))
                link(dve.tensor_tensor(cmp1, cmp1, cmp2, ALU.add))
                link(dve.tensor_reduce(rank, cmp1, AX.X, ALU.add))
                dve.tensor_scalar(Ab[:, :, :], rank, 1.5, None, ALU.is_lt).then_inc(sem(f"chosen{l}"), 1)
                for k in range(TOPK):
                    last = dve.tensor_scalar(M[:, k, :, :], rank, float(k), None, ALU.is_equal)
                link(last)
                dve.wait_ge(sem(f"lexp{l}"), 1)
                link(dve.tensor_reduce(small[:, 1, :], ex, AX.X, ALU.add))
                link(dve.reciprocal(small[:, 2, :], small[:, 1, :]))
                link(dve.tensor_scalar(small[:, 2, :], small[:, 2, :], tg[:, 2 + l:3 + l], None, ALU.mult))
                for k in range(TOPK):
                    link(dve.tensor_tensor(tmpE, ex, M[:, k, :, :], ALU.mult))
                    link(dve.tensor_reduce(small[:, 3, :], tmpE, AX.X, ALU.add))
                    link(dve.tensor_tensor(wk[:, k, :], small[:, 3, :], small[:, 2, :], ALU.mult))
                dve.wait_ge(sem(f"place_ps{l}"), 1)
                place = bank(6)[:, 0:NT * E].rearrange("p (t e) -> p t e", e=E)
                count = bank(6)[:, NT * E:(NT + 1) * E]
                link(dve.tensor_copy(tbl[:, 0, :], count))
                link(dve.tensor_tensor(n16, tbl[:, 0, :].unsqueeze(2).to_broadcast([P, E, NT]),
                                       cst[:, C_J:C_J + NT].unsqueeze(1).to_broadcast([P, E, NT]), ALU.is_gt))
                link(dve.tensor_reduce(tbl[:, 1, :], n16, AX.X, ALU.add))
                sq = n16[:, :, 0:E]
                for row, c0 in ((2, C_LT), (3, C_LE)):
                    link(dve.tensor_tensor(sq, tbl[:, 1, :].unsqueeze(1).to_broadcast([P, E, E]),
                                           cst[:, c0:c0 + E * E].rearrange("p (e f) -> p e f", e=E), ALU.mult))
                    link(dve.tensor_reduce(tbl[:, row, :], sq, AX.X, ALU.add))
                link(dve.tensor_scalar(tbl[:, 2, :], tbl[:, 2, :], float(P), None, ALU.mult))
                link(dve.tensor_tensor(rank, place, tbl[:, 2, :].unsqueeze(1).to_broadcast([P, NT, E]), ALU.add))
                for k in range(TOPK):
                    link(dve.tensor_tensor(tmpE, rank, M[:, k, :, :], ALU.mult))
                    link(dve.tensor_reduce(slot[:, :, k], tmpE, AX.X, ALU.add))
                link(dve.tensor_copy(sloti[:, 0, :], slot[:, :, :].rearrange("p t k -> p (t k)")))
                dve.tensor_scalar(sloti[:, 1, :], sloti[:, 0, :], P - 1, None, ALU.bitwise_and)
                link(dve.tensor_scalar(sloti[:, 2, :], sloti[:, 0, :], 7, None, ALU.logical_shift_right))
                link(dve.tensor_copy(slotb[:, :, :], sloti[:, 1:3, :]))
                link(dve.tensor_tensor(ohhi, cst[:, C_HI:C_HI + SLOTS].unsqueeze(1).to_broadcast([P, PAIRS, SLOTS]),
                                       slotb[:, 1, :].unsqueeze(2).to_broadcast([P, PAIRS, SLOTS]), ALU.is_equal))
                dve.tensor_scalar(ohpt[:, :, 0:SLOTS], ohhi, cst[:, C_P:C_P + 1], None, ALU.mult)
                dve.tensor_tensor(ohpt[:, :, SLOTS:2 * SLOTS], ohhi,
                                  cst[:, C_TK:C_TK + PAIRS].unsqueeze(2).to_broadcast([P, PAIRS, SLOTS]), ALU.mult)
                dve.tensor_tensor(ohlo, cst[:, C_LO:C_LO + P].unsqueeze(1).to_broadcast([P, PAIRS, P]),
                                  slotb[:, 0, :].unsqueeze(2).to_broadcast([P, PAIRS, P]), ALU.is_equal)\
                   .then_inc(sem(f"onehot{l}"), 1)
                link(dve.tensor_tensor(xof[:, 0:SLOTS, :], cst[0:1, C_HI:C_HI + SLOTS].unsqueeze(2).to_broadcast([1, SLOTS, E]),
                                       tbl[0:1, 3, :].unsqueeze(1).to_broadcast([1, SLOTS, E]), ALU.is_ge))
                link(dve.tensor_reduce(xoff[:, 0:SLOTS], xof[:, 0:SLOTS, :], AX.X, ALU.add))
                dve.tensor_scalar(xofi[:, 0, 0:SLOTS], xoff[:, 0:SLOTS], float(E - 1), float(F), ALU.min, ALU.mult)
                dve.tensor_scalar(xofi[:, 1, 0:SLOTS], xoff[:, 0:SLOTS], float(E - 1), float(BW), ALU.min, ALU.mult)\
                   .then_inc(sem(f"xof_ready{l}"), 1)
                dve.wait_ge(sem(f"inv_ps{l}"), 1)
                tk = idf[:, 1, :]
                link(dve.tensor_copy(idf[:, 0:2, :], bank(5)[:, 0:2 * SLOTS].rearrange("p (a s) -> p a s", a=2)))
                link(dve.tensor_scalar(idf[:, 2, :], tk, -1.0, float(P), ALU.add, ALU.mult))
                link(dve.tensor_tensor(idf[:, 0, :], idf[:, 0, :], idf[:, 2, :], ALU.add))
                link(dve.tensor_copy(idi[:, :], idf[:, 0, :]))
                dve.tensor_scalar(gidx[:, :], idi[:, :].bitcast(U32), B * Q - 1, None, ALU.bitwise_and)\
                   .then_inc(sem(f"gidx_ready{l}"), 1)
                link(dve.tensor_scalar(idf[:, 2, :], tk, 0.5, float(4 * B * Q), ALU.is_lt, ALU.mult))
                dve.tensor_tensor(sidx[:, :], idf[:, 0, :], idf[:, 2, :], ALU.add).then_inc(sem(f"sidx_ready{l}"), 1)

            def experts(l):
                dve.wait_ge(sem(f"xof_ready{l}"), 1)
                dve.wait_ge(sem(f"ew_in{l}"), 16 * 4)

                at = {}

                def load_expert(s, c):
                    at[c] = dve.value_load(xofi[0:1, 1, bass.ds(s, 1)], min_val=0, max_val=(E - 1) * BW)

                def x_copy(s, c):
                    dve.wait_ge(sem(f"xT_ps{l}"), s + 1)
                    if c >= 2:
                        dve.wait_ge(sem(f"h_ps{l}"), s - 1)
                    dve.tensor_copy(XT[:, c % 2, :], bank(c % 2)[:, 0:P]).then_inc(sem(f"xT_ready{l}"), 1)

                def bias(s, c):
                    dve.wait_ge(sem(f"h_ps{l}"), s + 1)
                    if c >= 2:
                        dve.wait_ge(sem(f"gelu{l}"), s - 1)
                    dve.tensor_tensor(hb[:, c % 2, :].rearrange("p (n q) -> p n q", n=FC),
                                      bank(2 + c % 2).rearrange("p (n q) -> p n q", n=FC),
                                      BB[:, bass.ds(at[c], FC)].unsqueeze(2).to_broadcast([P, FC, P]), ALU.add)\
                       .then_inc(sem(f"h_ready{l}"), 1)

                def finish(s, c, i):
                    dve.wait_ge(sem(f"yt_ps{l}"), s + 1)
                    if c >= 4:
                        dve.wait_ge(sem(f"scat{c % 4}"), 16 * (l * scatters_of(c % 4) + RING // 4 * i + c // 4))
                    dve.tensor_tensor(Yb[:, c % 4, :], bank(6 + c % 2)[:, 0:D], BB[:, bass.ds(at[c] + FC, D)], ALU.add)\
                       .then_inc(sem(f"y_ready{l}"), 1)

                def steps(i, first, n):
                    for c in range(first, first + n):
                        s = RING * i + c
                        load_expert(s + 2, c + 2)
                        x_copy(s + 3, c + 3)
                        bias(s + 2, c + 2)
                        if c < first + 2:
                            load_expert(s, c)
                        finish(s, c, i)

                for s in range(2):
                    load_expert(s, s)
                    x_copy(s, s)
                bias(0, 0)
                x_copy(2, 2)
                bias(1, 1)
                steps(0, 0, HEAD)
                with dve.Fori(0, ROUNDS) as i:
                    steps(i, HEAD, RING)
                for s in range(SLOTS - TAIL, SLOTS):
                    load_expert(s, s)
                    if s + 2 < SLOTS:
                        load_expert(s + 2, s + 2)
                        bias(s + 2, s + 2)
                    finish(s, s, 0)

            def combine(l, b):
                dve.wait_ge(sem(f"y_in{l}{b}"), 16 * TOPK)
                for k in range(TOPK):
                    for t in range(TPB * b, TPB * b + TPB):
                        last = dve.scalar_tensor_tensor(out=X[:, t, :], in0=Yin[:, k, t, :], scalar=wk[:, k, t:t + 1],
                                                        in1=X[:, t, :], op0=ALU.mult, op1=ALU.add)
                    if k < TOPK - 1:
                        link(last)
                last.then_inc(sem(f"x_done{l}"), 1)

            attention(0)
            routing(0)
            experts(0)
            for b in range(B):
                combine(0, b)
                if b < 2:
                    dve.wait_ge(sem("x_done0"), b + 1)
                    norm_x(1, b)
            dve.wait_ge(sem("x_done0"), B)
            attention(1)
            routing(1)
            experts(1)
            for b in range(B):
                combine(1, b)


_OUT = ((B * Q, D), "float32")


def kernel(**inputs):
    import concourse.bacc as bacc
    from concourse.bass_utils import run_bass_kernel_spmd as run

    a = {n: np.asarray(v) for n, v in inputs.items()}
    T = np.transpose
    attnw = np.stack([
        np.stack([T(a["L0_xattn_Wq"]), T(a["L0_xattn_Wk"]), T(a["L0_xattn_Wv"]), T(a["L0_xattn_Wo"])], 1),
        np.stack([T(a["L1_xattn_W_q"]), T(a["L1_xattn_W_k"]), T(a["L1_xattn_W_v"]), T(a["L1_xattn_W_o"])], 1)], 1)
    w1 = np.stack([T(a["L0_ffn_w1"], (1, 0, 2)).reshape(D, E * F), T(a["L1_ffn_w1"], (2, 1, 0)).reshape(D, E * F)])
    w2 = np.stack([T(a["L0_ffn_w2"].reshape(E, FC, P, D), (2, 0, 1, 3)).reshape(P, E * FC * D),
                   T(a["L1_ffn_w2"].reshape(D, E, FC, P), (3, 1, 2, 0)).reshape(P, E * FC * D)])
    arrays = {
        "x": a["x"].reshape(B * Q, D),
        "ctxT": T(a["ctx_1024"].reshape(B * KV, D)),
        "attnw": attnw,
        "bo": a["L0_xattn_bo"].reshape(1, D),
        "gates": np.concatenate([a["g_xattn"].reshape(1, 2), a["g_ffn"].reshape(1, 2)], 1),
        "posq": a["itok_BxS_8_8191"].reshape(1, B * Q),
        "posk": a["itok_BxS2_1_8191"].reshape(1, B * KV),
        "mask": a["mask_BxSxS2_if1"].reshape(B * Q, KV),
        "router": np.stack([a["L0_ffn_w_router"], T(a["L1_ffn_gate_w"])], 1),
        "w1": w1,
        "w2": w2,
        "b1": np.stack([T(a[f"L{l}_ffn_b1"].reshape(E, FC, P), (2, 0, 1)) for l in range(LAYERS)]),
        "b2": np.stack([a[f"L{l}_ffn_b2"] for l in range(LAYERS)]),
        "consts": constant_table(),
    }
    nc = bacc.Bacc("TRN2", target_bir_lowering=False, num_devices=1)
    feed, args = {}, {}
    for name, v in arrays.items():
        v = np.ascontiguousarray(v)
        feed[f"in_{name}"] = v
        args[name] = nc.dram_tensor(f"in_{name}", v.shape, mybir.dt.from_np(v.dtype), kind="ExternalInput").ap()
    args["out"] = nc.dram_tensor("out_x", _OUT[0], F32, kind="ExternalOutput").ap()
    build(nc, **args)
    r = run(nc, [feed], core_ids=[0])
    return r.results[0]["out_x"].reshape(B, Q, D)
```

```python
from contextlib import ExitStack

import numpy as np

import concourse.bass as bass
from concourse import mybir

F32, F32R, BF16 = mybir.dt.float32, mybir.dt.float32r, mybir.dt.bfloat16
I32, U32 = mybir.dt.int32, mybir.dt.uint32
ALU, ACT, AX = mybir.AluOpType, mybir.ActivationFunctionType, mybir.AxisListType

B, Q, KV, D, H, HD = 4, 512, 77, 128, 16, 8
E, F, TOPK = 8, 512, 2
P = 128
LAYERS = 2
NT = B * Q // P
TPB = Q // P
G = 4
JH = H // G
GK = JH * KV
PW = GK + 1
NC3 = 3
CH = PW // NC3
FC = F // P
BW = FC + D
SLOTS = B * Q * TOPK // P + E - 1
PAIRS = NT * TOPK
RING = 8
HEAD, TAIL = 4, 3
ROUNDS = (SLOTS - HEAD - TAIL) // RING
BIG = 1e30
HUGE = 3e38
LN_EPS = 1e-5

C_ID, C_LO = 0, 128
C_HI = 256
C_TRI = C_HI + SLOTS
C_TK = C_TRI + P
C_P = C_TK + PAIRS
C_HM = C_P + 1
C_NEG = C_HM + JH
C_QA = C_NEG + H
C_SL = C_QA + 3
C_BD = C_SL + 1
C_J = C_BD + LAYERS * NC3 * 32
C_LT = C_J + NT
C_LE = C_LT + E * E
C_END = C_LE + E * E


def constant_table():
    c = np.zeros((P, C_END), np.float32)
    p = np.arange(P)
    c[:, C_ID:C_ID + P] = np.eye(P)
    c[:, C_LO:C_LO + P] = np.arange(P)
    c[:, C_HI:C_HI + SLOTS] = np.arange(SLOTS)
    c[:, C_TRI:C_TRI + P] = p[:, None] < p[None, :]
    for t in range(NT):
        for k in range(TOPK):
            c[:, C_TK + TOPK * t + k] = t + NT * k + 1
    c[:, C_P] = p
    for j in range(JH):
        c[:96, C_HM + j] = (p[:96] % 32) // HD == j
    ratio = 2.0 ** (-8.0 / H)
    slope = np.array([ratio ** i for i in range(1, H + 1)], np.float32)
    high = (((slope.view(np.uint32) + 0x800) >> 12) << 12).astype(np.uint32).view(np.float32)
    for r, part in ((2, high), (3, slope - high), (4, high), (5, slope - high)):
        c[96 + r, C_NEG:C_NEG + H] = -part
    c[98:100, C_QA] = 1.0
    c[100:102, C_QA + 1] = 1.0
    c[96:98, C_QA + 2] = 1.0
    c[:H, C_SL] = slope
    for layer in range(LAYERS):
        for n in range(NC3):
            for i in range(CH):
                r = n * CH + i
                at = C_BD + (layer * NC3 + n) * 32
                if r < GK:
                    c[i, at + HD * (r // KV):at + HD * (r // KV) + HD] = 1.0
                elif layer == 1:
                    c[i, at:at + 32] = 1.0
    c[:, C_J:C_J + NT] = P * np.arange(NT)
    e = np.arange(E)
    c[:, C_LT:C_LT + E * E] = (e[None, :] < e[:, None]).reshape(1, -1)
    c[:, C_LE:C_LE + E * E] = (e[None, :] <= e[:, None]).reshape(1, -1)
    return c


def build(nc, x, ctxT, attnw, bo, gates, posq, posk, mask, router, w1, w2, b1, b2, consts, out):
    ctx = ExitStack()
    with ctx:
        def sb(name, shape, dt=F32):
            return ctx.enter_context(nc.sbuf_tensor(name, shape, dt))

        made = {}

        def sem(name):
            if name not in made:
                made[name] = ctx.enter_context(nc.semaphore(name))
            return made[name]

        cst = sb("cst", [P, C_END])
        aw = sb("aw", [P, LAYERS, 4, D])
        wq3 = sb("wq3", [P, LAYERS, G, 3, 32])
        rw = sb("rw", [P, LAYERS, E])
        X = sb("X", [P, NT, D])
        XM = sb("XM", [P, NT, D])
        xnT = sb("xnT", [P, 2, Q])
        misc = sb("misc", [P, 2 * Q])
        qaug = sb("qaug", [P, 2, G, Q], F32R)
        kaug = sb("kaug", [P, LAYERS, G * B, JH, KV], F32R)
        vbd = sb("vbd", [CH, LAYERS, NC3, B * G, 32])
        rsmall = sb("rsmall", [P, 256])
        pos = sb("pos", [P, B * Q], F32R)
        maskb = sb("maskb", [P, NT, KV], BF16)
        nanrow = sb("nanrow", [P, NT])
        W1 = sb("W1", [P, E * F])
        W2 = sb("W2", [P, E * FC * D])
        BB = sb("BB", [P, E * BW])
        scratch = sb("scratch", [P, 4004])
        tgbo = sb("tgbo", [P, D])
        gt = sb("gt", [P, 4])
        tg = sb("tg", [P, 4])
        identb = sb("identb", [P, P], BF16)
        trib = sb("trib", [P, P], BF16)
        onesb = sb("onesb", [P, P], BF16)
        stat = misc[:, 768:864].rearrange("p (t a) -> p t a", a=6)
        mv = misc[:, 864:896].rearrange("p (t a) -> p t a", a=2)
        rstd = misc[:, 896:944].rearrange("p (a t) -> p a t", a=3)
        mx = sb("mx", [P, 2, 8])
        arenaA = sb("arenaA", [P, 6144])
        arenaB = sb("arenaB", [P, 4216])
        PT = arenaA[0:CH, 0:2 * G * NC3 * P].rearrange("p (u m q) -> p u m q", u=2, m=G * NC3)
        Dm = arenaB[:, 0:2 * 2 * GK].rearrange("p (n g k) -> p n g k", n=2, g=2)
        Pr = arenaB[:, 4 * GK:4 * GK + 2 * G * PW].rearrange("p (u g k) -> p u g k", u=2, g=G)
        rden = arenaB[:, 3704:3704 + P]
        OT = arenaB[:, 3960:4216].rearrange("p (u q) -> p u q", u=2)
        GX = arenaA[:, 0:RING * D].rearrange("p (n d) -> p n d", n=RING)
        W1s = arenaA[:, RING * D:RING * D + 4 * F].rearrange("p (n f) -> p n f", n=4)
        XT = arenaB[:, 0:256].rearrange("p (n d) -> p n d", n=2)
        hb = arenaB[:, 256:1280].rearrange("p (n f) -> p n f", n=2)
        ge = arenaB[:, 1280:3328].rearrange("p (n f) -> p n f", n=4)
        Yb = arenaB[:, 3328:3840].rearrange("p (n d) -> p n d", n=4)
        wtie = arenaA[:, 0:128].rearrange("p (t e) -> p t e", e=E)
        Lrest = arenaA[:, 128:256].rearrange("p (t e) -> p t e", e=E)
        tmpK = arenaA[:, 256:512].rearrange("p (k t e) -> p k t e", k=TOPK, e=E)
        xmT = arenaA[:, 4096:6144].rearrange("p (b q) -> p b q", b=B)
        ohlo = arenaA[:, 2048:4096].bitcast(BF16).rearrange("p (n c) -> p n c", n=PAIRS)
        ohhi = arenaA[:, 4096:4096 + PAIRS * SLOTS // 2].bitcast(BF16).rearrange("p (n c) -> p n c", n=PAIRS)
        ohpt = arenaA[:, 4736:4736 + PAIRS * SLOTS].bitcast(BF16).rearrange("p (n c) -> p n c", n=PAIRS)
        Yin = arenaA[:, 0:4096].rearrange("p (k t d) -> p k t d", k=TOPK, t=NT)
        posi = W1[96:128, 0:2048].bitcast(I32)
        posf = W1[96:128, 2048:4096]
        posh = W2[96:128, 0:2048].bitcast(F32R)
        KR = [W2[0:96, 1232 * l:1232 * l + 1232].bitcast(F32R) for l in range(LAYERS)]
        Vs = [W2[0:KV, 2464 + 512 * l:2464 + 512 * l + 512] for l in range(LAYERS)]
        mski = scratch[:, 0:NT * KV].bitcast(I32)
        ctxs = scratch[:, 1232:1232 + B * KV]
        kpi = scratch[0:H, 1540:1540 + B * KV].bitcast(I32)
        kpf = scratch[0:H, 1848:1848 + B * KV]
        kph = scratch[0:H, 2156:2156 + B * KV].bitcast(F32R)
        kpl = scratch[0:H, 2464:2464 + B * KV].bitcast(F32R)
        mcnt = scratch[:, 2772:2772 + NT * KV]
        wk3 = misc[:, 0:LAYERS * 3 * D].rearrange("p (l g a c) -> p l g a c", l=LAYERS, g=G, a=3)
        w3 = (wq3, wk3)
        qhi = arenaA[:, 3072:3072 + Q].bitcast(F32R)
        qlo = arenaA[:, 3072 + Q:3072 + 2 * Q].bitcast(F32R)
        qh32, ql32 = misc[:, 0:Q], misc[:, Q:2 * Q]
        L, rank, ex, tmpE = (qh32[:, 128 * i:128 * i + 128].rearrange("p (t e) -> p t e", e=E) for i in range(4))
        M = ql32[:, 0:256].rearrange("p (k t e) -> p k t e", k=TOPK, e=E)
        n16 = ql32[:, 256:384].rearrange("p (e t) -> p e t", e=E)
        slot = ql32[:, 384:416].rearrange("p (t k) -> p t k", k=TOPK)
        slotb = ql32[:, 416:480].rearrange("p (a n) -> p a n", a=2)
        xof = arenaB[0:1, 0:SLOTS * E].rearrange("p (s e) -> p s e", e=E)
        Ab = sb("Ab", [P, NT, E], BF16)
        wk = sb("wk", [P, TOPK, NT])
        small = rsmall[:, 160:160 + 4 * NT].rearrange("p (a t) -> p a t", a=4)
        tbl = rsmall[:, 224:256].rearrange("p (a e) -> p a e", a=4)
        xoff = arenaB[0:1, 400:400 + SLOTS]
        sloti = arenaB[:, 512:512 + 3 * PAIRS].bitcast(I32).rearrange("p (a n) -> p a n", a=3)
        xofi = sb("xofi", [1, 2, SLOTS + 1], I32)
        idf = rsmall[:, 0:3 * SLOTS].rearrange("p (a s) -> p a s", a=3)
        idi = rsmall[:, 3 * SLOTS:4 * SLOTS].bitcast(I32)
        gidx = sb("gidx", [P, SLOTS], U32)
        sidx = sb("sidx", [P, SLOTS], U32)

        PS = ctx.enter_context(nc.psum_tensor("PS", [P, 8 * 512], F32))

        def bank(n):
            return PS[:, 512 * n:512 * n + 512]

        xnd = [nc.dram_tensor(f"xnd{l}", (B * Q, D), F32, kind="Internal").ap() for l in range(LAYERS)]
        yd = [nc.dram_tensor(f"yd{l}", (TOPK * B * Q, D), F32, kind="Internal").ap() for l in range(LAYERS)]

        def xm_wait(engine, l, b, tiles=TPB):
            if b < B - 1:
                engine.wait_ge(sem(f"xm_ready{l}"), b + 1)
            else:
                engine.wait_ge(sem(f"xm_own{l}"), tiles)

        def normalise(engine, link, t0, n, signal):
            y, var, t = (rstd[:, i, t0:t0 + n] for i in range(3))
            for _ in range(3):
                link(engine.tensor_tensor(t, y, y, ALU.mult))
                link(engine.tensor_tensor(t, t, var, ALU.mult))
                if engine is nc.gpsimd:
                    link(engine.tensor_scalar(t, t, 1.5, None, ALU.add))
                    link(engine.tensor_tensor(y, t, y, ALU.mult))
                else:
                    link(engine.scalar_tensor_tensor(out=y, in0=t, scalar=1.5, in1=y, op0=ALU.add, op1=ALU.mult))
            for i in range(t0, t0 + n):
                last = engine.tensor_scalar(XM[:, i, :], X[:, i, :], mv[:, i, 0:1], y[:, i - t0:i - t0 + 1],
                                            ALU.subtract, ALU.mult)
                if i == t0 + n - 1 or signal == "xn_pool" and i % TPB == TPB - 1 or signal.startswith("xm_own"):
                    last.then_inc(sem(signal), 1)
                elif engine is nc.gpsimd:
                    link(last)

        def tk_product(half):
            n = PAIRS // 2
            rows = slice(n * half, n * half + n)
            return (ohpt[:, rows, SLOTS:2 * SLOTS], ohhi[:, rows, :],
                    cst[:, C_TK + n * half:C_TK + n * half + n].unsqueeze(2).to_broadcast([P, n, SLOTS]), ALU.mult)

        def low_onehot(c):
            rows = slice(8 * c, 8 * c + 8)
            return (ohlo[:, rows, :], cst[:, C_LO:C_LO + P].unsqueeze(1).to_broadcast([P, 8, P]),
                    slotb[:, 0, rows].unsqueeze(2).to_broadcast([P, 8, P]), ALU.is_equal)

        def k_banks(l):
            return PS[:, 2048 * l:2048 * l + 2048].rearrange("p (g c) -> p g c", g=G)[:, :, 0:B * KV]

        def k_heads(engine, j):
            src, dst = KR[0].bitcast(F32).rearrange("p (n k) -> p n k", k=KV), kaug[0:96, 0, :, j, :]
            only = cst[0:96, C_HM + j:C_HM + j + 1]
            if engine is nc.scalar:
                return nc.scalar.activation(dst, src, ACT.Copy, scale=only)
            return nc.vector.tensor_scalar(dst, src, only, None, ALU.mult)

        def q_plan(t):
            b, i = t // TPB, t % TPB
            return b + 1 if b + 1 < B and i == 0 else None

        def q_done(l, b):
            return b + 1 + l

        def q_half(rows, l, half):
            n = Q >> l
            ps = PS[rows, 2048 * half:2048 * half + 2048].rearrange("p (g c) -> p g c", g=G)[:, :, 0:n]
            return qaug[rows, 0, :, n * half:n * half + n], ps

        def xn_plan(t):
            return t // TPB + 2 if t % TPB == 2 and t // TPB + 2 < B else None

        def gathers_of(j):
            return (SLOTS - j + RING - 1) // RING

        def scatters_of(j):
            return (SLOTS - j + 3) // 4

        ident = cst[:, C_ID:C_ID + P]
        x_v = x.rearrange("(t p) d -> p t d", p=P)
        out_v = out.rearrange("(t p) d -> p t d", p=P)

        block = ctx.enter_context(nc.Block())

        @block.sync
        def _(sp):
            sp.dma_start(scratch[:, 1232:1232 + B * KV], ctxT).then_inc(sem("ctx_in"), 16)
            sp.dma_start(aw[:, 0], attnw[:, 0]).then_inc(sem("aw_in0"), 16)
            for b in range(B):
                sp.dma_start(X[:, TPB * b:TPB * b + TPB, :], x_v[:, TPB * b:TPB * b + TPB, :])\
                  .then_inc(sem(f"x_in{b}"), 16)
            sp.dma_start(aw[:, 1], attnw[:, 1]).then_inc(sem("aw_in1"), 16)
            sp.dma_start(mski, mask.rearrange("(t p) k -> p t k", p=P)).then_inc(sem("mask_in"), 16)
            sp.dma_start(rw[:, :, :], router).then_inc(sem("rw_in"), 16)

            def spread_v(l):
                sp.wait_ge(sem("v_ready"), l + 1)
                sp.wait_ge(sem("vbd_zero"), 1)
                for j in range(JH):
                    k = 0
                    while k < KV:
                        n, r = divmod(KV * j + k, CH)
                        m = min(CH - r, KV - k)
                        src = Vs[l][k:k + m, :].rearrange("k (b g j d) -> k (b g) j d", b=B, g=G, j=JH)
                        sp.dma_start(vbd[r:r + m, l, n, :, HD * j:HD * j + HD], src[:, :, j, :])\
                          .then_inc(sem(f"vbd_in{l}"), 16)
                        k += m

            def spread_q(l, b):
                sp.wait_ge(sem(f"qlo_ready{l}"), q_done(l, b))
                if b >= 2:
                    sp.wait_ge(sem(f"s_ps{l}"), 2 * TPB * (b - 1))
                elif l:
                    sp.wait_ge(sem("s_ps0"), 2 * NT)
                for g in range(G):
                    for part, src in enumerate((qhi, qhi, qlo)):
                        sp.dma_start(qaug[32 * part:32 * part + 32, b % 2, g, :].bitcast(F32),
                                     src[32 * g:32 * g + 32, :].bitcast(F32)).then_inc(sem(f"qa_in{l}"), 16)

            def positions(b):
                if b == 0:
                    sp.wait_ge(sem("pos_ready"), 1)
                if b < 2:
                    sp.wait_ge(sem("s_ps0"), 2 * NT)
                else:
                    sp.wait_ge(sem("s_ps1"), 2 * TPB * (b - 1))
                sp.dma_start(qaug[96:128, b % 2, :, :].bitcast(F32),
                             pos[96:128, Q * b:Q * b + Q].bitcast(F32).unsqueeze(1).to_broadcast([32, G, Q]))\
                  .then_inc(sem(f"pos_in{b}"), 16)

            spread_v(0)
            spread_v(1)
            spread_q(0, 1)

            def expert_weights(l):
                sp.dma_start(W1[:, :], w1[l]).then_inc(sem(f"ew_in{l}"), 16)
                sp.dma_start(W2[:, :], w2[l]).then_inc(sem(f"ew_in{l}"), 16)
                biases = BB[:, :].rearrange("p (e c) -> p e c", c=BW)
                sp.dma_start(biases[:, :, 0:FC], b1[l]).then_inc(sem(f"ew_in{l}"), 16)
                sp.dma_start(biases[:, :, FC:BW], b2[l:l + 1].to_broadcast([P, E, D])).then_inc(sem(f"ew_in{l}"), 16)

            for l in range(LAYERS):
                if l == 0:
                    spread_q(0, 2)
                    spread_q(0, 3)
                    sp.wait_ge(sem("kbias_ready"), 1)
                    sp.wait_ge(sem("kconst_ready"), G)
                    for h in range(H):
                        g, j = divmod(h, JH)
                        for r, src in enumerate((kph, kpl)):
                            dst = kaug[96 + r:97 + r, 1, B * g:B * g + B, j, :].bitcast(F32)
                            sp.dma_start(dst, src[h:h + 1, :].bitcast(F32).rearrange("p (b k) -> p b k", b=B))\
                              .then_inc(sem("kbias_in"), 16)
                    sp.wait_ge(sem("pos_ready"), 1)
                    sp.wait_ge(sem("kaug_ready"), 1)
                    sp.wait_ge(sem("kaug_ready1"), JH)
                    sp.wait_ge(sem("vbd_in0"), 16 * 6)
                    sp.wait_ge(sem("vbd_in1"), 16 * 6)
                    expert_weights(0)
                else:
                    spread_q(1, 1)
                    spread_q(1, 2)
                    positions(2)
                    spread_q(1, 3)
                    positions(3)
                for b in range(B):
                    xm_wait(sp, l, b)
                    sp.dma_start(xnd[l].rearrange("(t p) d -> p t d", p=P)[:, TPB * b:TPB * b + TPB, :],
                                 XM[:, TPB * b:TPB * b + TPB, :]).then_inc(sem(f"xnd_in{l}"), 16)
                if l == 0:
                    positions(0)
                    positions(1)
                for j in range(4):
                    sp.wait_ge(sem(f"scat{j}"), 16 * (l + 1) * scatters_of(j))
                yv = yd[l].rearrange("(k t p) d -> p k t d", k=TOPK, p=P)
                for b in range(B):
                    for k in range(TOPK):
                        sp.dma_start(Yin[:, k, TPB * b:TPB * b + TPB, :], yv[:, k, TPB * b:TPB * b + TPB, :])\
                          .then_inc(sem(f"y_in{l}{b}"), 16)
                if l == 0:
                    expert_weights(1)
            for b in range(B):
                sp.wait_ge(sem("x_done1"), b + 1)
                sp.dma_start(out_v[:, TPB * b:TPB * b + TPB, :], X[:, TPB * b:TPB * b + TPB, :])\
                  .then_inc(sem("out_done"), 16)
            sp.wait_ge(sem("out_done"), 16 * B)

        @block.gpsimd
        def _(pool):
            chain = [0]

            def link(ins):
                chain[0] += 1
                ins.then_inc(sem("pool_chain"), 1)
                pool.wait_ge(sem("pool_chain"), chain[0])

            def apart(name, count):
                pool.wait_ge(sem(name), count)

            pool.memset(vbd[:, :, :, :, :], 0.0).then_inc(sem("vbd_zero"), 1)
            pool.memset(onesb[:, :], 1.0).then_inc(sem("ones_ready"), 1)
            pool.memset(Pr[:, :, :, GK:PW], 1.0).then_inc(sem("pad_ready0"), 1)
            pool.wait_ge(sem("cst_in"), 16)
            pool.tensor_copy(identb[:, :], ident).then_inc(sem("identb_ready"), 1)
            pool.tensor_copy(trib[:, :], cst[:, C_TRI:C_TRI + P]).then_inc(sem("trib_ready"), 1)

            guesses = [0]

            def finish_norm(t0, n, signal):
                guesses[0] += 1
                pool.wait_ge(sem("guess_ready"), guesses[0])
                normalise(pool, link, t0, n, signal)

            def finish_xm(l, b):
                pool.wait_ge(sem(f"xt_ps{l}"), b + 1)
                finish_norm(TPB * b, TPB, f"xm_ready{l}")
                apart(f"xm_ready{l}", b + 1)

            def biased(b):
                pool.tensor_tensor(X[:, TPB * b:TPB * b + TPB, :], X[:, TPB * b:TPB * b + TPB, :],
                                   tgbo[:, :].unsqueeze(1).to_broadcast([P, TPB, D]), ALU.add)\
                    .then_inc(sem("xb_ready0"), 1)
                apart("xb_ready0", b + 1)

            pool.wait_ge(sem("tg_ready"), 1)
            pool.wait_ge(sem("bo_in"), 16)
            link(pool.tensor_scalar(tgbo[:, :], tgbo[:, :], tg[:, 0:1], None, ALU.mult))
            pool.wait_ge(sem("norm_own"), 1)
            biased(0)
            finish_norm(TPB, NT - TPB, "xn_pool")
            apart("xn_pool", B - 1)
            for b in range(1, B):
                biased(b)
            pool.wait_ge(sem("kpos_in"), 16)
            link(pool.tensor_copy(kpf, kpi))
            link(pool.tensor_scalar(kpf, kpf, cst[0:H, C_SL:C_SL + 1], None, ALU.mult))
            link(pool.tensor_copy(kph, kpf))
            pool.tensor_tensor(kpl, kpf, kph.bitcast(F32), ALU.subtract).then_inc(sem("kbias_ready"), 1)
            apart("kbias_ready", 1)
            pool.wait_ge(sem("kl_ready"), 2)
            for j in range(JH):
                pool.tensor_scalar(kaug[0:96, 1, :, j, :],
                                   KR[1].bitcast(F32).rearrange("p (n k) -> p n k", k=KV),
                                   cst[0:96, C_HM + j:C_HM + j + 1], None, ALU.mult)\
                    .then_inc(sem("kaug_ready1"), 1)
                apart("kaug_ready1", j + 1)
            pool.wait_ge(sem("pos_parts"), 2)
            link(pool.tensor_tensor(posf, posf, posh.bitcast(F32), ALU.subtract))
            link(pool.tensor_scalar(posf, posf, cst[96:128, C_QA + 1:C_QA + 2],
                                    cst[96:128, C_QA + 2:C_QA + 3], ALU.mult, ALU.add))
            link(pool.tensor_scalar(posh, posh.bitcast(F32), cst[96:128, C_QA:C_QA + 1], None, ALU.mult))
            pool.tensor_tensor(pos[96:128, :], posh.bitcast(F32), posf, ALU.add).then_inc(sem("pos_ready"), 1)
            apart("pos_ready", 1)
            for b in range(B - 1):
                finish_xm(0, b)

            for l in range(LAYERS):
                if l:
                    pool.wait_ge(sem("y_ready0"), SLOTS)
                    for j in range(4):
                        pool.wait_ge(sem(f"scat{j}"), 16 * scatters_of(j))
                    pool.memset(Pr[:, :, :, GK:PW], 1.0).then_inc(sem("pad_ready1"), 1)
                    apart("pad_ready1", 1)
                    pool.wait_ge(sem("mask_ready"), 1)
                    for b in range(B):
                        if b == 0:
                            pool.wait_ge(sem("norm_own"), 2)
                        if b == 1:
                            finish_norm(TPB, TPB, "xn_pool")
                            apart("xn_pool", B)
                        if b == 2:
                            finish_norm(2 * TPB, NT - 2 * TPB, "xn_pool")
                            apart("xn_pool", 2 * (B - 1))
                        pool.tensor_tensor(X[:, TPB * b:TPB * b + TPB, :], X[:, TPB * b:TPB * b + TPB, :],
                                           nanrow[:, TPB * b:TPB * b + TPB].unsqueeze(2).to_broadcast([P, TPB, D]),
                                           ALU.add).then_inc(sem("xb_ready1"), 1)
                        apart("xb_ready1", b + 1)
                    for b in range(B - 1):
                        finish_xm(1, b)

                def gather(s):
                    pool.indirect_dma_start(GX[:, s % RING, :], None, xnd[l],
                                            bass.IndirectOffsetOnAxis(ap=gidx[:, s:s + 1], axis=0))\
                        .then_inc(sem(f"gath{s % RING}"), 16)

                pool.wait_ge(sem(f"ohhi_ready{l}"), 1)
                for half in range(2):
                    pool.tensor_tensor(*tk_product(half)).then_inc(sem(f"ohtk{l}"), 1)
                    apart(f"ohtk{l}", half + 1)
                pool.wait_ge(sem(f"gidx_ready{l}"), 1)
                pool.wait_ge(sem(f"xnd_in{l}"), 16 * B)
                pool.wait_ge(sem(f"resid{l}"), NT)
                for s in range(RING):
                    gather(s)
                pool.wait_ge(sem(f"sidx_ready{l}"), 1)
                for s in range(SLOTS):
                    if s + RING < SLOTS:
                        pool.wait_ge(sem(f"xT_ps{l}"), s + 1)
                        gather(s + RING)
                    pool.wait_ge(sem(f"y_ready{l}"), s + 1)
                    pool.indirect_dma_start(yd[l], bass.IndirectOffsetOnAxis(ap=sidx[:, s:s + 1], axis=0),
                                            Yb[:, s % 4, :], None, bounds_check=TOPK * B * Q - 1,
                                            oob_is_err=False).then_inc(sem(f"scat{s % 4}"), 16)

        @block.scalar
        def _(act):
            act.dma_start(cst[:, :], consts).then_inc(sem("cst_in"), 16)
            act.dma_start(gt[:, :], gates.to_broadcast([P, 4])).then_inc(sem("gt_in"), 16)
            act.dma_start(tgbo[:, :], bo.to_broadcast([P, D])).then_inc(sem("bo_in"), 16)
            act.dma_start(kpi, posk.to_broadcast([H, B * KV])).then_inc(sem("kpos_in"), 16)
            act.dma_start(posi, posq.to_broadcast([32, B * Q])).then_inc(sem("qpos_in"), 16)

            def triple(l, w):
                act.activation(w3[w][:, l], aw[:, l, w, :].rearrange("p (g c) -> p g c", g=G).unsqueeze(2)
                               .to_broadcast([P, G, 3, 32]), ACT.Copy).then_inc(sem("w3_ready"), 1)

            act.wait_ge(sem("aw_in0"), 16)
            triple(0, 1)
            triple(0, 0)
            act.wait_ge(sem("gt_in"), 16)
            act.activation(tg[:, :], gt[:, :], ACT.Tanh).then_inc(sem("tg_ready"), 1)

            def k_high(l):
                act.wait_ge(sem("k_ps"), l + 1)
                act.activation(KR[l].rearrange("p (g c) -> p g c", g=G), k_banks(l)[0:96], ACT.Copy,
                               scale=HD ** -0.5).then_inc(sem("kh_ready"), 1)

            def v_copy(l):
                act.wait_ge(sem("v_ps"), l + 1)
                act.activation(Vs[l], bank(4 + l)[0:KV, :], ACT.Copy).then_inc(sem("v_ready"), 1)

            def xnT_copy(l, b):
                act.wait_ge(sem(f"xt_ps{l}"), b + 1)
                act.activation(xnT[:, b % 2, :], bank(7), ACT.Copy).then_inc(sem(f"xt_ready{l}"), 1)

            def q_high_first(l, half):
                act.wait_ge(sem(f"q_ps{l}"), half + 1)
                if l and half == 0:
                    act.wait_ge(sem("s_ps0"), 2 * NT)
                dst, src = q_half(slice(0, 96), l, half)
                act.activation(dst, src, ACT.Copy).then_inc(sem(f"qhi_ready{l}"), 1)

            def q_high(l, b):
                act.wait_ge(sem(f"q_ps{l}"), q_done(l, b))
                if b >= 2:
                    act.wait_ge(sem(f"qa_in{l}"), 16 * 3 * G * (b - 1))
                act.activation(qhi, bank(7), ACT.Copy).then_inc(sem(f"qhi_ready{l}"), 1)

            def key_constants(g):
                neg = cst[96:128, C_NEG:C_NEG + H].rearrange("p (g j) -> p g j", g=G)
                kc = kaug[96:128, 1, :, :, :].rearrange("p (g b) j k -> p g b (j k)", g=G)
                for j in range(JH):
                    dst = kc[:, g, :, KV * j:KV * j + KV]
                    last = act.activation(dst, neg[:, g, j:j + 1].unsqueeze(2).to_broadcast([32, B, KV]), ACT.Copy)
                last.then_inc(sem("kconst_ready"), 1)

            def attention(l):
                if l == 0:
                    k_high(0)
                xnT_copy(l, 0)
                if l == 0:
                    act.wait_ge(sem("kl_ready"), 1)
                    for j in (2, 3):
                        k_heads(act, j).then_inc(sem("kaug_a"), 1)
                    v_copy(0)
                    v_copy(1)
                    act.wait_ge(sem("aw_in1"), 16)
                    triple(1, 1)
                for half in range(1 + l):
                    q_high_first(l, half)
                if l == 0:
                    k_high(1)
                    triple(1, 0)
                for t in range(NT):
                    b = t // TPB
                    for hf in range(2):
                        n = 2 * t + hf
                        act.wait_ge(sem(f"sub{l}"), n + 1)
                        if t >= 2:
                            act.wait_ge(sem(f"pt_ps{l}"), G * (t - 1))
                        act.activation(Pr[:, t % 2, 2 * hf:2 * hf + 2, 0:GK], Dm[:, hf, :, :], ACT.Exp)\
                           .then_inc(sem(f"exp{l}"), 1)
                    if t == 0:
                        xnT_copy(l, 1)
                    elif q_plan(t):
                        q_high(l, q_plan(t))
                    if l == 0 and 1 <= t <= G:
                        key_constants(t - 1)
                    if l == 0 and t == 5:
                        act.wait_ge(sem("qpos_in"), 16)
                        act.activation(posf, posi, ACT.Copy).then_inc(sem("pos_parts"), 1)
                    if l == 0 and t == 6:
                        act.wait_ge(sem("pos_parts"), 1)
                        act.activation(posh, posf, ACT.Copy).then_inc(sem("pos_parts"), 1)
                    if t >= 2:
                        act.wait_ge(sem(f"o_ps{l}"), 2 * (t - 1))
                    for g in range(G):
                        m = G * t + g
                        act.wait_ge(sem(f"pt_ps{l}"), m + 1)
                        act.activation(PT[:, t % 2, NC3 * g:NC3 * g + NC3, :],
                                       bank(4 + m % 2)[0:CH, 0:NC3 * P].rearrange("p (c q) -> p c q", c=NC3),
                                       ACT.Copy).then_inc(sem(f"pt_ready{l}"), 1)
                    if t == 0:
                        q_high(l, 1)
                    elif xn_plan(t):
                        xnT_copy(l, xn_plan(t))

            def routing(l):
                for b in range(B):
                    act.wait_ge(sem(f"xmt_ps{l}"), b + 1)
                    act.activation(xmT[:, b, :], bank(b), ACT.Copy).then_inc(sem(f"xmt_ready{l}"), 1)
                act.wait_ge(sem(f"lsub{l}"), 1)
                act.activation(ex, tmpE, ACT.Exp).then_inc(sem(f"lexp{l}"), 1)

            def experts(l):
                def gelu(s, c):
                    act.wait_ge(sem(f"h_ready{l}"), s + 1)
                    if c >= 4:
                        act.wait_ge(sem(f"yt_ps{l}"), s - 3)
                    act.activation(ge[:, c % 4, :], hb[:, c % 2, :], ACT.Gelu_apprx_tanh)\
                       .then_inc(sem(f"gelu{l}"), 1)

                def w1_copy(s, c):
                    e = act.value_load(xofi[0:1, 0, bass.ds(s, 1)], min_val=0, max_val=(E - 1) * F)
                    if c >= 4:
                        act.wait_ge(sem(f"h_ps{l}"), s - 3)
                    act.activation(W1s[:, c % 4, :], W1[:, bass.ds(e, F)], ACT.Copy)\
                       .then_inc(sem(f"w1_ready{l}"), 1)

                act.wait_ge(sem(f"xof_ready{l}"), 1)
                act.wait_ge(sem(f"ew_in{l}"), 16 * 4)
                act.wait_ge(sem(f"inv_ps{l}"), 1)
                for s in range(3):
                    w1_copy(s, s)
                for s in range(HEAD):
                    gelu(s, s)
                    w1_copy(s + 3, s + 3)
                with act.Fori(0, ROUNDS) as i:
                    for c in range(HEAD, HEAD + RING):
                        gelu(RING * i + c, c)
                        w1_copy(RING * i + c + 3, c + 3)
                for s in range(SLOTS - TAIL, SLOTS):
                    gelu(s, s)

            def weighted(l, b):
                act.wait_ge(sem(f"y_in{l}{b}"), 16 * TOPK)
                for t in range(TPB * b, TPB * b + TPB):
                    last = act.activation(Yin[:, 1, t, :], Yin[:, 1, t, :], ACT.Copy, scale=wk[:, 1, t:t + 1])
                last.then_inc(sem(f"y_weighted{l}"), 1)

            for l in range(LAYERS):
                attention(l)
                routing(l)
                experts(l)
                for b in range(B):
                    weighted(l, b)

        @block.tensor
        def _(pe):
            pe.wait_ge(sem("cst_in"), 16)
            pe.wait_ge(sem("ctx_in"), 16)

            def three(l, w, g):
                return w3[w][:, l, g, :, :].rearrange("p a c -> p (a c)")

            def k_product(l):
                for g in range(G):
                    last = pe.matmul(k_banks(l)[0:96, g, :], three(l, 1, g), ctxs, start=True, stop=True)
                last.then_inc(sem("k_ps"), 1)

            def v_product(l):
                for b in range(B):
                    last = pe.matmul(bank(4 + l)[0:KV, P * b:P * b + P], ctxs[:, KV * b:KV * b + KV],
                                     aw[:, l, 2, :], start=True, stop=True)
                last.then_inc(sem("v_ps"), 1)

            reader = {}

            def take_bank7(l):
                if l in reader:
                    pe.wait_ge(sem(reader[l][0]), reader[l][1])

            def xn_turn(l, b):
                if b == 0:
                    pe.wait_ge(sem("norm_own"), l + 1)
                else:
                    pe.wait_ge(sem("xn_pool"), l * (B - 1) + b)
                take_bank7(l)
                for i in range(TPB):
                    last = pe.transpose(bank(7)[:, P * i:P * i + P], XM[:, TPB * b + i, :], ident)
                last.then_inc(sem(f"xt_ps{l}"), 1)
                reader[l] = (f"xt_ready{l}", b + 1)

            def q_product(l, b):
                pe.wait_ge(sem(f"xt_ready{l}"), b + 1)
                if b:
                    take_bank7(l)
                    pe.matmul(bank(7), aw[:, l, 0, :], xnT[:, b % 2, :], start=True, stop=True)\
                      .then_inc(sem(f"q_ps{l}"), 1)
                    reader[l] = (f"qlo_ready{l}", q_done(l, b))
                    return
                for half in range(1 + l):
                    n = Q >> l
                    for g in range(G):
                        last = pe.matmul(q_half(slice(0, 96), l, half)[1][:, g, :], three(l, 0, g),
                                         xnT[:, 0, n * half:n * half + n], start=True, stop=True)
                    last.then_inc(sem(f"q_ps{l}"), 1)
                if l:
                    reader[l] = ("qlo_ready1", 2)

            def scores(l, t):
                b = t // TPB
                if t == 0:
                    if l == 0:
                        pe.wait_ge(sem("kaug_ready"), 1)
                        pe.wait_ge(sem("kaug_a"), 2)
                    else:
                        pe.wait_ge(sem("kaug_ready1"), JH)
                        pe.wait_ge(sem("kbias_in"), 16 * 2 * H)
                        pe.wait_ge(sem("maskb_ready"), 1)
                        pe.wait_ge(sem("identb_ready"), 1)
                if l and t == 2:
                    pe.wait_ge(sem("qlo_ready1"), 2)
                if t % TPB == 0:
                    if b:
                        pe.wait_ge(sem(f"qa_in{l}"), 16 * 3 * G * b)
                    else:
                        pe.wait_ge(sem(f"qlo_ready{l}"), 1)
                    if l:
                        pe.wait_ge(sem(f"pos_in{b}"), 16)
                K = P if l else 96
                for hf in range(2):
                    n = 2 * t + hf
                    if n >= 2:
                        pe.wait_ge(sem(f"sub{l}"), n - 1)
                    for g in (2 * hf, 2 * hf + 1):
                        at = P * (t % TPB)
                        rhs = kaug[0:K, l, B * g + b, :, :].rearrange("p j k -> p (j k)")
                        last = pe.matmul(bank(g)[:, 0:GK], qaug[0:K, b % 2, g, at:at + P], rhs,
                                         start=True, stop=(l == 0))
                        if l:
                            last = pe.matmul(bank(g)[:, 0:GK].rearrange("p (j k) -> p j k", j=JH), identb[:, :],
                                             maskb[:, t, :].unsqueeze(1).to_broadcast([P, JH, KV]),
                                             start=False, stop=True)
                    last.then_inc(sem(f"s_ps{l}"), 1)

            def xm_turn(l, b):
                if b == 0:
                    pe.wait_ge(sem(f"sub{l}"), 2 * NT)
                for i in range(TPB):
                    if i == 0 or b == B - 1:
                        xm_wait(pe, l, b, i + 1)
                    last = pe.transpose(bank(b)[:, P * i:P * i + P], XM[:, TPB * b + i, :], ident)
                last.then_inc(sem(f"xmt_ps{l}"), 1)

            def turn(l, t, hf):
                for g in (2 * hf, 2 * hf + 1):
                    m = G * t + g
                    if g % 2 == 0:
                        pe.wait_ge(sem(f"exp{l}"), 2 * t + g // 2 + 1)
                    if t == 0 and g == 0:
                        pe.wait_ge(sem(f"pad_ready{l}"), 1)
                    if m >= 2:
                        pe.wait_ge(sem(f"pt_ready{l}"), m - 1)
                    for c in range(NC3):
                        last = pe.transpose(bank(4 + m % 2)[0:CH, P * c:P * c + P],
                                            Pr[:, t % 2, g, CH * c:CH * c + CH], ident)
                    last.then_inc(sem(f"pt_ps{l}"), 1)

            def values(l, t, den):
                b = t // TPB
                pe.wait_ge(sem(f"pt_ready{l}"), G * (t + 1))
                if t == 0:
                    pe.wait_ge(sem(f"vbd_in{l}"), 16 * 6)
                if t and not den:
                    pe.wait_ge(sem(f"ot_ready{l}"), t)
                for c in range(NC3):
                    for g in range(G):
                        at = C_BD + (l * NC3 + c) * 32
                        lhs = cst[0:CH, at:at + 32] if den else vbd[:, l, c, G * b + g, :]
                        last = pe.matmul(bank(6)[32 * g:32 * g + 32, P * den:P * den + P], lhs,
                                         PT[:, t % 2, NC3 * g + c, :], start=(c == 0), stop=(c == NC3 - 1))
                last.then_inc(sem(f"o_ps{l}"), 1)

            def out_product(l, t):
                pe.wait_ge(sem(f"ot_ready{l}"), t + 1)
                take_bank7(l)
                reader[l] = (f"resid{l}", t + 1)
                pe.matmul(bank(7)[:, 0:D], OT[:, t % 2, :], aw[:, l, 3, :], start=True, stop=True)\
                  .then_inc(sem(f"y_ps{l}"), 1)

            def attention(l):
                if l == 0:
                    pe.wait_ge(sem("w3_ready"), 1)
                    k_product(0)
                    pe.wait_ge(sem("aw_in0"), 16)
                    v_product(0)
                    pe.wait_ge(sem("aw_in1"), 16)
                    v_product(1)
                xn_turn(l, 0)
                if l == 0:
                    pe.wait_ge(sem("kl_ready"), 1)
                    pe.wait_ge(sem("w3_ready"), 2)
                q_product(l, 0)
                if l == 0:
                    pe.wait_ge(sem("v_ready"), 2)
                    pe.wait_ge(sem("w3_ready"), 3)
                    k_product(1)
                    reader[0] = ("kl_ready", 2)
                pe.wait_ge(sem(f"qlo_ready{l}"), 1)
                scores(l, 0)
                for t in range(NT):
                    b = t // TPB
                    if t + 1 < NT:
                        scores(l, t + 1)
                    if t == 0:
                        xn_turn(l, 1)
                    elif q_plan(t):
                        q_product(l, q_plan(t))
                    if t == NT - 1:
                        turn(l, t, 0)
                        turn(l, t, 1)
                    if t >= 1:
                        values(l, t - 1, 0)
                    if t >= 2 and not q_plan(t):
                        out_product(l, t - 2)
                    if l == 0 and t == 0:
                        pe.wait_ge(sem("kl_ready"), 2)
                    if l and t == 0:
                        pe.wait_ge(sem("qlo_ready1"), 2)
                    if t < NT - 1:
                        turn(l, t, 0)
                    if t >= 1:
                        values(l, t - 1, 1)
                    if t < NT - 1:
                        turn(l, t, 1)
                    if t == 0:
                        q_product(l, 1)
                    elif q_plan(t):
                        out_product(l, t - 2)
                    elif xn_plan(t):
                        xn_turn(l, xn_plan(t))
                xm_turn(l, 0)
                xm_turn(l, 1)
                out_product(l, NT - 2)
                values(l, NT - 1, 0)
                values(l, NT - 1, 1)
                xm_turn(l, 2)
                out_product(l, NT - 1)

            def routing(l):
                def logits(b):
                    pe.wait_ge(sem(f"xmt_ready{l}"), b + 1)
                    for i in range(TPB):
                        t = TPB * b + i
                        last = pe.matmul(bank(7)[:, E * t:E * t + E], xmT[:, b, P * i:P * i + P],
                                         rw[:, l, :], start=True, stop=True)
                    last.then_inc(sem(f"lg_ps{l}"), 1)

                if l == 0:
                    pe.wait_ge(sem("rw_in"), 16)
                pe.wait_ge(sem(f"resid{l}"), NT)
                for b in range(B - 1):
                    logits(b)
                xm_turn(l, B - 1)
                logits(B - 1)
                pe.wait_ge(sem(f"chosen{l}"), 1)
                if l == 0:
                    pe.wait_ge(sem("trib_ready"), 1)
                    pe.wait_ge(sem("ones_ready"), 1)
                place = bank(6)[:, 0:(NT + 1) * E]
                pe.matmul(place[:, 0:NT * E], trib[:, :], Ab[:, :, :].rearrange("p t e -> p (t e)"),
                          start=True, stop=False, skip_group_check=True)
                for t in range(NT):
                    n = NT - t
                    last = pe.matmul(place[:, E * (t + 1):].rearrange("p (t e) -> p t e", e=E), onesb[:, :],
                                     Ab[:, t, :].unsqueeze(1).to_broadcast([P, n, E]),
                                     start=False, stop=(t == NT - 1), skip_group_check=True)
                last.then_inc(sem(f"place_ps{l}"), 1)
                for n in range(PAIRS):
                    if n % (PAIRS // 2) == 0:
                        pe.wait_ge(sem(f"ohtk{l}"), n // (PAIRS // 2) + 1)
                    if n % 8 == 0:
                        pe.wait_ge(sem(f"onehot{l}"), n // 8 + 1)
                    last = pe.matmul(bank(5)[:, 0:2 * SLOTS], ohlo[:, n, :], ohpt[:, n, :],
                                     start=(n == 0), stop=(n == PAIRS - 1))
                last.then_inc(sem(f"inv_ps{l}"), 1)

            def experts(l):
                pe.wait_ge(sem(f"xof_ready{l}"), 1)
                pe.wait_ge(sem(f"ew_in{l}"), 16 * 4)

                at = {}

                def load_expert(s, c):
                    at[c] = pe.value_load(xofi[0:1, 0, bass.ds(s, 1)], min_val=0, max_val=(E - 1) * F)

                def x_turn(s, c, i):
                    pe.wait_ge(sem(f"gath{c % RING}"), 16 * (l * gathers_of(c % RING) + i + c // RING + 1))
                    if c >= 2:
                        pe.wait_ge(sem(f"xT_ready{l}"), s - 1)
                    pe.transpose(bank(c % 2)[:, 0:P], GX[:, c % RING, :], ident).then_inc(sem(f"xT_ps{l}"), 1)

                def up(s, c):
                    pe.wait_ge(sem(f"xT_ready{l}"), s + 1)
                    if c >= 2:
                        pe.wait_ge(sem(f"h_ready{l}"), s - 1)
                    pe.wait_ge(sem(f"w1_ready{l}"), s + 1)
                    for n in range(FC):
                        last = pe.matmul(bank(2 + c % 2)[:, P * n:P * n + P], W1s[:, c % 4, P * n:P * n + P],
                                         XT[:, c % 2, :], start=True, stop=True)
                    last.then_inc(sem(f"h_ps{l}"), 1)

                def down(s, c):
                    pe.wait_ge(sem(f"gelu{l}"), s + 1)
                    if c >= 2:
                        pe.wait_ge(sem(f"y_ready{l}"), s - 1)
                    for n in range(FC):
                        last = pe.matmul(bank(6 + c % 2)[:, 0:D], ge[:, c % 4, P * n:P * n + P],
                                         W2[:, bass.ds(at[c] + n * D, D)], start=(n == 0), stop=(n == FC - 1))
                    last.then_inc(sem(f"yt_ps{l}"), 1)

                def steps(i, first, n):
                    for c in range(first, first + n):
                        s = RING * i + c
                        x_turn(s + 3, c + 3, i)
                        up(s + 2, c + 2)
                        load_expert(s, c)
                        down(s, c)

                for s in range(3):
                    x_turn(s, s, 0)
                for s in range(2):
                    up(s, s)
                steps(0, 0, HEAD)
                with pe.Fori(0, ROUNDS) as i:
                    steps(i, HEAD, RING)
                for s in range(SLOTS - TAIL, SLOTS):
                    load_expert(s, s)
                    if s + 2 < SLOTS:
                        up(s + 2, s + 2)
                    down(s, s)

            for l in range(LAYERS):
                if l:
                    pe.wait_ge(sem("w3_ready"), 4)
                attention(l)
                routing(l)
                experts(l)

        @block.vector
        def _(dve):
            chain = [0]

            def link(ins):
                chain[0] += 1
                ins.then_inc(sem("dve_chain"), 1)
                dve.wait_ge(sem("dve_chain"), chain[0])

            def measure(t0, n):
                for t in range(t0, t0 + n):
                    last = dve.bn_stats(stat[:, t, :], X[:, t, :])
                link(last)
                for t in range(t0, t0 + n):
                    last = dve.bn_aggr(mv[:, t, :], stat[:, t, :])
                return last

            def statistics(t0, n, measured=0):
                link(measure(t0 + measured, n - measured))
                y, var = rstd[:, 0, t0:t0 + n], rstd[:, 1, t0:t0 + n]
                link(dve.tensor_scalar(var, mv[:, t0:t0 + n, 1], LN_EPS, None, ALU.add))
                link(dve.tensor_scalar(y.bitcast(I32), var.bitcast(I32), 1, None, ALU.logical_shift_right))
                dve.tensor_scalar(var, var, -0.5, None, ALU.mult)
                return dve.tensor_scalar(y.bitcast(I32), y.bitcast(I32), -1.0, float(0x5F3759DF), ALU.mult, ALU.add)

            def norm_x(l, b, n, finish):
                if l == 0:
                    for a in range(b, b + n):
                        dve.wait_ge(sem(f"x_in{a}"), 16)
                else:
                    dve.wait_ge(sem("xnd_in0"), 16 * B)
                last = statistics(TPB * b, TPB * n)
                if finish:
                    link(last)
                    normalise(dve, link, TPB * b, TPB * n, "norm_own")
                else:
                    last.then_inc(sem("guess_ready"), 1)

            def k_low(l):
                dve.wait_ge(sem("kh_ready"), l + 1)
                low = KR[l][32:64].rearrange("p (g c) -> p g c", g=G)
                dve.scalar_tensor_tensor(out=low, in0=k_banks(l)[32:64], scalar=HD ** -0.5,
                                         in1=low.bitcast(F32), op0=ALU.mult, op1=ALU.subtract)\
                   .then_inc(sem("kl_ready"), 1)

            def q_low_first(l, half):
                dve.wait_ge(sem(f"qhi_ready{l}"), half + 1)
                low, ps = q_half(slice(64, 96), l, half)
                dve.tensor_tensor(low, ps, low.bitcast(F32), ALU.subtract).then_inc(sem(f"qlo_ready{l}"), 1)

            def q_low(l, b):
                dve.wait_ge(sem(f"qhi_ready{l}"), q_done(l, b))
                if b >= 2:
                    dve.wait_ge(sem(f"qa_in{l}"), 16 * 3 * G * (b - 1))
                dve.tensor_tensor(qlo, bank(7), qhi.bitcast(F32), ALU.subtract).then_inc(sem(f"qlo_ready{l}"), 1)

            def soft(l, t):
                ready = []
                for hf in range(2):
                    dve.wait_ge(sem(f"s_ps{l}"), 2 * t + hf + 1)
                    s = PS[:, 1024 * hf:1024 * hf + 1024].rearrange("p (g c) -> p g c", g=2)[:, :, 0:GK]\
                        .rearrange("p g (j k) -> p g j k", j=JH)
                    m = mx[:, hf, :].rearrange("p (g j) -> p g j", g=2)
                    dve.tensor_reduce(m, s, AX.X, ALU.max).then_inc(sem("dve_chain"), 1)
                    chain[0] += 1
                    ready.append((s, m, chain[0]))
                for hf, (s, m, count) in enumerate(ready):
                    dve.wait_ge(sem("dve_chain"), count)
                    if t >= 1:
                        dve.wait_ge(sem(f"exp{l}"), 2 * t + hf - 1)
                    dve.tensor_tensor(Dm[:, hf, :, :].rearrange("p g (j k) -> p g j k", j=JH), s,
                                      m.unsqueeze(3).to_broadcast([P, 2, JH, KV]), ALU.subtract)\
                       .then_inc(sem(f"sub{l}"), 1)

            def divide(l, t):
                dve.wait_ge(sem(f"o_ps{l}"), 2 * (t + 1))
                link(dve.reciprocal(rden, bank(6)[:, P:2 * P]))
                if t >= 2:
                    dve.wait_ge(sem(f"y_ps{l}"), t - 1)
                dve.tensor_tensor(OT[:, t % 2, :], bank(6)[:, 0:P], rden, ALU.mult).then_inc(sem(f"ot_ready{l}"), 1)

            def residual(l, t):
                dve.wait_ge(sem(f"y_ps{l}"), t + 1)
                b = t // TPB
                dve.wait_ge(sem(f"xb_ready{l}"), b + 1)
                dve.scalar_tensor_tensor(out=X[:, t, :], in0=bank(7)[:, 0:D], scalar=tg[:, l:l + 1],
                                         in1=X[:, t, :], op0=ALU.mult, op1=ALU.add).then_inc(sem(f"resid{l}"), 1)

            def norm_xm(l, b):
                dve.wait_ge(sem(f"resid{l}"), TPB * (b + 1))
                last = statistics(TPB * b, TPB, TPB - 1 if b == B - 1 else 0)
                if b < B - 1:
                    last.then_inc(sem("guess_ready"), 1)
                else:
                    link(last)
                    dve.wait_ge(sem(f"xt_ps{l}"), b + 1)
                    normalise(dve, link, TPB * b, TPB, f"xm_own{l}")

            def attention(l):
                if l == 0:
                    norm_x(0, 0, 1, True)
                    dve.wait_ge(sem("cst_in"), 16)
                    k_low(0)
                    dve.wait_ge(sem("kl_ready"), 1)
                    for j in (0, 1):
                        last = k_heads(nc.vector, j)
                    last.then_inc(sem("kaug_ready"), 1)
                    norm_x(0, 1, B - 1, False)
                for half in range(1 + l):
                    q_low_first(l, half)
                for t in range(NT):
                    b = t // TPB
                    soft(l, t)
                    if l == 0 and t == 0:
                        k_low(1)
                    if t and q_plan(t - 1):
                        q_low(l, q_plan(t - 1))
                        if t >= 3:
                            divide(l, t - 2)
                            residual(l, t - 3)
                    else:
                        if t >= 3:
                            residual(l, t - 3)
                        if t >= 2:
                            divide(l, t - 2)
                    if l and t == 0:
                        norm_x(1, 2, B - 2, False)
                    if b and t % TPB == 2:
                        norm_xm(l, b - 1)
                residual(l, NT - 3)
                for t in (NT - 2, NT - 1):
                    divide(l, t)
                    residual(l, t)
                    if t == NT - 2:
                        dve.wait_ge(sem(f"resid{l}"), t + 1)
                        measure(NT - TPB, TPB - 1)
                norm_xm(l, B - 1)

            def routing(l):
                if l == 0:
                    dve.wait_ge(sem("mask_in"), 16)
                    link(dve.tensor_scalar(mcnt, mski, 0.0, None, ALU.is_equal))
                    dve.tensor_scalar(maskb[:, :, :], mcnt.rearrange("p (t k) -> p t k", t=NT), -BIG, None, ALU.mult)\
                       .then_inc(sem("maskb_ready"), 1)
                    link(dve.tensor_reduce(nanrow[:, :], mcnt.rearrange("p (t k) -> p t k", t=NT), AX.X, ALU.min))
                    link(dve.tensor_scalar(nanrow[:, :], nanrow[:, :], -HUGE, 10.0, ALU.mult, ALU.mult))
                    dve.tensor_scalar(nanrow[:, :], nanrow[:, :], 0.0, None, ALU.mult).then_inc(sem("mask_ready"), 1)
                dve.wait_ge(sem(f"lg_ps{l}"), B)
                link(dve.tensor_copy(L, bank(7)[:, 0:NT * E].rearrange("p (t e) -> p t e", e=E)))
                number = cst[:, C_HI:C_HI + E].unsqueeze(1).to_broadcast([P, NT, E])

                def over_experts(a):
                    return a.unsqueeze(2).to_broadcast([P, NT, E])

                for k, src in enumerate((L, Lrest)):
                    link(dve.tensor_reduce(small[:, 3 * k, :], src, AX.X, ALU.max))
                    link(dve.tensor_tensor(wtie, src, over_experts(small[:, 3 * k, :]), ALU.is_equal))
                    link(dve.scalar_tensor_tensor(out=wtie, in0=wtie, scalar=-float(E), in1=number,
                                                  op0=ALU.mult, op1=ALU.add))
                    if k:
                        link(dve.scalar_tensor_tensor(out=wtie, in0=M[:, 0, :, :], scalar=2.0 * E, in1=wtie,
                                                      op0=ALU.mult, op1=ALU.add))
                    link(dve.tensor_reduce(small[:, 1, :], wtie, AX.X, ALU.min))
                    link(dve.tensor_tensor(M[:, k, :, :], wtie, over_experts(small[:, 1, :]), ALU.is_equal))
                    if k == 0:
                        link(dve.scalar_tensor_tensor(out=Lrest, in0=M[:, 0, :, :], scalar=-BIG, in1=L,
                                                      op0=ALU.mult, op1=ALU.add))
                dve.tensor_tensor(Ab[:, :, :], M[:, 0, :, :], M[:, 1, :, :], ALU.add).then_inc(sem(f"chosen{l}"), 1)
                dve.tensor_tensor(tmpE, L, over_experts(small[:, 0, :]), ALU.subtract).then_inc(sem(f"lsub{l}"), 1)
                dve.wait_ge(sem(f"place_ps{l}"), 1)
                place = bank(6)[:, 0:NT * E].rearrange("p (t e) -> p t e", e=E)
                count = bank(6)[:, NT * E:(NT + 1) * E]
                link(dve.tensor_copy(tbl[:, 0, :], count))
                link(dve.tensor_tensor(n16, tbl[:, 0, :].unsqueeze(2).to_broadcast([P, E, NT]),
                                       cst[:, C_J:C_J + NT].unsqueeze(1).to_broadcast([P, E, NT]), ALU.is_gt))
                link(dve.tensor_reduce(tbl[:, 1, :], n16, AX.X, ALU.add))
                sq = n16[:, :, 0:E]

                def up_to(row, c0, factor):
                    link(dve.scalar_tensor_tensor(out=sq, in0=tbl[:, 1, :].unsqueeze(1).to_broadcast([P, E, E]),
                                                  scalar=factor, in1=cst[:, c0:c0 + E * E]
                                                  .rearrange("p (e f) -> p e f", e=E), op0=ALU.mult, op1=ALU.mult))
                    link(dve.tensor_reduce(tbl[:, row, :], sq, AX.X, ALU.add))

                up_to(2, C_LT, float(P))
                link(dve.tensor_tensor(rank, place, tbl[:, 2, :].unsqueeze(1).to_broadcast([P, NT, E]), ALU.add))
                link(dve.tensor_tensor(tmpK, rank.unsqueeze(1).to_broadcast([P, TOPK, NT, E]), M, ALU.mult))
                link(dve.tensor_reduce(slot[:, :, :].rearrange("p t k -> p k t"), tmpK, AX.X, ALU.add))
                link(dve.tensor_copy(sloti[:, 0, :], slot[:, :, :].rearrange("p t k -> p (t k)")))
                dve.tensor_scalar(sloti[:, 1, :], sloti[:, 0, :], P - 1, None, ALU.bitwise_and)
                link(dve.tensor_scalar(sloti[:, 2, :], sloti[:, 0, :], 7, None, ALU.logical_shift_right))
                link(dve.tensor_copy(slotb[:, :, :], sloti[:, 1:3, :]))
                dve.tensor_tensor(ohhi, cst[:, C_HI:C_HI + SLOTS].unsqueeze(1).to_broadcast([P, PAIRS, SLOTS]),
                                       slotb[:, 1, :].unsqueeze(2).to_broadcast([P, PAIRS, SLOTS]), ALU.is_equal)\
                   .then_inc(sem(f"ohhi_ready{l}"), 1)
                dve.wait_ge(sem(f"ohhi_ready{l}"), 1)
                dve.tensor_scalar(ohpt[:, :, 0:SLOTS], ohhi, cst[:, C_P:C_P + 1], None, ALU.mult)
                for c in range(4):
                    dve.tensor_tensor(*low_onehot(c)).then_inc(sem(f"onehot{l}"), 1)
                dve.wait_ge(sem(f"inv_ps{l}"), 1)
                p_ps, tk_ps = bank(5)[:, 0:SLOTS], bank(5)[:, SLOTS:2 * SLOTS]
                dve.tensor_scalar(idf[:, 1, :], tk_ps, 0.5, float(4 * B * Q), ALU.is_lt, ALU.mult)
                link(dve.tensor_scalar(idf[:, 2, :], tk_ps, -1.0, float(P), ALU.add, ALU.mult))
                link(dve.tensor_tensor(idf[:, 0, :], p_ps, idf[:, 2, :], ALU.add))
                link(dve.tensor_copy(idi[:, :], idf[:, 0, :]))
                dve.tensor_scalar(gidx[:, :], idi[:, :].bitcast(U32), B * Q - 1, None, ALU.bitwise_and)\
                   .then_inc(sem(f"gidx_ready{l}"), 1)
                dve.tensor_tensor(sidx[:, :], idf[:, 0, :], idf[:, 1, :], ALU.add).then_inc(sem(f"sidx_ready{l}"), 1)
                up_to(3, C_LE, 1.0)
                link(dve.tensor_tensor(xof[:, 0:SLOTS, :], cst[0:1, C_HI:C_HI + SLOTS].unsqueeze(2).to_broadcast([1, SLOTS, E]),
                                       tbl[0:1, 3, :].unsqueeze(1).to_broadcast([1, SLOTS, E]), ALU.is_ge))
                link(dve.tensor_reduce(xoff[:, 0:SLOTS], xof[:, 0:SLOTS, :], AX.X, ALU.add))
                dve.tensor_scalar(xofi[:, 0, 0:SLOTS], xoff[:, 0:SLOTS], float(E - 1), float(F), ALU.min, ALU.mult)
                dve.tensor_scalar(xofi[:, 1, 0:SLOTS], xoff[:, 0:SLOTS], float(E - 1), float(BW), ALU.min, ALU.mult)\
                   .then_inc(sem(f"xof_ready{l}"), 1)
                dve.wait_ge(sem(f"lexp{l}"), 1)
                link(dve.tensor_reduce(small[:, 1, :], ex, AX.X, ALU.add))
                link(dve.reciprocal(small[:, 2, :], small[:, 1, :]))
                link(dve.tensor_scalar(small[:, 2, :], small[:, 2, :], tg[:, 2 + l:3 + l], None, ALU.mult))
                for k in range(TOPK):
                    link(dve.tensor_tensor(tmpE, ex, M[:, k, :, :], ALU.mult))
                    link(dve.tensor_reduce(small[:, 3, :], tmpE, AX.X, ALU.add))
                    link(dve.tensor_tensor(wk[:, k, :], small[:, 3, :], small[:, 2, :], ALU.mult))

            def experts(l):
                dve.wait_ge(sem(f"xof_ready{l}"), 1)
                dve.wait_ge(sem(f"ew_in{l}"), 16 * 4)

                at = {}

                def load_expert(s, c):
                    at[c] = dve.value_load(xofi[0:1, 1, bass.ds(s, 1)], min_val=0, max_val=(E - 1) * BW)

                def x_copy(s, c):
                    dve.wait_ge(sem(f"xT_ps{l}"), s + 1)
                    if c >= 2:
                        dve.wait_ge(sem(f"h_ps{l}"), s - 1)
                    dve.tensor_copy(XT[:, c % 2, :], bank(c % 2)[:, 0:P]).then_inc(sem(f"xT_ready{l}"), 1)

                def bias(s, c):
                    dve.wait_ge(sem(f"h_ps{l}"), s + 1)
                    if c >= 2:
                        dve.wait_ge(sem(f"gelu{l}"), s - 1)
                    dve.tensor_tensor(hb[:, c % 2, :].rearrange("p (n q) -> p n q", n=FC),
                                      bank(2 + c % 2).rearrange("p (n q) -> p n q", n=FC),
                                      BB[:, bass.ds(at[c], FC)].unsqueeze(2).to_broadcast([P, FC, P]), ALU.add)\
                       .then_inc(sem(f"h_ready{l}"), 1)

                def finish(s, c, i):
                    dve.wait_ge(sem(f"yt_ps{l}"), s + 1)
                    if c >= 4:
                        dve.wait_ge(sem(f"scat{c % 4}"), 16 * (l * scatters_of(c % 4) + RING // 4 * i + c // 4))
                    dve.tensor_tensor(Yb[:, c % 4, :], bank(6 + c % 2)[:, 0:D], BB[:, bass.ds(at[c] + FC, D)], ALU.add)\
                       .then_inc(sem(f"y_ready{l}"), 1)

                def steps(i, first, n):
                    for c in range(first, first + n):
                        s = RING * i + c
                        load_expert(s + 2, c + 2)
                        x_copy(s + 3, c + 3)
                        bias(s + 2, c + 2)
                        if c < first + 2:
                            load_expert(s, c)
                        finish(s, c, i)

                for s in range(2):
                    load_expert(s, s)
                    x_copy(s, s)
                bias(0, 0)
                x_copy(2, 2)
                bias(1, 1)
                steps(0, 0, HEAD)
                with dve.Fori(0, ROUNDS) as i:
                    steps(i, HEAD, RING)
                for s in range(SLOTS - TAIL, SLOTS):
                    load_expert(s, s)
                    if s + 2 < SLOTS:
                        load_expert(s + 2, s + 2)
                        bias(s + 2, s + 2)
                    finish(s, s, 0)

            def combine(l, b):
                dve.wait_ge(sem(f"y_in{l}{b}"), 16 * TOPK)
                for t in range(TPB * b, TPB * b + TPB):
                    last = dve.scalar_tensor_tensor(out=X[:, t, :], in0=Yin[:, 0, t, :], scalar=wk[:, 0, t:t + 1],
                                                    in1=X[:, t, :], op0=ALU.mult, op1=ALU.add)
                link(last)
                dve.wait_ge(sem(f"y_weighted{l}"), b + 1)
                xs = X[:, TPB * b:TPB * b + TPB, :]
                dve.tensor_tensor(xs, xs, Yin[:, 1, TPB * b:TPB * b + TPB, :], ALU.add).then_inc(sem(f"x_done{l}"), 1)

            attention(0)
            routing(0)
            experts(0)
            for b in range(B):
                combine(0, b)
                if b == 0:
                    dve.wait_ge(sem("x_done0"), 1)
                    norm_x(1, 0, 1, True)
            dve.wait_ge(sem("x_done0"), B)
            norm_x(1, 1, 1, False)
            attention(1)
            routing(1)
            experts(1)
            for b in range(B):
                combine(1, b)


_OUT = ((B * Q, D), "float32")


def kernel(**inputs):
    import concourse.bacc as bacc
    from concourse.bass_utils import run_bass_kernel_spmd as run

    a = {n: np.asarray(v) for n, v in inputs.items()}
    T = np.transpose
    attnw = np.stack([
        np.stack([T(a["L0_xattn_Wq"]), T(a["L0_xattn_Wk"]), T(a["L0_xattn_Wv"]), T(a["L0_xattn_Wo"])], 1),
        np.stack([T(a["L1_xattn_W_q"]), T(a["L1_xattn_W_k"]), T(a["L1_xattn_W_v"]), T(a["L1_xattn_W_o"])], 1)], 1)
    w1 = np.stack([T(a["L0_ffn_w1"], (1, 0, 2)).reshape(D, E * F), T(a["L1_ffn_w1"], (2, 1, 0)).reshape(D, E * F)])
    w2 = np.stack([T(a["L0_ffn_w2"].reshape(E, FC, P, D), (2, 0, 1, 3)).reshape(P, E * FC * D),
                   T(a["L1_ffn_w2"].reshape(D, E, FC, P), (3, 1, 2, 0)).reshape(P, E * FC * D)])
    arrays = {
        "x": a["x"].reshape(B * Q, D),
        "ctxT": T(a["ctx_1024"].reshape(B * KV, D)),
        "attnw": attnw,
        "bo": a["L0_xattn_bo"].reshape(1, D),
        "gates": np.concatenate([a["g_xattn"].reshape(1, 2), a["g_ffn"].reshape(1, 2)], 1),
        "posq": a["itok_BxS_8_8191"].reshape(1, B * Q),
        "posk": a["itok_BxS2_1_8191"].reshape(1, B * KV),
        "mask": a["mask_BxSxS2_if1"].reshape(B * Q, KV),
        "router": np.stack([a["L0_ffn_w_router"], T(a["L1_ffn_gate_w"])], 1),
        "w1": w1,
        "w2": w2,
        "b1": np.stack([T(a[f"L{l}_ffn_b1"].reshape(E, FC, P), (2, 0, 1)) for l in range(LAYERS)]),
        "b2": np.stack([a[f"L{l}_ffn_b2"] for l in range(LAYERS)]),
        "consts": constant_table(),
    }
    nc = bacc.Bacc("TRN2", target_bir_lowering=False, num_devices=1)
    feed, args = {}, {}
    for name, v in arrays.items():
        v = np.ascontiguousarray(v)
        feed[f"in_{name}"] = v
        args[name] = nc.dram_tensor(f"in_{name}", v.shape, mybir.dt.from_np(v.dtype), kind="ExternalInput").ap()
    args["out"] = nc.dram_tensor("out_x", _OUT[0], F32, kind="ExternalOutput").ap()
    build(nc, **args)
    r = run(nc, [feed], core_ids=[0])
    return r.results[0]["out_x"].reshape(B, Q, D)
```
